# Optimizing a Trainium2 kernel written in Bass

```python
import numpy as np
import jax
import jax.numpy as jnp

def _softmax(x, axis=-1):
    return jax.nn.softmax(x, axis=axis)

def _gelu(x):
    return jax.nn.gelu(x, approximate=True)

def _silu(x):
    return jax.nn.silu(x)

def _sigmoid(x):
    return jax.nn.sigmoid(x)

def _layernorm(x, axis=-1, eps=1e-05):
    m = jnp.mean(x, axis=axis, keepdims=True)
    v = jnp.var(x, axis=axis, keepdims=True)
    return (x - m) / jnp.sqrt(v + eps)

def _scatter_add(tgt, idx, src, axis=0):
    return tgt.at[idx].add(src)

def _segment_sum(src, seg, n):
    return jax.ops.segment_sum(src, seg, n)
kernel_name = 'mk_gnn_ffn_d1_gnn_r8_a18304'

def setup_inputs(seed: int=0):
    np.random.seed(seed)
    _w = jnp.asarray

    def _rec_inputs():
        import jax
        import jax.numpy as jnp
        _gk = jax.random.key(seed)
        x = -0.0002117 + 1 * jax.random.normal(jax.random.fold_in(_gk, 1), (1250, 512), jnp.float32)
        src = jax.random.randint(jax.random.fold_in(_gk, 2), (20000,), 0, 1250, jnp.int32)
        dst = jax.random.randint(jax.random.fold_in(_gk, 3), (20000,), 0, 1250, jnp.int32)
        _o = jnp.argsort(dst, stable=True)
        src = src[_o]
        dst = dst[_o]
        edge_type_8 = jax.random.randint(jax.random.fold_in(_gk, 12), (20000,), 0, 8, jnp.int32)
        edge_weight = jax.random.uniform(jax.random.fold_in(_gk, 13), (20000,), jnp.float32, 0.0, 0.999999)
        return (x, src, dst, edge_type_8, edge_weight)
    x, src, dst, edge_type_8, edge_weight = _rec_inputs()

    def _L0_gnn_setup():
        import jax, jax.numpy as jnp
        import numpy as np
        N, IN_DIM, H, D, E = (6250, 512, 8, 64, 100000)
        NEG_SLOPE = 0.2
        LN_EPS = 1e-05
        key = jax.random.key(seed)
        ks = jax.random.split(key, 8)
        x = jax.random.normal(ks[0], (N, IN_DIM), dtype=jnp.float32)
        edge_index = jax.random.randint(ks[1], (2, E), 0, N, dtype=jnp.int64)
        edge_type = jax.random.randint(ks[2], (E,), 0, 8, dtype=jnp.int64)
        edge_weight = jax.random.uniform(ks[3], (E,), dtype=jnp.float32)
        W = jax.random.normal(ks[4], (H * D, IN_DIM), dtype=jnp.float32) * (1.0 / np.sqrt(IN_DIM))
        a_src = jax.random.normal(ks[5], (H, D), dtype=jnp.float32) * (1.0 / np.sqrt(D))
        a_dst = jax.random.normal(ks[6], (H, D), dtype=jnp.float32) * (1.0 / np.sqrt(D))
        et_emb = jax.random.normal(ks[7], (8, H), dtype=jnp.float32)
        ln_gamma = jnp.ones((H * D,), dtype=jnp.float32)
        ln_beta = jnp.zeros((H * D,), dtype=jnp.float32)
        return {'x': x, 'edge_index': edge_index, 'edge_type': edge_type, 'edge_weight': edge_weight, 'W': W, 'a_src': a_src, 'a_dst': a_dst, 'et_emb': et_emb, 'ln_gamma': ln_gamma, 'ln_beta': ln_beta}
    _L0_gnn_all = _L0_gnn_setup()
    _L0_gnn_in = {k: v for k, v in _L0_gnn_all.items() if k in ('W', 'a_src', 'a_dst', 'et_emb', 'ln_gamma', 'ln_beta')}
    del _L0_gnn_all

    def _L0_ffn_setup():
        import jax, jax.numpy as jnp
        import numpy as np
        B, S, D = (1, 512, 512)
        E, K, H = (64, 2, 256)
        HS = 256
        EPS = 1e-05
        key = jax.random.key(seed)
        ks = jax.random.split(key, 16)
        n = lambda k, shp, s=0.02: jax.random.normal(k, shp, dtype=jnp.float32) * s
        return {'x': jax.random.normal(ks[0], (B, S, D), dtype=jnp.float32), 'Wg': n(ks[1], (E, D)), 'bg': n(ks[2], (E,)), 'gamma': 1.0 + n(ks[3], (E, D)), 'beta': n(ks[4], (E, D)), 'W1': n(ks[5], (E, D, H)), 'b1': n(ks[6], (E, H)), 'W3': n(ks[7], (E, D, H)), 'b3': n(ks[8], (E, H)), 'W2': n(ks[9], (E, H, D)), 'b2': n(ks[10], (E, D)), 'gs': 1.0 + n(ks[11], (D,)), 'bs': n(ks[11], (D,)), 'Ws1': n(ks[12], (D, HS)), 'bs1': n(ks[12], (HS,)), 'Ws3': n(ks[13], (D, HS)), 'bs3': n(ks[13], (HS,)), 'Ws2': n(ks[14], (HS, D)), 'bs2': n(ks[15], (D,))}
    _L0_ffn_all = _L0_ffn_setup()
    _L0_ffn_in = {k: v for k, v in _L0_ffn_all.items() if k in ('Wg', 'bg', 'gamma', 'beta', 'W1', 'b1', 'W3', 'b3', 'W2', 'b2', 'gs', 'bs', 'Ws1', 'bs1', 'Ws3', 'bs3', 'Ws2', 'bs2')}
    del _L0_ffn_all
    return {'x': x, 'src': src, 'dst': dst, 'edge_type_8': edge_type_8, 'edge_weight': edge_weight, 'L0_gnn_W': _L0_gnn_in['W'], 'L0_gnn_a_src': _L0_gnn_in['a_src'], 'L0_gnn_a_dst': _L0_gnn_in['a_dst'], 'L0_gnn_et_emb': _L0_gnn_in['et_emb'], 'L0_gnn_ln_gamma': _L0_gnn_in['ln_gamma'], 'L0_gnn_ln_beta': _L0_gnn_in['ln_beta'], 'L0_ffn_Wg': _L0_ffn_in['Wg'], 'L0_ffn_bg': _L0_ffn_in['bg'], 'L0_ffn_gamma': _L0_ffn_in['gamma'], 'L0_ffn_beta': _L0_ffn_in['beta'], 'L0_ffn_W1': _L0_ffn_in['W1'], 'L0_ffn_b1': _L0_ffn_in['b1'], 'L0_ffn_W3': _L0_ffn_in['W3'], 'L0_ffn_b3': _L0_ffn_in['b3'], 'L0_ffn_W2': _L0_ffn_in['W2'], 'L0_ffn_b2': _L0_ffn_in['b2'], 'L0_ffn_gs': _L0_ffn_in['gs'], 'L0_ffn_bs': _L0_ffn_in['bs'], 'L0_ffn_Ws1': _L0_ffn_in['Ws1'], 'L0_ffn_bs1': _L0_ffn_in['bs1'], 'L0_ffn_Ws3': _L0_ffn_in['Ws3'], 'L0_ffn_bs3': _L0_ffn_in['bs3'], 'L0_ffn_Ws2': _L0_ffn_in['Ws2'], 'L0_ffn_bs2': _L0_ffn_in['bs2']}

def reference(x, src, dst, edge_type_8, edge_weight, L0_gnn_W, L0_gnn_a_src, L0_gnn_a_dst, L0_gnn_et_emb, L0_gnn_ln_gamma, L0_gnn_ln_beta, L0_ffn_Wg, L0_ffn_bg, L0_ffn_gamma, L0_ffn_beta, L0_ffn_W1, L0_ffn_b1, L0_ffn_W3, L0_ffn_b3, L0_ffn_W2, L0_ffn_b2, L0_ffn_gs, L0_ffn_bs, L0_ffn_Ws1, L0_ffn_bs1, L0_ffn_Ws3, L0_ffn_bs3, L0_ffn_Ws2, L0_ffn_bs2):
    import jax
    import jax.numpy as jnp

    def _L0_gnn_ref(x, edge_index, edge_type, edge_weight, W, a_src, a_dst, et_emb, ln_gamma, ln_beta):
        import jax, jax.numpy as jnp
        import numpy as np
        N, IN_DIM, H, D, E = (6250, 512, 8, 64, 100000)
        NEG_SLOPE = 0.2
        LN_EPS = 1e-05
        n, h_, d_ = (x.shape[0], a_src.shape[0], a_src.shape[1])
        h = (x @ W.T).reshape(n, h_, d_)
        src, dst = (edge_index[0], edge_index[1])
        h_src = h[src]
        e_src = jnp.einsum('ehd,hd->eh', h_src, a_src)
        e_dst = jnp.einsum('ehd,hd->eh', h[dst], a_dst)
        e = jax.nn.leaky_relu(e_src + e_dst, NEG_SLOPE)
        e = e * (1.0 + et_emb[edge_type])
        e = e * edge_weight[:, None]
        e_max = jnp.zeros((n, h_), x.dtype).at[dst].max(e)
        e = jnp.exp(e - e_max[dst])
        e_sum = jnp.zeros((n, h_), x.dtype).at[dst].add(e)
        alpha = e / (e_sum[dst] + 1e-10)
        msg = h_src * alpha[:, :, None]
        out = jnp.zeros((n, h_, d_), x.dtype).at[dst].add(msg).reshape(n, h_ * d_)
        out = out + x
        mu = jnp.mean(out, axis=-1, keepdims=True)
        var = jnp.var(out, axis=-1, keepdims=True)
        return (out - mu) / jnp.sqrt(var + LN_EPS) * ln_gamma + ln_beta

    def _L0_ffn_ref(x, Wg, bg, gamma, beta, W1, b1, W3, b3, W2, b2, gs, bs, Ws1, bs1, Ws3, bs3, Ws2, bs2):
        import jax, jax.numpy as jnp
        import numpy as np
        B, S, D = (1, 512, 512)
        E, K, H = (64, 2, 256)
        HS = 256
        EPS = 1e-05
        shape = x.shape
        xt = x.reshape(-1, D)
        T = xt.shape[0]
        scores = jax.nn.sigmoid(xt @ Wg.T + bg)
        w, idx = jax.lax.top_k(scores, K)
        w = w / w.sum(-1, keepdims=True)
        cw = jnp.zeros((T, E), xt.dtype).at[jnp.arange(T)[:, None], idx].add(w)
        mu = xt.mean(-1, keepdims=True)
        var = ((xt - mu) ** 2).mean(-1, keepdims=True)
        nx = (xt - mu) * jax.lax.rsqrt(var + EPS)
        W1p = gamma[:, :, None] * W1
        b1p = b1 + jnp.einsum('ed,edh->eh', beta, W1)
        W3p = gamma[:, :, None] * W3
        b3p = b3 + jnp.einsum('ed,edh->eh', beta, W3)
        h1 = jnp.einsum('td,edh->eth', nx, W1p) + b1p[:, None, :]
        h3 = jnp.einsum('td,edh->eth', nx, W3p) + b3p[:, None, :]
        h = jax.nn.silu(h1) * h3
        hw = h * cw.T[:, :, None]
        y = jnp.einsum('eth,ehd->td', hw, W2) + cw @ b2
        nxs = nx * gs + bs
        hs = jax.nn.silu(nxs @ Ws1 + bs1) * (nxs @ Ws3 + bs3)
        z = hs @ Ws2 + bs2
        return (y + z).reshape(shape)
    edge_index = jnp.stack([src, dst])
    x = x + _L0_gnn_ref(_layernorm(x, axis=-1), edge_index, edge_type_8, edge_weight, L0_gnn_W, L0_gnn_a_src, L0_gnn_a_dst, L0_gnn_et_emb, L0_gnn_ln_gamma, L0_gnn_ln_beta)
    x = x + _L0_ffn_ref(_layernorm(x, axis=-1)[None], L0_ffn_Wg, L0_ffn_bg, L0_ffn_gamma, L0_ffn_beta, L0_ffn_W1, L0_ffn_b1, L0_ffn_W3, L0_ffn_b3, L0_ffn_W2, L0_ffn_b2, L0_ffn_gs, L0_ffn_bs, L0_ffn_Ws1, L0_ffn_bs1, L0_ffn_Ws3, L0_ffn_bs3, L0_ffn_Ws2, L0_ffn_bs2)[0]
    return x

_drawn_inputs = setup_inputs


def setup_inputs(seed=0):
    import zlib

    import numpy as np

    out = dict(_drawn_inputs(seed))
    spreads = {'L0_gnn_ln_gamma': (1.0, 0.2), 'L0_gnn_ln_beta': (0.0, 0.1)}
    factors = {'L0_ffn_Wg': 4.011,
     'L0_ffn_bg': 8.0,
     'L0_ffn_gamma': 8.0,
     'L0_ffn_beta': 8.0,
     'L0_ffn_W1': 4.63,
     'L0_ffn_b1': 52.723,
     'L0_ffn_W3': 4.533,
     'L0_ffn_b3': 52.431,
     'L0_ffn_W2': 4.537,
     'L0_ffn_b2': 63.704,
     'L0_ffn_gs': 35.102,
     'L0_ffn_bs': 35.935,
     'L0_ffn_Ws1': 3.263,
     'L0_ffn_bs1': 64.0,
     'L0_ffn_Ws3': 3.195,
     'L0_ffn_bs3': 64.0,
     'L0_ffn_Ws2': 3.208,
     'L0_ffn_bs2': 45.072}
    for name, (base, spread) in spreads.items():
        noise = np.random.default_rng([zlib.crc32(name.encode()), seed]).standard_normal(out[name].shape)
        drawn = base * np.exp(spread * noise) if base else spread * noise
        out[name] = jnp.asarray(drawn.astype(out[name].dtype))
    for name, factor in factors.items():
        out[name] = (out[name] * factor).astype(out[name].dtype)
    return out
```

```python
from contextlib import ExitStack

import concourse.bass as bass
from concourse import mybir

F32 = mybir.dt.float32
BF16 = mybir.dt.bfloat16
I32 = mybir.dt.int32
U32 = mybir.dt.uint32
ALU = mybir.AluOpType
ACT = mybir.ActivationFunctionType
AX_X = mybir.AxisListType.X

P = 128
EPS = 1e-5
TOKENS = 80


def gnn_moe_kernel(nc, x, src, dst, etype, eweight, W, a_src, a_dst, et_emb, ln_gamma, ln_beta,
                   Wg, bg, gamma, beta, W1, b1, W3, b3, W2, b2, gs, bs, Ws1, bs1, Ws3, bs3, Ws2, bs2, out):
    N, D = x.shape
    NE = src.shape[0]
    H, HD = a_src.shape
    TY = et_emb.shape[0]
    NT = -(-N // P)
    NPAD = NT * P
    LAST = N - (NT - 1) * P
    A = D // P
    GE = 2 * P
    NG = -(-NE // GE)
    NC = 2 * NG
    NX = NT - 1
    NI = NG + NX
    NCX = 2 * NI
    EPAD = NC * P
    PADNODE = NPAD - 1
    IB = 8
    SLOTS = 2 * IB
    ITER = NI // IB
    assert NI % IB == 0
    RW = GE + 2
    FULLC = NE // P
    REST = NE - FULLC * P

    NEX, _, HF = W1.shape
    M = HF // P
    TS = TOKENS
    NOV = (2 * N) // TS
    NTILE = NEX + NOV
    KMAX = (N - 1) // TS
    U = 4
    NIT = NEX // U
    SKIP = 1 << 20

    nx_d = nc.dram_tensor("nx_rows", [NPAD, D], F32).ap()
    y_d = nc.dram_tensor("y_rows", [2 * NPAD, D], F32).ap()
    slot_d = nc.dram_tensor("slot_rows", [TS * NTILE, 2], I32).ap()
    h_d = nc.dram_tensor("h_rows", [NPAD, D], F32).ap()
    bkey_d = nc.dram_tensor("edge_keys", [3, EPAD], BF16).ap()

    with ExitStack() as ctx:
        ctx.enter_context(nc.allow_non_contiguous_dma(reason="a few hundred single elements of small inputs"))
        def sb(name, shape, dt=F32):
            return ctx.enter_context(nc.sbuf_tensor(name, shape, dt))

        def sem(name):
            return ctx.enter_context(nc.semaphore(name))

        arena = sb("arena", [P, 17500])

        class Carver:
            def __init__(self, buf, size):
                self.buf, self.size, self.at = buf, size, 0

            def __call__(self, shape, dt=F32):
                n = 1
                for d in shape[1:]:
                    n *= d
                words = (n * (2 if dt == BF16 else 4) + 3) // 4
                a = self.buf[0:shape[0], self.at:self.at + words]
                self.at += words
                assert self.at <= self.size, (self.at, self.size)
                if dt != F32:
                    a = a.bitcast(dt)[:, 0:n]
                if len(shape) > 2:
                    names = " ".join(f"d{k}" for k in range(1, len(shape)))
                    a = a.rearrange(f"p ({names}) -> p {names}", **{f"d{k}": shape[k] for k in range(1, len(shape))})
                return a

        first = Carver(arena, 17500)
        ps = ctx.enter_context(nc.psum_tensor("ps", [P, 8, 512], F32))

        ident = sb("ident", [P, P])
        ones = sb("ones", [P, P])
        iota_row = sb("iota_row", [P, P])
        spare = sb("spare", [P, 16])
        iota_p = sb("iota_p", [P, 1])
        x_sb = sb("x_sb", [P, NT, D])
        xn = sb("xn", [P, NT, D])
        xT = sb("xT", [P, A, NPAD])
        acc = sb("acc", [P, NT, D])
        accs = sb("accs", [P, NT, H])
        stats = sb("stats", [P, NT, 6])
        mv = sb("mv", [P, NT, 2])
        rstd = sb("rstd", [P, NT])
        ring = sb("ring", [P, SLOTS, D])
        W_sb = first([P, A, D])
        WT = first([P, A, D])
        attn = first([P, 2, A])
        ablk = first([P, A * 2 * H])
        V = first([P, A, 2 * H])
        tab = first([P, 2, NT * H])
        tabr = first([P, 2 * NT * H])
        tab3 = first([P, 3, 2, NT * H], BF16)
        emb = first([TY, H])
        embr = first([TY, H])
        emb3 = first([TY, 3, H], BF16)
        erow = first([P, 2, 4, P], I32)
        erowf = first([P, 2, 4, P])
        ecol = sb("ecol", [P, 4, NC])
        hi = first([P, 2, NC], I32)
        hif = first([P, 2, NC])
        sel_hi = first([P, 2, NC, NT])
        srcx = sb("srcx", [P, NCX], U32)
        dloc = sb("dloc", [P, NCX])
        e_c = sb("e_c", [P, NC, H])
        p_c = sb("p_c", [P, NCX, H])
        PIECE = 10
        keys = first([P, 2, 3, PIECE * P], BF16)
        prod = first([P, 5 * 2 * NT * H])
        S = sb("S", [P, 4, P])
        idx_stage = sb("idx_stage", [P, 2, IB], U32)
        low = first([1, NG], I32)
        lowf = first([1, NG])
        cnt = sb("cnt", [P, NX])
        cmp = first([P, NC])
        start_i = sb("start_i", [P, NX], I32)
        grp = sb("grp", [P, NX], I32)
        rem = sb("rem", [P, NX], I32)
        shift = sb("shift", [P, NX])
        witem = sb("witem", [1, NI], I32)
        kint = first([P, 3, 160], I32)
        kb = first([P, 3, 160], BF16)
        kpad = first([3, EPAD - NE], BF16)
        E1 = acc[0:NG, :, :].rearrange("p t d -> p (t d)")[:, 0:H * RW].rearrange("p (h k) -> p h k", h=H)
        E2 = acc[0:NG, :, :].rearrange("p t d -> p (t d)")[:, H * RW:2 * H * RW].rearrange("p (h k) -> p h k", h=H)
        F1 = xT[0:NG, :, :].rearrange("p t d -> p (t d)")[:, 0:H * RW].rearrange("p (h k) -> p h k", h=H)
        F2 = xT[0:NG, :, :].rearrange("p t d -> p (t d)")[:, H * RW:2 * H * RW].rearrange("p (h k) -> p h k", h=H)
        dx_i = first([NG, RW], I32)
        dx = first([NG, RW])
        eq = first([NG, RW])
        ends = sb("ends", [NG, 4, H])
        allsame = sb("allsame", [NG, 1])
        endsT = sb("endsT", [H, 4, NG])
        carry = sb("carry", [H, 2, NG + 1])
        router = Carver(acc[:, :, :].rearrange("p t d -> p (t d)"), NT * D)
        top = sb("top", [P, NT, 8])
        topi = sb("topi", [P, NT, 8], U32)
        wk = sb("wk", [P, NT, 2])
        wsum = sb("wsum", [P, NT])
        mean2 = sb("mean2", [P, NT])
        inv_r2 = sb("inv_r2", [P, NT])
        fac = sb("fac", [P, NT])
        slot_tab = sb("slot_tab", [TS, NTILE, 2], I32)
        slot_idx = sb("slot_idx", [P, NT, 2], U32)
        payload = sb("payload", [P, NT, 2, 2], I32)
        stage_g = sb("stage_g", [TS, U], U32)
        stage_s = sb("stage_s", [TS, U], U32)
        nover_i = sb("nover_i", [1, 1], I32)
        over_i = sb("over_i", [1, NOV], I32)
        later = Carver(arena, 17500)
        w13 = later([P, U, 2, A, HF])
        w2s = later([P, U, M, D])
        gam = later([NEX, D])
        bet = later([NEX, D])
        bb1 = later([NEX, 2, HF])
        wg = later([NEX, D])
        gT = later([P, 2, A, NEX])
        bT = later([P, 2, M, NEX])
        wgT = later([P, A, NEX])
        bg_b = later([P, NEX])
        shared = Carver(ring[:, :, :].rearrange("p k d -> p (k d)"), SLOTS * D)
        ws13 = shared([P, 2, A, HF])
        ws2 = shared([P, M, D])
        nxs = shared([P, A, 512])
        hsT = shared([P, M, NPAD])
        sil = shared([P, 512])
        yin = Carver(ring[:, :, :].rearrange("p k d -> p (k d)"), SLOTS * D)([P, 4, 2, D])
        lnp = later([P, 2, D])
        sg = later([P, 2, A])
        sbias = later([P, 2, M])
        b2a = later([NEX + 1, D])
        toks = Carver(xn[:, :, :].rearrange("p t d -> p (t d)"), NT * D)
        xg = toks([TS, U, D])
        yo = toks([TS, U, D])
        xgT = toks([P, 2, A, TS])
        lg = router([P, NT, NEX])
        oh = router([P, NT, 2, NEX])
        tmp = router([P, NT, 2, NEX])
        hits = router([P, NT, NEX])
        before = router([P, NT + 1, NEX])
        eidx = sb("eidx", [P, NT, 2])
        gates = Carver(hits[:, :, :].rearrange("p t e -> p (t e)"), NT * NEX)
        s1 = gates([P, 2, M, TS])
        hT = gates([P, 2, M, TS])
        topf = sb("topf", [P, NT, 2])
        rnk = sb("rnk", [P, NT, 2])
        kk = sb("kk", [P, NT, 2])
        obs = sb("obs", [P, NT, 2])
        real = sb("real", [P, 1])
        counts = sb("counts", [P, NEX])
        nov = sb("nov", [P, NEX])
        inc = sb("inc", [P, NEX])
        exc = sb("exc", [P, NEX])
        tri = sb("tri", [P, P])
        cw = lg
        cwT = tmp[0:NEX + 1, :, :, :].rearrange("p t k e -> p (t k e)")

        names = {}

        def s(name):
            if name not in names:
                names[name] = sem(name)
            return names[name]

        w_landed = [sem(f"w_landed{k}") for k in range(U)]
        xg_landed = [sem(f"xg_landed{k}") for k in range(U)]
        y_out = [sem(f"y_out{k}") for k in range(U)]
        landed = [sem(f"row_landed{k}") for k in range(SLOTS)]

        block = ctx.enter_context(nc.Block())

        ek = bkey_d
        x_main = x[0:(NT - 1) * P].rearrange("(t p) d -> p t d", p=P)
        PIECES = [(q * PIECE, min(PIECE, NC - q * PIECE)) for q in range(-(-NC // PIECE))]
        GROUPS = []
        for q, (c0, n) in enumerate(PIECES):
            for c in range(c0, c0 + n, 5):
                GROUPS.append((q, c, min(5, c0 + n - c)))
        KP = NE // 160

        @block.sync
        def _(sp):
            sp.wait_ge(s("erow_pad"), 1)
            for k, a in enumerate((src, dst, etype, eweight.bitcast(I32))):
                sp.dma_start(erow[:, 0, k, :], a[0:P * P].rearrange("(c e) -> c e", e=P)).then_inc(s("erow_in"), 16)
                sp.dma_start(erow[0:FULLC - P, 1, k, :],
                             a[P * P:FULLC * P].rearrange("(c e) -> c e", e=P)).then_inc(s("erow_in"), 16)
                sp.dma_start(erow[FULLC - P:FULLC - P + 1, 1, k, 0:REST],
                             a[FULLC * P:NE].rearrange("(a e) -> a e", a=1)).then_inc(s("erow_in"), 16)
            for k, a in enumerate((src, dst, etype)):
                sp.dma_start(kint[0:KP, k, :], a.rearrange("(p j) -> p j", j=160)).then_inc(s("key_in"), 16)
            sp.wait_ge(s("x_pad"), 1)
            for t in range(0, NT - 1, 3):
                sp.dma_start(x_sb[:, t:t + 3, :], x_main[:, t:t + 3, :]).then_inc(s("x_in"), 16)
            sp.dma_start(x_sb[0:LAST, NT - 1, :], x[(NT - 1) * P:N, :]).then_inc(s("x_in"), 16)
            sp.wait_ge(s("key_ready"), 3)
            for k in range(3):
                sp.dma_start(ek[k, 0:NE].rearrange("(p j) -> p j", j=160), kb[0:KP, k, :]).then_inc(s("key_out"), 16)
            sp.dma_start(ek[:, NE:EPAD], kpad[:, :]).then_inc(s("key_out"), 16)
            sp.wait_ge(s("key_out"), 64)
            for q, (c0, n) in enumerate(PIECES):
                if q >= 2:
                    sp.wait_ge(s("pe_sel"), sum(1 for g in GROUPS if g[0] <= q - 2))
                for k in range(3):
                    rows = P if k < 2 else TY
                    sp.dma_start(keys[0:rows, q % 2, k, 0:n * P],
                                 bass.AP(tensor=ek.tensor, offset=k * EPAD + c0 * P, ap=[[0, rows], [1, n * P]])
                                 ).then_inc(s(f"keys_landed{q % 2}"), 16)
            for t in range(NT):
                sp.wait_ge(s("act_h"), t + 1)
                sp.dma_start(h_d[t * P:(t + 1) * P, :], ring[:, t, :]).then_inc(s("h_out"), 16)
            sp.wait_ge(s("e_done"), 1)
            sp.wait_ge(s("dx_read"), 1)
            for o, i in ((gam[:, :], gamma[:, :]), (bet[:, :], beta[:, :]), (bb1[:, 0, :], b1[:, :]),
                         (bb1[:, 1, :], b3[:, :]), (wg[:, :], Wg[:, :]), (b2a[0:NEX, :], b2[:, :]),
                         (b2a[NEX:NEX + 1, :], bs2.rearrange("(a d) -> a d", a=1)),
                         (bg_b[:, :], bass.AP(tensor=bg.tensor, offset=0, ap=[[0, P], [1, NEX]])),
                         (lnp[:, 0, :], bass.AP(tensor=ln_gamma.tensor, offset=0, ap=[[0, P], [1, D]])),
                         (lnp[:, 1, :], bass.AP(tensor=ln_beta.tensor, offset=0, ap=[[0, P], [1, D]])),
                         (sg[:, 0, :], gs.rearrange("(p a) -> p a", a=A)), (sg[:, 1, :], bs.rearrange("(p a) -> p a", a=A)),
                         (sbias[:, 0, :], bs1.rearrange("(m p) -> p m", p=P)),
                         (sbias[:, 1, :], bs3.rearrange("(m p) -> p m", p=P))):
                sp.dma_start(o, i).then_inc(s("param_in"), 16)

            def load_expert(u, e):
                sp.dma_start(w13[:, u, 0, :, :].rearrange("p a h -> p (a h)"),
                             W1[e, :, :].rearrange("o (p a) h -> p (o a h)", a=A)).then_inc(w_landed[u], 16)
                sp.dma_start(w13[:, u, 1, :, :].rearrange("p a h -> p (a h)"),
                             W3[e, :, :].rearrange("o (p a) h -> p (o a h)", a=A)).then_inc(w_landed[u], 16)
                sp.dma_start(w2s[:, u, :, :], W2[e, :, :].rearrange("o (m p) d -> p (o m) d", p=P)).then_inc(w_landed[u], 16)

            for u in range(U):
                load_expert(u, bass.ds(u, 1))
            sp.wait_ge(s("pe_item"), NI)
            for k, w in enumerate((Ws1, Ws3)):
                sp.dma_start(ws13[:, k, :, :].rearrange("p a h -> p (a h)"),
                             w.rearrange("(p a) h -> p (a h)", a=A)).then_inc(s("sh_in"), 16)
            sp.dma_start(ws2[:, :, :], Ws2.rearrange("(m p) d -> p m d", p=P)).then_inc(s("sh_in"), 16)
            for t in range(NT):
                sp.wait_ge(s("nx_done"), t + 1)
                sp.dma_start(nx_d[t * P:(t + 1) * P, :], xn[:, t, :]).then_inc(s("nx_out"), 16)
            sp.wait_ge(s("slots_out"), 16 * 2 * NT)
            sp.dma_start(slot_tab[:, :, :], slot_d.rearrange("(r t) k -> r t k", t=NTILE)).then_inc(s("slot_in"), 16)
            with sp.Fori(1, NIT) as i:
                for u in range(U):
                    sp.wait_ge(s("pe_y"), U * (i - 1) + u + 1)
                    load_expert(u, bass.ds(U * i + u, 1))
            sp.wait_ge(s("over_done"), 1)
            sp.wait_ge(s("pe_y"), NEX)
            n = sp.value_load(nover_i[0:1, 0:1], min_val=0, max_val=NOV)
            with sp.If(n > 0):
                with sp.Fori(0, n) as j:
                    sp.wait_ge(s("ov_end"), j + 1)
                    e = sp.value_load(over_i[0:1, bass.ds(j, 1)], min_val=0, max_val=NEX - 1)
                    sp.dma_start(w13[:, 0, 0, :, :].rearrange("p a h -> p (a h)"),
                                 W1[bass.ds(e, 1), :, :].rearrange("o (p a) h -> p (o a h)", a=A)).then_inc(s("ov_w"), 16)
                    sp.dma_start(w13[:, 0, 1, :, :].rearrange("p a h -> p (a h)"),
                                 W3[bass.ds(e, 1), :, :].rearrange("o (p a) h -> p (o a h)", a=A)).then_inc(s("ov_w"), 16)
                    sp.dma_start(w2s[:, 0, :, :], W2[bass.ds(e, 1), :, :].rearrange("o (m p) d -> p (o m) d", p=P)
                                 ).then_inc(s("ov_w"), 16)
            sp.wait_ge(s("y_all"), 1)
            yv = y_d.rearrange("(t p k) d -> t p (k d)", p=P, k=2)
            for t in range(NT):
                if t >= 4:
                    sp.wait_ge(s("out_ready"), t - 3)
                rows = P if t < NT - 1 else LAST
                sp.dma_start(yin[0:rows, t % 4, :, :].rearrange("p k d -> p (k d)"), yv[t, 0:rows, :]).then_inc(s(f"y_in{t % 4}"), 16)

        @block.gpsimd
        def _(pool):
            pool.memset(erow[0:32, 1, 0:2, :], PADNODE)
            pool.memset(erow[0:32, 1, 2:4, :], 0).then_inc(s("erow_pad"), 1)
            pool.memset(dx_i[:, :], PADNODE).then_inc(s("dx_pad"), 1)
            pool.memset(ident[:, :], 0.0).then_inc(s("poolc"), 1)
            pool.wait_ge(s("poolc"), 1)
            pool.affine_select(out=ident[:, :], in_=ident[:, :], compare_op=ALU.not_equal, fill=1.0, base=0,
                               pattern=[[-1, P]], channel_multiplier=1)
            pool.memset(ones[:, :], 1.0)
            pool.iota(iota_p[:, :], pattern=[[0, 1]], base=0, channel_multiplier=1,
                      allow_small_or_imprecise_dtypes=True)
            pool.iota(iota_row[:, :], pattern=[[1, P]], base=0, channel_multiplier=0,
                      allow_small_or_imprecise_dtypes=True).then_inc(s("const"), 1)
            pool.memset(tri[:, :], 1.0)
            pool.memset(real[:, :], 1.0).then_inc(s("tri_done"), 1)
            pool.memset(slot_tab[:, :, 0:1], PADNODE)
            pool.memset(slot_tab[:, :, 1:2], SKIP).then_inc(s("fill"), 1)
            pool.wait_ge(s("tri_done"), 1)
            pool.affine_select(out=tri[:, :], in_=tri[:, :], compare_op=ALU.is_gt, fill=0.0, base=0,
                               pattern=[[1, P]], channel_multiplier=-1).then_inc(s("tri_done"), 1)
            pool.affine_select(out=real[:, :], in_=real[:, :], compare_op=ALU.is_gt, fill=0.0, base=LAST,
                               pattern=[[0, 1]], channel_multiplier=-1).then_inc(s("tri_done"), 1)
            pool.iota(payload[:, :, :, 0], pattern=[[P, NT], [0, 2]], base=0, channel_multiplier=1)
            pool.iota(payload[:, :, :, 1], pattern=[[2 * P, NT], [1, 2]], base=0, channel_multiplier=2).then_inc(s("tri_done"), 1)
            pool.wait_ge(s("srcx_done"), 1)
            pool.wait_ge(s("h_out"), 16 * NT)

            def settle(k):
                pool.tensor_tensor(spare[:, k:k + 1], iota_p[:, :], iota_p[:, :], ALU.add)

            def body(i, first):
                for half in range(2):
                    if not first:
                        for k in range(half * IB, (half + 1) * IB):
                            pool.wait_ge(landed[k], 16 * i)
                    if not first:
                        settle(12 + half)
                    pool.tensor_copy(idx_stage[:, half, :], srcx[:, bass.ds(SLOTS * i + IB * half, IB)]
                                     ).then_inc(s("stage"), 1)
                    pool.wait_ge(s("stage"), 2 * i + half + 1)
                    settle(14 + half)
                    for k in range(IB):
                        slot = half * IB + k
                        if not first and k % 2 == 0:
                            pool.wait_ge(s("pe_item"), IB * (i - 1) + slot // 2 + 1)
                            settle(slot // 2)
                        pool.indirect_dma_start(
                            out=ring[:, slot, :], out_offset=None, in_=h_d[:, :],
                            in_offset=bass.IndirectOffsetOnAxis(ap=idx_stage[:, half, k:k + 1], axis=0)
                        ).then_inc(landed[slot], 16)

            body(0, True)
            with pool.Fori(1, ITER) as i:
                body(i, False)
            pool.wait_ge(s("param_in"), 16 * 14)
            for t in range(NT):
                o = pool.tensor_tensor(x_sb[:, t, :], x_sb[:, t, :], lnp[:, 1, :], ALU.add)
            o.then_inc(s("poolc"), 1)
            pool.wait_ge(s("poolc"), 2)
            for t in range(NT):
                pool.wait_ge(s("gnn_norm"), t + 1)
                pool.tensor_tensor(acc[:, t, :], acc[:, t, :], lnp[:, 0, :], ALU.mult).then_inc(s("gnn_gam"), 1)
                pool.wait_ge(s("gnn_gam"), t + 1)
                pool.tensor_tensor(x_sb[:, t, :], x_sb[:, t, :], acc[:, t, :], ALU.add).then_inc(s("x1_done"), 1)
            pool.wait_ge(s("pos_done"), 1)
            pool.wait_ge(s("tri_done"), 4)
            pool.wait_ge(s("filled"), 16)
            for t in range(NT):
                rows = P if t < NT - 1 else LAST
                for k in range(2):
                    pool.indirect_dma_start(out=slot_d[:, :], out_offset=bass.IndirectOffsetOnAxis(ap=slot_idx[0:rows, t, k:k + 1], axis=0),
                                            in_=payload[0:rows, t, k, :], in_offset=None).then_inc(s("slots_out"), 16)
            pool.wait_ge(s("slot_in"), 16)
            pool.wait_ge(s("nx_out"), 16 * NT)
            pool.wait_ge(s("pe_nxT"), NT)

            def gather(u, sems):
                pool.indirect_dma_start(out=xg[:, u, :], out_offset=None, in_=nx_d[:, :],
                                        in_offset=bass.IndirectOffsetOnAxis(ap=stage_g[:, u:u + 1], axis=0)).then_inc(sems, 16)

            def scatter(u, y, sems):
                pool.indirect_dma_start(out=y_d[:, :], out_offset=bass.IndirectOffsetOnAxis(ap=stage_s[:, u:u + 1], axis=0),
                                        in_=yo[:, y, :], in_offset=None, bounds_check=2 * NPAD - 1,
                                        oob_is_err=False).then_inc(sems, 16)

            pool.tensor_copy(stage_g[:, :], slot_tab[:, 0:U, 0]).then_inc(s("stage_g"), 1)
            pool.wait_ge(s("stage_g"), 1)
            for u in range(U):
                gather(u, xg_landed[u])

            def experts(i, first, last):
                if not first:
                    for u in range(U):
                        pool.wait_ge(y_out[u], 16 * i)
                if not last:
                    for u in range(U):
                        pool.wait_ge(xg_landed[u], 16 * i + 16)
                    pool.tensor_tensor(spare[:, 0:1], iota_p[:, :], iota_p[:, :], ALU.add)
                    pool.tensor_copy(stage_g[:, :], slot_tab[:, bass.ds(U * i + U, U), 0])
                elif not first:
                    pool.tensor_tensor(spare[:, 0:1], iota_p[:, :], iota_p[:, :], ALU.add)
                pool.tensor_copy(stage_s[:, :], slot_tab[:, bass.ds(U * i, U), 1]).then_inc(s("stage_s"), 1)
                pool.wait_ge(s("stage_s"), i + 1)
                settle(1)
                for u in range(U):
                    if not last:
                        pool.wait_ge(s("pe_xgT"), U * i + u + 1)
                        settle(2 + 2 * u)
                        gather(u, xg_landed[u])
                    pool.wait_ge(s("y_ready"), U * i + u + 1)
                    settle(3 + 2 * u)
                    scatter(u, u, y_out[u])

            experts(0, True, False)
            with pool.Fori(1, NIT - 1) as i:
                experts(i, False, False)
            experts(NIT - 1, False, True)
            for u in range(U):
                pool.wait_ge(y_out[u], 16 * NIT)
            n = pool.value_load(nover_i[0:1, 0:1], min_val=0, max_val=NOV)
            with pool.If(n > 0):
                with pool.Fori(0, n) as j:
                    pool.wait_ge(s("ov_end"), j + 1)
                    settle(10)
                    pool.tensor_copy(stage_g[:, 0:1], slot_tab[:, bass.ds(NEX + j, 1), 0])
                    pool.tensor_copy(stage_s[:, 0:1], slot_tab[:, bass.ds(NEX + j, 1), 1]).then_inc(s("ov_stage"), 1)
                    pool.wait_ge(s("ov_stage"), j + 1)
                    settle(11)
                    gather(0, s("ov_g"))
                    pool.wait_ge(s("ov_step"), 7 * j + 7)
                    settle(12)
                    scatter(0, 0, s("ov_s"))
                    pool.wait_ge(s("ov_s"), 16 * j + 16)
                    pool.tensor_tensor(spare[:, 13:14], iota_p[:, :], iota_p[:, :], ALU.add).then_inc(s("ov_end"), 1)
            pool.nop().then_inc(s("y_all"), 1)

        @block.scalar
        def _(act):
            act.dma_start(W_sb[:, :, :], W.rearrange("(t p) d -> p t d", p=P)).then_inc(s("w_in"), 16)
            act.dma_start(attn[:, 0, :], a_src.rearrange("h d -> (h d)").rearrange("(t p) -> p t", p=P)).then_inc(s("small_in"), 16)
            act.dma_start(attn[:, 1, :], a_dst.rearrange("h d -> (h d)").rearrange("(t p) -> p t", p=P)).then_inc(s("small_in"), 16)
            act.dma_start(emb[:, :], et_emb[:, :]).then_inc(s("small_in"), 16)
            act.dma_start(low[:, :], bass.AP(tensor=dst.tensor, offset=0, ap=[[0, 1], [GE, NG]])).then_inc(s("small_in"), 16)
            act.wait_ge(s("dx_pad"), 1)
            act.dma_start(dx_i[1:NG - 1, :], bass.AP(tensor=dst.tensor, offset=GE - 1, ap=[[GE, NG - 2], [1, RW]])).then_inc(s("dx_in"), 16)
            act.dma_start(dx_i[0:1, 1:RW], dst[0:RW - 1].rearrange("(a e) -> a e", a=1)).then_inc(s("dx_in"), 16)
            act.dma_start(dx_i[NG - 1:NG, 0:NE - (NG - 1) * GE + 1],
                          dst[(NG - 1) * GE - 1:NE].rearrange("(a e) -> a e", a=1)).then_inc(s("dx_in"), 16)
            act.wait_ge(s("fill"), 1)
            act.dma_start(slot_d.rearrange("(r t) k -> r t k", t=NTILE), slot_tab[:, :, :]).then_inc(s("filled"), 16)
            act.wait_ge(s("ln_scr"), 1)
            act.activation(rstd[:, :], rstd[:, :], ACT.Sqrt).then_inc(s("ln1_std"), 1)
            for a in range(A):
                act.wait_ge(s("pe_wt"), a + 1)
                act.copy(WT[:, a, :], ps[:, 6 + a % 2, :]).then_inc(s("act_wt"), 1)
            act.wait_ge(s("pe_v"), 1)
            act.copy(V[:, :, :].rearrange("p a h -> p (a h)"), ps[:, 3, 0:A * 2 * H]).then_inc(s("v_done"), 1)
            for t in range(NT):
                act.wait_ge(s("pe_xt"), t + 1)
                act.copy(xT[:, :, t * P:(t + 1) * P],
                         ps[:, t % 2, :].rearrange("p (a n) -> p a n", a=A)).then_inc(s("act_xt"), 1)
            for t in range(NT):
                act.wait_ge(s("pe_h"), t + 1)
                act.copy(ring[:, t, :], ps[:, 7, :]).then_inc(s("act_h"), 1)
            for b in range(4):
                act.wait_ge(s("pe_er"), b + 1)
                for k in range(4):
                    h, q = (4 * b + k) // 2, (4 * b + k) % 2
                    act.copy(E1[:, h, 1 + q * P:1 + (q + 1) * P], ps[0:NG, b, k * P:(k + 1) * P]).then_inc(s("act_er"), 1)
            act.wait_ge(s("dve_d"), 1)
            act.activation(p_c[:, 0:NC, :], e_c[:, :, :], ACT.Exp).then_inc(s("p_done"), 1)
            act.wait_ge(s("px_done"), 1)

            def body(i, first):
                for k in range(SLOTS):
                    act.wait_ge(landed[k], 16 * i + 16)
                    for h in (H - 2, H - 1):
                        o = act.activation(ring[:, k, h * HD:(h + 1) * HD], ring[:, k, h * HD:(h + 1) * HD], ACT.Copy,
                                           scale=p_c[:, bass.ds(SLOTS * i + k, 1), h:h + 1].rearrange("p a b -> p (a b)"))
                    o.then_inc(s("act_msg"), 1)

            body(0, True)
            with act.Fori(1, ITER) as i:
                body(i, False)
            half = NT // 2

            def root(name, k, a):
                act.wait_ge(s(name + "_var"), k)
                act.activation(a, a, ACT.Sqrt).then_inc(s(name + "_std"), 1)

            def gnn_norm(k):
                for t in range(k * half, (k + 1) * half):
                    act.activation(acc[:, t, :], acc[:, t, :], ACT.Identity, bias=mean2[:, t:t + 1],
                                   scale=rstd[:, t:t + 1]).then_inc(s("gnn_norm"), 1)

            def x1_norm(k):
                for t in range(k * half, (k + 1) * half):
                    act.activation(xn[:, t, :], x_sb[:, t, :], ACT.Identity, bias=mean2[:, t:t + 1],
                                   scale=fac[:, t:t + 1]).then_inc(s("nx_done"), 1)

            for k in range(2):
                root("gnn", k + 1, rstd[:, k * half:(k + 1) * half])
                act.wait_ge(s("gnn_var"), 3 + k)
                gnn_norm(k)
            for k in range(2):
                root("x1", k + 1, rstd[:, k * half:(k + 1) * half])
                act.wait_ge(s("r2_var"), k + 1)
                act.activation(inv_r2[:, k * half:(k + 1) * half], inv_r2[:, k * half:(k + 1) * half],
                               ACT.Sqrt).then_inc(s("r2_std"), 1)
                act.wait_ge(s("nx_ready"), k + 1)
                x1_norm(k)
            for t in range(NT):
                act.wait_ge(s("pe_nxT"), t + 1)
                act.copy(xT[:, :, t * P:(t + 1) * P],
                         ps[:, t % 2, :].rearrange("p (a n) -> p a n", a=A)).then_inc(s("act_nxT"), 1)
            act.wait_ge(s("top_done"), 1)
            act.activation(wk[:, :, :], topf[:, :, :], ACT.Exp, scale=-1.0).then_inc(s("exp_top"), 1)
            for n in range(-(-NPAD // 512)):
                c0, c1 = 512 * n, min(512 * n + 512, NPAD)
                if n:
                    act.wait_ge(s("pe_sh3"), M * n)
                for a in range(A):
                    act.activation(nxs[:, a, 0:c1 - c0], xT[:, a, c0:c1], ACT.Identity, bias=sg[:, 1, a:a + 1],
                                   scale=sg[:, 0, a:a + 1]).then_inc(s("nxs_done"), 1)
                for m in range(M):
                    k = M * n + m
                    act.wait_ge(s("pe_sh1"), k + 1)
                    if k:
                        act.wait_ge(s("hs_done"), k)
                    act.activation(sil[:, 0:c1 - c0], ps[:, 2 * (k % 2), 0:c1 - c0], ACT.Silu,
                                   bias=sbias[:, 0, m:m + 1]).then_inc(s("act_sh"), 1)

            def gate(u, e, k, done, bank):
                for m in range(M):
                    o = act.activation(s1[:, k, m, :], ps[:, bank, m * TS:(m + 1) * TS], ACT.Silu,
                                       bias=bT[:, 0, m, e])
                o.then_inc(s(done), 1)

            def out_rows(y, bank, done):
                act.copy(yo[:, y, :], ps[0:TS, bank, :]).then_inc(s(done), 1)

            def experts(i, lo):
                for u in range(U):
                    act.wait_ge(s("pe_h1"), U * i + u + 1)
                    if U * lo + u >= 2:
                        act.wait_ge(s("hT_done"), U * i + u - 1)
                    gate(u, bass.ds(U * i + u, 1), u % 2, "act_s1", 2 + u % 2)
                    if U * lo + u >= 1:
                        act.wait_ge(s("pe_y"), U * i + u)
                        if U * lo + u - 1 >= U:
                            act.wait_ge(y_out[(u - 1) % U], 16 * i if u else 16 * i - 16)
                        out_rows((u - 1) % U, 6 + (u - 1) % 2, "y_ready")

            experts(0, 0)
            experts(1, 1)
            with act.Fori(2, NIT) as i:
                experts(i, 2)
            act.wait_ge(s("pe_y"), NEX)
            act.wait_ge(y_out[U - 1], 16 * (NIT - 1))
            out_rows(U - 1, 6 + (U - 1) % 2, "y_ready")
            act.wait_ge(s("over_done"), 1)
            n = act.value_load(nover_i[0:1, 0:1], min_val=0, max_val=NOV)
            with act.If(n > 0):
                with act.Fori(0, n) as j:
                    act.wait_ge(s("ov_step"), 7 * j + 3)
                    e = act.value_load(over_i[0:1, bass.ds(j, 1)], min_val=0, max_val=NEX - 1)
                    gate(0, bass.ds(e, 1), 0, "ov_step", 2)
                    act.wait_ge(s("ov_step"), 7 * j + 6)
                    out_rows(0, 6, "ov_step")
            for t in range(NT):
                act.wait_ge(s("out_ready"), t + 1)
                rows = P if t < NT - 1 else LAST
                act.dma_start(out[t * P:t * P + rows, :], x_sb[0:rows, t, :]).then_inc(s("stored"), 16)
            act.wait_ge(s("stored"), 16 * NT)

        @block.tensor
        def _(pe):
            def T(o, i, n=P):
                return pe.transpose(o, i, ident[0:n, 0:n])

            pe.wait_ge(s("const"), 1)
            pe.wait_ge(s("erow_f"), 1)
            for k in range(4):
                b, col = 4 + k // 2, (k % 2) * NC
                T(ps[:, b, col:col + P], erowf[:, 0, k, :])
                o = T(ps[:, b, col + P:col + NC], erowf[0:NC - P, 1, k, :], NC - P)
            o.then_inc(s("pe_erow"), 1)
            pe.wait_ge(s("w_in"), 16)
            for a in range(A):
                if a >= 2:
                    pe.wait_ge(s("act_wt"), a - 1)
                for t in range(A):
                    o = T(ps[:, 6 + a % 2, t * P:(t + 1) * P], W_sb[:, t, a * P:(a + 1) * P])
                o.then_inc(s("pe_wt"), 1)
            pe.wait_ge(s("ablk_done"), 1)
            for a in range(A):
                for t in range(A):
                    o = pe.matmul(ps[:, 3, a * 2 * H:(a + 1) * 2 * H], W_sb[:, t, a * P:(a + 1) * P],
                                  ablk[:, t * 2 * H:(t + 1) * 2 * H], start=(t == 0), stop=(t == A - 1))
            o.then_inc(s("pe_v"), 1)
            for t in range(NT):
                pe.wait_ge(s("ln1"), t + 1)
                if t >= 2:
                    pe.wait_ge(s("act_xt"), t - 1)
                for a in range(A):
                    o = T(ps[:, t % 2, a * P:(a + 1) * P], xn[:, t, a * P:(a + 1) * P])
                o.then_inc(s("pe_xt"), 1)
            pe.wait_ge(s("v_done"), 1)
            for t in range(NT):
                pe.wait_ge(s("act_xt"), t + 1)
                for a in range(A):
                    o = pe.matmul(ps[:, 2, t * 2 * H:(t + 1) * 2 * H], xT[:, a, t * P:(t + 1) * P], V[:, a, :],
                                  start=(a == 0), stop=(a == A - 1))
            o.then_inc(s("pe_tab"), 1)
            pe.wait_ge(s("srcx_done"), 1)
            pe.matmul(ps[:, 6, 0:NX], ones[:, :], cnt[:, :], start=True, stop=True)
            pe.matmul(ps[:, 6, 64:64 + NG], ones[0:1, :], lowf[:, :], start=True, stop=True).then_inc(s("pe_low"), 1)

            def h_tile(t):
                if t == 0:
                    pe.wait_ge(s("act_wt"), A)
                else:
                    pe.wait_ge(s("act_h"), t)
                for a in range(A):
                    o = pe.matmul(ps[:, 7, :], xT[:, a, t * P:(t + 1) * P], WT[:, a, :],
                                  start=(a == 0), stop=(a == A - 1))
                o.then_inc(s("pe_h"), 1)

            pe.wait_ge(s("tab_done"), 1)
            pe.wait_ge(s("emb_done"), 1)
            pe.wait_ge(s("dve_low"), 1)
            for g, (q, c0, n) in enumerate(GROUPS):
                if g == 0 or GROUPS[g - 1][0] != q:
                    pe.wait_ge(s("hot"), q + 1)
                if g >= 2:
                    pe.wait_ge(s("sel_read"), g - 1)
                for side in range(2):
                    for c in range(c0, c0 + n):
                        oh = keys[:, q % 2, side, (c - PIECES[q][0]) * P:(c - PIECES[q][0] + 1) * P]
                        for r in range(3):
                            o = pe.matmul(ps[:, 2 * (g % 2) + side, (c - c0) * NT * H:(c - c0 + 1) * NT * H], oh,
                                          tab3[:, r, side, :], start=(r == 0), stop=(r == 2))
                for c in range(c0, c0 + n):
                    oh = keys[0:TY, q % 2, 2, (c - PIECES[q][0]) * P:(c - PIECES[q][0] + 1) * P]
                    for r in range(3):
                        o = pe.matmul(ps[:, 4 + c // 64, (c % 64) * H:(c % 64 + 1) * H], oh, emb3[:, r, :],
                                      start=(r == 0), stop=(r == 2))
                o.then_inc(s("pe_sel"), 1)
                if g % 3 == 2 and g // 3 < NT:
                    h_tile(g // 3)
            pe.wait_ge(s("e_done"), 1)
            for b in range(4):
                for k in range(4):
                    h, q = (4 * b + k) // 2, (4 * b + k) % 2
                    o = T(ps[0:NG, b, k * P:(k + 1) * P], e_c[:, q::2, h])
                o.then_inc(s("pe_er"), 1)
            pe.wait_ge(s("ends_done"), 1)
            for k in range(4):
                o = T(ps[0:H, 4, k * NG:(k + 1) * NG], ends[:, k, :], NG)
            o.then_inc(s("pe_ends"), 1)
            pe.wait_ge(s("carry_done"), 1)
            T(ps[0:NG, 5, 0:H], carry[:, 0, 0:NG], H)
            T(ps[0:NG, 5, H:2 * H], carry[:, 1, 1:NG + 1], H).then_inc(s("pe_carry"), 1)
            pe.wait_ge(s("m_done"), 1)
            for k in range(2 * H):
                h, q = k // 2, k % 2
                o = T(ps[:, k // 6, (k % 6) * NG:(k % 6 + 1) * NG], E1[:, h, 1 + q * P:1 + (q + 1) * P], NG)
            o.then_inc(s("pe_m"), 1)

            def body(i, first):
                for j in range(IB):
                    if not (first and j < 4):
                        pe.wait_ge(s("acc_done"), IB * i + j - 3)
                    for u in range(2):
                        k = 2 * j + u
                        pe.wait_ge(s("dve_msg"), SLOTS * i + k + 1)
                        pe.wait_ge(s("act_msg"), SLOTS * i + k + 1)
                        pe.matmul(ps[:, j % 4, :], S[:, k % 4, :], ring[:, k, :], start=(u == 0), stop=(u == 1))
                    for u in range(2):
                        k = 2 * j + u
                        o = pe.matmul(ps[:, 4 + j % 4, 0:H], S[:, k % 4, :],
                                      p_c[:, bass.ds(SLOTS * i + k, 1), :].rearrange("p a h -> p (a h)"),
                                      start=(u == 0), stop=(u == 1))
                    o.then_inc(s("pe_item"), 1)

            body(0, True)
            with pe.Fori(1, ITER) as i:
                body(i, False)
            pe.wait_ge(s("param_in"), 16 * 14)
            pe.wait_ge(s("acc_done"), NI)
            for a in range(A):
                T(ps[:, 4, a * NEX:(a + 1) * NEX], gam[:, a::A], NEX)
                T(ps[:, 4, (A + a) * NEX:(A + a + 1) * NEX], bet[:, a::A], NEX)
                T(ps[:, 5, (A + a) * NEX:(A + a + 1) * NEX], wg[:, a::A], NEX)
            for k in range(2):
                for m in range(M):
                    o = T(ps[:, 5, (k * M + m) * NEX:(k * M + m + 1) * NEX], bb1[:, k, m * P:(m + 1) * P], NEX)
            o.then_inc(s("pe_param"), 1)
            for t in range(NT):
                pe.wait_ge(s("nx_done"), t + 1)
                if t >= 2:
                    pe.wait_ge(s("act_nxT"), t - 1)
                for a in range(A):
                    o = T(ps[:, t % 2, a * P:(a + 1) * P], xn[:, t, a::A])
                o.then_inc(s("pe_nxT"), 1)
            pe.wait_ge(s("param_done"), 1)
            for t in range(NT):
                pe.wait_ge(s("act_nxT"), t + 1)
                if t >= 2:
                    pe.wait_ge(s("lg_read"), t - 1)
                for a in range(A):
                    o = pe.matmul(ps[:, 2 + t % 2, 0:NEX], xT[:, a, t * P:(t + 1) * P], wgT[:, a, :],
                                  start=(a == 0), stop=(a == A - 1))
                o.then_inc(s("pe_lg"), 1)
            pe.wait_ge(s("lg_read"), NT)
            pe.wait_ge(s("sh_in"), 48)

            def shared_up(n):
                c0, c1 = 512 * n, min(512 * n + 512, NPAD)
                for m in range(M):
                    k = M * n + m
                    pe.wait_ge(s("nxs_done"), A * (n + 1))
                    if k >= 2:
                        pe.wait_ge(s("act_sh"), k - 1)
                        pe.wait_ge(s("hs_done"), k - 1)
                    for w in range(2):
                        for a in range(A):
                            o = pe.matmul(ps[:, 2 * (k % 2) + w, 0:c1 - c0], ws13[:, w, a, m * P:(m + 1) * P],
                                          nxs[:, a, 0:c1 - c0], start=(a == 0), stop=(a == A - 1))
                        o.then_inc(s("pe_sh1" if w == 0 else "pe_sh3"), 1)

            shared_up(0)
            pe.wait_ge(s("before_done"), 1)
            for t in range(NT):
                o = ps[:, 6 + t // 8, (t % 8) * NEX:(t % 8 + 1) * NEX]
                pe.matmul(o, tri[:, :], hits[:, t, :], start=True, stop=False)
                pe.matmul(o, ones[:, :], before[:, t, :], start=False, stop=True)
            pe.matmul(ps[:, 7, 2 * NEX:3 * NEX], ones[:, :], before[:, NT, :], start=True, stop=True).then_inc(s("pe_rank"), 1)
            for n in range(1, -(-NPAD // 512)):
                shared_up(n)
            pe.wait_ge(s("cw_done"), 1)
            for t in range(NT):
                o = T(ps[0:NEX, 4 + t // 4, (t % 4) * P:(t % 4 + 1) * P], cw[:, t, :])
            o.then_inc(s("pe_cwT"), 1)
            pe.wait_ge(s("cwT_done"), 1)
            pe.wait_ge(s("hs_done"), M * (-(-NPAD // 512)))
            for t in range(NT):
                if t >= 2:
                    pe.wait_ge(s("z_added"), t - 1)
                z = ps[:, 4 + t % 2, :]
                for m in range(M):
                    pe.matmul(z, hsT[:, m, t * P:(t + 1) * P], ws2[:, m, :], start=(m == 0), stop=False)
                pe.matmul(z, cwT[:, t * P:(t + 1) * P], b2a[:, :], start=False, stop=True).then_inc(s("pe_z"), 1)

            def turn(u, bank, done):
                for a in range(A):
                    o = T(ps[:, bank, a * TS:(a + 1) * TS], xg[:, u, a::A], TS)
                o.then_inc(s(done), 1)

            def up(u, k, bank, done1, done3):
                for w, done in ((0, done1), (1, done3)):
                    for m in range(M):
                        for a in range(A):
                            o = pe.matmul(ps[:, bank + 2 * w, m * TS:(m + 1) * TS], w13[:, u, w, a, m * P:(m + 1) * P],
                                          xgT[:, k, a, :], start=(a == 0), stop=(a == A - 1))
                    if done:
                        o.then_inc(s(done), 1)

            def down(u, k, bank, done):
                for m in range(M):
                    o = pe.matmul(ps[0:TS, bank, :], hT[:, k, m, :], w2s[:, u, m, :], start=(m == 0), stop=(m == M - 1))
                o.then_inc(s(done), 1)

            def experts(i, lo, last):
                for u in range(U):
                    e = U * i + u
                    pe.wait_ge(w_landed[u], 48 * i + 48)
                    pe.wait_ge(s("xgT_done"), e + 1)
                    if U * lo + u >= 2:
                        pe.wait_ge(s("act_s1"), e - 1)
                        pe.wait_ge(s("hT_done"), e - 1)
                    up(u, u % 2, 2 + u % 2, "pe_h1", "pe_h3")
                    if not (last and u == U - 1):
                        v_ = (u + 1) % U
                        pe.wait_ge(xg_landed[v_], 16 * i + (16 if v_ else 32))
                        turn(v_, (u + 1) % 2, "pe_xgT")
                    if U * lo + u >= 1:
                        pe.wait_ge(s("hT_done"), e)
                        if U * lo + u >= 3:
                            pe.wait_ge(s("y_ready"), e - 2)
                        down((u - 1) % U, (u - 1) % 2, 6 + (u - 1) % 2, "pe_y")

            pe.wait_ge(xg_landed[0], 16)
            pe.wait_ge(s("z_added"), NT)
            turn(0, 0, "pe_xgT")
            experts(0, 0, False)
            with pe.Fori(1, NIT - 1) as i:
                experts(i, 1, False)
            experts(NIT - 1, NIT - 1, True)
            pe.wait_ge(s("hT_done"), NEX)
            pe.wait_ge(s("y_ready"), NEX - 2)
            down(U - 1, (U - 1) % 2, 6 + (U - 1) % 2, "pe_y")
            pe.wait_ge(s("over_done"), 1)
            pe.wait_ge(s("y_ready"), NEX)
            n = pe.value_load(nover_i[0:1, 0:1], min_val=0, max_val=NOV)
            with pe.If(n > 0):
                with pe.Fori(0, n) as j:
                    pe.wait_ge(s("ov_g"), 16 * j + 16)
                    turn(0, 0, "ov_step")
                    pe.wait_ge(s("ov_step"), 7 * j + 2)
                    pe.wait_ge(s("ov_w"), 48 * j + 48)
                    up(0, 0, 2, None, "ov_step")
                    pe.wait_ge(s("ov_step"), 7 * j + 5)
                    down(0, 0, 6, "ov_step")

        @block.vector
        def _(v):
            chain = [0]

            def link(ins):
                chain[0] += 1
                ins.then_inc(s("dve"), 1)
                v.wait_ge(s("dve"), chain[0])

            v.memset(x_sb[96:P, NT - 1, :], 0.0).then_inc(s("x_pad"), 1)
            v.wait_ge(s("key_in"), 48)
            v.tensor_single_scalar(kint[0:KP, 0, :], kint[0:KP, 0, :], P - 1, op=ALU.bitwise_and)
            link(v.tensor_single_scalar(kint[0:KP, 1, :], kint[0:KP, 1, :], P - 1, op=ALU.bitwise_and))
            v.tensor_copy(kb[0:KP, :, :], kint[0:KP, :, :]).then_inc(s("key_ready"), 1)
            v.memset(kpad[:, :], float(PADNODE % P)).then_inc(s("key_ready"), 1)
            v.nop().then_inc(s("key_ready"), 1)
            v.wait_ge(s("erow_in"), 16 * 12)
            v.tensor_copy(erowf[:, 0, 0:3, :], erow[:, 0, 0:3, :])
            v.tensor_copy(erowf[:, 0, 3, :], erow[:, 0, 3, :].bitcast(F32))
            v.tensor_copy(erowf[0:32, 1, 0:3, :], erow[0:32, 1, 0:3, :])
            v.tensor_copy(erowf[0:32, 1, 3, :], erow[0:32, 1, 3, :].bitcast(F32)).then_inc(s("erow_f"), 1)
            v.wait_ge(s("small_in"), 64)
            link(v.memset(ablk[:, :], 0.0))
            for side in range(2):
                for half in range(2):
                    rows = slice(64 * half, 64 * half + 64)
                    o = side * H + half
                    last = v.tensor_copy(ablk[rows, o:o + 3 * (2 * H + 2) + 1:2 * H + 2], attn[rows, side, :])
            last.then_inc(s("ablk_done"), 1)

            def split(parts, value, rest):
                link(v.tensor_copy(parts[0], value))
                link(v.tensor_tensor(rest, value, parts[0], ALU.subtract))
                link(v.tensor_copy(parts[1], rest))
                link(v.tensor_tensor(rest, rest, parts[1], ALU.subtract))
                link(v.tensor_copy(parts[2], rest))

            link(v.tensor_scalar(emb[:, :], emb[:, :], 1.0, None, ALU.add))
            split([emb3[:, r, :] for r in range(3)], emb[:, :], embr[:, :])
            v.nop().then_inc(s("emb_done"), 1)
            v.wait_ge(s("x_in"), 64)
            for t in range(NT):
                o = v.bn_stats(stats[:, t, :], x_sb[:, t, :])
            link(o)
            for t in range(NT):
                o = v.bn_aggr(mv[:, t, :], stats[:, t, :])
            link(o)
            v.tensor_scalar(rstd[:, :], mv[:, :, 1], EPS, None, ALU.add).then_inc(s("ln_scr"), 1)
            v.wait_ge(s("ln1_std"), 1)
            link(v.reciprocal(rstd[:, :], rstd[:, :]))
            for t in range(NT):
                v.tensor_scalar(xn[:, t, :], x_sb[:, t, :], mv[:, t, 0:1], rstd[:, t:t + 1],
                                ALU.subtract, ALU.mult).then_inc(s("ln1"), 1)
            v.wait_ge(s("pe_erow"), 1)
            v.tensor_copy(ecol[:, 0:2, :], ps[:, 4, 0:2 * NC].rearrange("p (k c) -> p k c", k=2))
            link(v.tensor_copy(ecol[:, 2:4, :], ps[:, 5, 0:2 * NC].rearrange("p (k c) -> p k c", k=2)))
            v.wait_ge(s("const"), 1)
            link(v.tensor_single_scalar(low[:, :], low[:, :], 7, op=ALU.arith_shift_right))
            v.tensor_copy(lowf[:, :], low[:, :])
            v.tensor_copy(witem[:, 0:NG], low[:, :])
            for w in range(NX):
                v.memset(witem[:, NG + w:NG + w + 1], w + 1)
                link(v.tensor_scalar(cmp[:, :], ecol[:, 1, :], float(P * (w + 1)), 0.0, ALU.is_lt, ALU.add,
                                     accum_out=cnt[:, w:w + 1]))
            v.tensor_copy(srcx[:, 0:NC], ecol[:, 0, :])
            link(v.tensor_copy(hi[:, :, :], ecol[:, 0:2, :]))
            link(v.tensor_single_scalar(hi[:, :, :], hi[:, :, :], 7, op=ALU.arith_shift_right))
            link(v.tensor_copy(hif[:, :, :], hi[:, :, :]))
            v.nop().then_inc(s("srcx_done"), 1)
            ib = iota_row[:, 0:NT].unsqueeze(1).to_broadcast([P, 2 * NC, NT])
            v.tensor_tensor(sel_hi[:, :, :, :].rearrange("p s c a -> p (s c) a"),
                            hif[:, :, :].rearrange("p s c -> p (s c)").unsqueeze(2).to_broadcast([P, 2 * NC, NT]), ib, ALU.is_equal)
            v.wait_ge(s("pe_tab"), 1)
            pt = ps[:, 2, 0:NT * 2 * H].rearrange("p (a s h) -> p s a h", a=NT, s=2)
            link(v.tensor_copy(tab[:, :, :].rearrange("p s (a h) -> p s a h", a=NT), pt))
            tf = tab[:, :, :].rearrange("p s k -> p (s k)")
            split([tab3[:, r, :, :].rearrange("p s k -> p (s k)") for r in range(3)], tf, tabr[:, :])
            v.nop().then_inc(s("tab_done"), 1)
            v.wait_ge(s("pe_low"), 1)
            link(v.tensor_copy(start_i[:, :], ps[:, 6, 0:NX]))
            v.tensor_single_scalar(grp[:, :], start_i[:, :], 8, op=ALU.arith_shift_right)
            link(v.tensor_single_scalar(rem[:, :], start_i[:, :], GE - 1, op=ALU.bitwise_and))
            link(v.tensor_scalar(shift[:, :], rem[:, :], 0.0, 1.0e6, ALU.is_equal, ALU.mult))
            for w in range(NX):
                o = v.tensor_scalar(shift[:, w:w + 1], shift[:, w:w + 1], float(P * (w + 1)), None, ALU.add)
            link(o)
            lo2 = ps[:, 6, 64:64 + NG].unsqueeze(2).to_broadcast([P, NG, 2])
            v.scalar_tensor_tensor(out=dloc[:, 0:NC].rearrange("p (g u) -> p g u", u=2), in0=lo2, scalar=-float(P),
                                   in1=ecol[:, 1, :].rearrange("p (g u) -> p g u", u=2), op0=ALU.mult,
                                   op1=ALU.add).then_inc(s("dve_low"), 1)
            for w in range(NX):
                g = v.value_load(grp[0:1, w:w + 1], min_val=0, max_val=NG - 1)
                c = NC + 2 * w
                v.tensor_copy(srcx[:, c:c + 2], ecol[:, 0, bass.ds(2 * g, 2)])
                v.tensor_scalar(dloc[:, c:c + 2], ecol[:, 1, bass.ds(2 * g, 2)], shift[:, w:w + 1], None, ALU.subtract)
            v.nop().then_inc(s("srcx_done"), 1)
            v.wait_ge(s("dx_in"), 48)
            link(v.tensor_copy(dx[:, :], dx_i[:, :]))
            link(v.tensor_tensor(eq[:, 1:RW], dx[:, 1:RW], dx[:, 0:RW - 1], ALU.is_equal))
            link(v.tensor_reduce(allsame[:, :], eq[:, 2:GE + 1], AX_X, ALU.min))
            for h in range(H):
                v.tensor_scalar(ends[:, 2, h:h + 1], eq[:, 1:2], allsame[:, 0:1], None, ALU.mult)
                v.tensor_scalar(ends[:, 3, h:h + 1], eq[:, RW - 1:RW], allsame[:, 0:1], None, ALU.mult)

            def hot(q):
                c0, n = PIECES[q]
                v.wait_ge(s(f"keys_landed{q % 2}"), 48 * (q // 2 + 1))
                v.tensor_scalar(keys[:, q % 2, 0:2, 0:n * P], keys[:, q % 2, 0:2, 0:n * P], iota_p[:, 0:1], None, ALU.is_equal)
                v.tensor_scalar(keys[0:TY, q % 2, 2, 0:n * P], keys[0:TY, q % 2, 2, 0:n * P], iota_p[0:TY, 0:1], None,
                                ALU.is_equal).then_inc(s("hot"), 1)

            hot(0)
            for g, (q, c0, n) in enumerate(GROUPS):
                if g + 1 < len(GROUPS) and GROUPS[g + 1][0] != q:
                    hot(q + 1)
                v.wait_ge(s("pe_sel"), g + 1)
                pr = prod[:, 0:n * 2 * NT * H].rearrange("p (c s a h) -> p s c a h", c=n, s=2, a=NT)
                for side in range(2):
                    o = v.tensor_tensor(pr[:, side, :, :, :],
                                        ps[:, 2 * (g % 2) + side, 0:n * NT * H].rearrange("p (c a h) -> p c a h", c=n, a=NT),
                                        sel_hi[:, side, c0:c0 + n, :].unsqueeze(3).to_broadcast([P, n, NT, H]), ALU.mult)
                    o.then_inc(s("dve"), 1)
                    chain[0] += 1
                v.wait_ge(s("dve"), chain[0])
                v.nop().then_inc(s("sel_read"), 1)
                link(v.tensor_reduce(e_c[:, c0:c0 + n, :],
                                     prod[:, 0:n * 2 * NT * H].rearrange("p (c k h) -> p c h k", c=n, h=H), AX_X, ALU.add))
            ef = e_c[:, :, :].rearrange("p c h -> p (c h)")
            link(v.scalar_tensor_tensor(out=ef, in0=ef, scalar=0.2, in1=ef, op0=ALU.mult, op1=ALU.max))
            for b in range(3):
                c0, c1 = 64 * b, min(64 * b + 64, NC)
                o = v.tensor_tensor(e_c[:, c0:c1, :].rearrange("p c h -> p (c h)"),
                                    ps[:, 4 + b, 0:(c1 - c0) * H], e_c[:, c0:c1, :].rearrange("p c h -> p (c h)"), ALU.mult)
            link(o)
            v.tensor_tensor(e_c[:, :, :], e_c[:, :, :], ecol[:, 3, :].unsqueeze(2).to_broadcast([P, NC, H]),
                            ALU.mult).then_inc(s("e_done"), 1)
            v.wait_ge(s("act_h"), NT)
            v.memset(E1[:, :, 0:1], 0.0)
            v.memset(E1[:, :, RW - 1:RW], 0.0)
            v.memset(F1[:, :, 0:1], 0.0)
            v.memset(F1[:, :, RW - 1:RW], 0.0)
            v.memset(F2[:, :, 0:1], 0.0)
            v.memset(F2[:, :, RW - 1:RW], 0.0)
            v.tensor_copy(F1[:, :, 1:GE + 1], eq[:, 1:GE + 1].unsqueeze(1).to_broadcast([NG, H, GE]))
            link(v.tensor_copy(F2[:, :, 1:GE + 1], eq[:, 2:GE + 2].unsqueeze(1).to_broadcast([NG, H, GE])))
            v.nop().then_inc(s("dx_read"), 1)
            e1, e2, f1, f2 = (z.rearrange("p h k -> p (h k)") for z in (E1, E2, F1, F2))

            def segment_max():
                link(v.tensor_tensor_scan(e2, f1, e1, 0.0, ALU.mult, ALU.max))
                link(v.tensor_tensor_scan(e1[:, ::-1], f2[:, ::-1], e2[:, ::-1], 0.0, ALU.mult, ALU.max))

            v.wait_ge(s("act_er"), 16)
            segment_max()
            v.tensor_copy(ends[:, 0, :], E1[:, :, GE])
            v.tensor_copy(ends[:, 1, :], E1[:, :, 1]).then_inc(s("ends_done"), 1)
            v.wait_ge(s("pe_ends"), 1)
            link(v.tensor_copy(endsT[:, :, :].rearrange("h k g -> h (k g)"), ps[0:H, 4, 0:4 * NG]))
            v.memset(carry[:, 0, 0:1], 0.0)
            v.memset(carry[:, 1, NG:NG + 1], 0.0)
            v.tensor_tensor_scan(carry[:, 0, 1:NG + 1], endsT[:, 2, :], endsT[:, 0, :], 0.0, ALU.mult, ALU.max)
            v.tensor_tensor_scan(carry[:, 1, 0:NG][:, ::-1], endsT[:, 3, ::-1], endsT[:, 1, ::-1], 0.0, ALU.mult,
                                 ALU.max).then_inc(s("carry_done"), 1)
            v.wait_ge(s("pe_carry"), 1)
            v.tensor_copy(E1[:, :, 0], ps[0:NG, 5, 0:H])
            link(v.tensor_copy(E1[:, :, RW - 1], ps[0:NG, 5, H:2 * H]))
            segment_max()
            v.nop().then_inc(s("m_done"), 1)
            v.wait_ge(s("pe_m"), 1)
            for k in range(2 * H):
                h, q = k // 2, k % 2
                o = v.tensor_tensor(e_c[:, q::2, h], e_c[:, q::2, h], ps[:, k // 6, (k % 6) * NG:(k % 6 + 1) * NG], ALU.subtract)
            o.then_inc(s("dve_d"), 1)
            v.memset(acc[:, :, :], 0.0)
            v.memset(accs[:, :, :], 0.0)
            v.memset(ps[:, 3, :], 0.0)
            link(v.memset(ps[:, 7, 0:H], 0.0))
            v.wait_ge(s("p_done"), 1)
            for w in range(NX):
                g = v.value_load(grp[0:1, w:w + 1], min_val=0, max_val=NG - 1)
                o = v.tensor_copy(p_c[:, NC + 2 * w:NC + 2 * w + 2, :], p_c[:, bass.ds(2 * g, 2), :])
            link(o)
            v.nop().then_inc(s("px_done"), 1)

            def add_item(it, j, number):
                w = v.value_load(witem[0:1, it], min_val=0, max_val=NT - 1)
                a = acc[:, bass.ds(w, 1), :].rearrange("p a d -> p (a d)")
                b = accs[:, bass.ds(w, 1), :].rearrange("p a d -> p (a d)")
                v.tensor_tensor(b, ps[:, 4 + j % 4, 0:H], b, ALU.add)
                v.tensor_tensor(a, ps[:, j % 4, :], a, ALU.add).then_inc(s("acc_done"), 1)

            def body(i, first):
                for j in range(IB):
                    for u in range(2):
                        k = 2 * j + u
                        if not (first and j < 2):
                            v.wait_ge(s("pe_item"), IB * i + j - 1)
                        v.tensor_scalar(S[:, k % 4, :], iota_row[:, :],
                                        dloc[:, bass.ds(SLOTS * i + k, 1)], None, ALU.is_equal)
                        v.wait_ge(landed[k], 16 * i + 16)
                        n = (H - 2) * HD
                        v.tensor_tensor(ring[:, k, 0:n].rearrange("p (h d) -> p h d", d=HD),
                                        ring[:, k, 0:n].rearrange("p (h d) -> p h d", d=HD),
                                        p_c[:, bass.ds(SLOTS * i + k, 1), 0:H - 2].rearrange("p a h -> p (a h)")
                                        .unsqueeze(2).to_broadcast([P, H - 2, HD]), ALU.mult).then_inc(s("dve_msg"), 1)
                    if not (first and j == 0):
                        v.wait_ge(s("pe_item"), IB * i + j)
                        if not (first and j == 1):
                            v.wait_ge(s("acc_done"), IB * i + j - 1)
                        add_item(bass.ds(IB * i + j - 1, 1), j - 1, None)

            body(0, True)
            with v.Fori(1, ITER) as i:
                body(i, False)
            v.wait_ge(s("pe_item"), NI)
            v.wait_ge(s("acc_done"), NI - 1)
            add_item(slice(NI - 1, NI), IB - 1, None)
            v.wait_ge(s("acc_done"), NI)
            link(v.tensor_scalar(accs[:, :, :], accs[:, :, :], 1e-10, None, ALU.add))
            link(v.reciprocal(accs[:, :, :], accs[:, :, :]))
            half = NT // 2
            for k in range(2):
                hs_ = slice(k * half, (k + 1) * half)
                for t in range(k * half, (k + 1) * half):
                    o3 = acc[:, t, :].rearrange("p (h d) -> p h d", h=H)
                    link(v.tensor_tensor(o3, o3, accs[:, t, :].unsqueeze(2).to_broadcast([P, H, HD]), ALU.mult))
                    link(v.tensor_tensor(acc[:, t, :], acc[:, t, :], xn[:, t, :], ALU.add))
                    o = v.bn_stats(stats[:, t, :], acc[:, t, :])
                link(o)
                for t in range(k * half, (k + 1) * half):
                    o = v.bn_aggr(mv[:, t, :], stats[:, t, :])
                link(o)
                v.tensor_scalar(rstd[:, hs_], mv[:, hs_, 1], EPS, None, ALU.add).then_inc(s("gnn_var"), 1)
            for k in range(2):
                hs_ = slice(k * half, (k + 1) * half)
                v.wait_ge(s("gnn_std"), k + 1)
                link(v.reciprocal(rstd[:, hs_], rstd[:, hs_]))
                v.scalar_tensor_tensor(out=mean2[:, hs_], in0=mv[:, hs_, 0], scalar=-1.0, in1=rstd[:, hs_], op0=ALU.mult,
                                       op1=ALU.mult).then_inc(s("gnn_var"), 1)
            v.wait_ge(s("pe_param"), 1)
            v.tensor_copy(gT[:, :, :, :].rearrange("p k a e -> p (k a e)"), ps[:, 4, 0:2 * A * NEX])
            v.tensor_copy(bT[:, :, :, :].rearrange("p k m e -> p (k m e)"), ps[:, 5, 0:2 * M * NEX])
            v.tensor_copy(wgT[:, :, :].rearrange("p a e -> p (a e)"), ps[:, 5, A * NEX:2 * A * NEX]).then_inc(s("param_done"), 1)
            v.wait_ge(s("gnn_norm"), NT)
            for k in range(2):
                hs_ = slice(k * half, (k + 1) * half)
                for t in range(k * half, (k + 1) * half):
                    v.wait_ge(s("x1_done"), t + 1)
                    o = v.bn_stats(stats[:, t, :], x_sb[:, t, :])
                link(o)
                for t in range(k * half, (k + 1) * half):
                    o = v.bn_aggr(mv[:, t, :], stats[:, t, :])
                link(o)
                v.tensor_scalar(rstd[:, hs_], mv[:, hs_, 1], EPS, None, ALU.add).then_inc(s("x1_var"), 1)
                v.wait_ge(s("x1_std"), k + 1)
                link(v.reciprocal(rstd[:, hs_], rstd[:, hs_]))
                link(v.tensor_tensor(fac[:, hs_], rstd[:, hs_], rstd[:, hs_], ALU.mult))
                link(v.tensor_tensor(inv_r2[:, hs_], fac[:, hs_], mv[:, hs_, 1], ALU.mult))
                v.tensor_scalar(inv_r2[:, hs_], inv_r2[:, hs_], EPS, None, ALU.add).then_inc(s("r2_var"), 1)
                v.wait_ge(s("r2_std"), k + 1)
                link(v.reciprocal(fac[:, hs_], inv_r2[:, hs_]))
                link(v.tensor_tensor(fac[:, hs_], fac[:, hs_], rstd[:, hs_], ALU.mult))
                v.scalar_tensor_tensor(out=mean2[:, hs_], in0=mv[:, hs_, 0], scalar=-1.0, in1=fac[:, hs_], op0=ALU.mult,
                                       op1=ALU.mult).then_inc(s("nx_ready"), 1)
            for t in range(NT):
                v.wait_ge(s("pe_lg"), t + 1)
                v.scalar_tensor_tensor(out=lg[:, t, :], in0=ps[:, 2 + t % 2, 0:NEX], scalar=inv_r2[:, t:t + 1], in1=bg_b[:, :],
                                       op0=ALU.mult, op1=ALU.add).then_inc(s("lg_read"), 1)
                v.wait_ge(s("lg_read"), t + 1)
                link(v.max(top[:, t, :], lg[:, t, :]))
                o = v.max_index(topi[:, t, :], top[:, t, :], lg[:, t, :])
            link(o)
            v.tensor_copy(topf[:, :, :], top[:, :, 0:2]).then_inc(s("top_done"), 1)
            link(v.tensor_copy(eidx[:, :, :], topi[:, :, 0:2]))
            erow2 = iota_row[:, 0:NEX].unsqueeze(1).to_broadcast([P, 2 * NT, NEX])
            ohf, tmpf = (z[:, :, :, :].rearrange("p t k e -> p (t k) e") for z in (oh, tmp))
            link(v.tensor_tensor(ohf, erow2, eidx[:, :, :].rearrange("p t k -> p (t k)").unsqueeze(2).to_broadcast([P, 2 * NT, NEX]),
                                 ALU.is_equal))
            v.wait_ge(s("tri_done"), 3)
            link(v.tensor_scalar(oh[:, NT - 1, :, :], oh[:, NT - 1, :, :], real[:, 0:1], None, ALU.mult))
            v.memset(before[:, 0, :], 0.0)
            link(v.tensor_tensor(hits[:, :, :], oh[:, :, 0, :], oh[:, :, 1, :], ALU.add))
            for t in range(NT):
                link(v.tensor_tensor(before[:, t + 1, :], before[:, t, :], hits[:, t, :], ALU.add))
            v.nop().then_inc(s("before_done"), 1)
            v.wait_ge(s("pe_rank"), 1)
            v.tensor_tensor(tmp[:, 0:8, :, :], oh[:, 0:8, :, :],
                            ps[:, 6, :].rearrange("p (t e) -> p t e", t=8).unsqueeze(2).to_broadcast([P, 8, 2, NEX]), ALU.mult)
            v.tensor_copy(counts[:, :], ps[:, 7, 2 * NEX:3 * NEX])
            v.memset(nov[:, :], 0.0)
            v.memset(kk[:, :, :], 0.0)
            link(v.tensor_tensor(tmp[:, 8:NT, :, :], oh[:, 8:NT, :, :],
                                 ps[:, 7, 0:(NT - 8) * NEX].rearrange("p (t e) -> p t e", e=NEX).unsqueeze(2)
                                 .to_broadcast([P, NT - 8, 2, NEX]), ALU.mult))
            rf, kf, of, ef_ = (z[:, :, :].rearrange("p t k -> p (t k)") for z in (rnk, kk, obs, eidx))
            link(v.tensor_reduce(rf, tmpf, AX_X, ALU.add))
            for k in range(1, KMAX + 1):
                v.scalar_tensor_tensor(out=nov[:, :], in0=counts[:, :], scalar=float(TS * k), in1=nov[:, :], op0=ALU.is_gt,
                                       op1=ALU.add)
                link(v.scalar_tensor_tensor(out=kf, in0=rf, scalar=float(TS * k), in1=kf, op0=ALU.is_ge, op1=ALU.add))
            link(v.tensor_tensor_scan(inc[:, :], ones[:, 0:NEX], nov[:, :], 0.0, ALU.mult, ALU.add))
            link(v.tensor_tensor(exc[:, :], inc[:, :], nov[:, :], ALU.subtract))
            link(v.tensor_tensor(tmpf, ohf, exc[:, :].unsqueeze(1).to_broadcast([P, 2 * NT, NEX]), ALU.mult))
            link(v.tensor_reduce(of, tmpf, AX_X, ALU.add))
            link(v.scalar_tensor_tensor(out=of, in0=of, scalar=float(NEX - 1), in1=kf, op0=ALU.add, op1=ALU.add))
            link(v.tensor_tensor(of, of, ef_, ALU.subtract))
            link(v.scalar_tensor_tensor(out=of, in0=kf, scalar=1.0, in1=of, op0=ALU.min, op1=ALU.mult))
            link(v.tensor_tensor(of, of, ef_, ALU.add))
            link(v.scalar_tensor_tensor(out=rf, in0=kf, scalar=-float(TS), in1=rf, op0=ALU.mult, op1=ALU.add))
            link(v.scalar_tensor_tensor(out=of, in0=rf, scalar=float(NTILE), in1=of, op0=ALU.mult, op1=ALU.add))
            v.tensor_copy(slot_idx[:, :, :].rearrange("p t k -> p (t k)"), of).then_inc(s("pos_done"), 1)
            for j0 in range(0, NOV, 16):
                n = min(16, NOV - j0)
                c3 = tmpf[0:1, 0:n, :]
                link(v.tensor_tensor(c3, inc[0:1, :].unsqueeze(1).to_broadcast([1, n, NEX]),
                                     iota_row[0:1, j0:j0 + n].unsqueeze(2).to_broadcast([1, n, NEX]), ALU.is_le))
                link(v.tensor_reduce(counts[0:1, j0:j0 + n], c3, AX_X, ALU.add))
            v.tensor_copy(over_i[:, :], counts[0:1, 0:NOV])
            v.tensor_copy(nover_i[:, :], inc[0:1, NEX - 1:NEX]).then_inc(s("over_done"), 1)
            v.wait_ge(s("exp_top"), 1)
            link(v.tensor_scalar(wk[:, :, :], wk[:, :, :], 1.0, None, ALU.add))
            link(v.reciprocal(wk[:, :, :], wk[:, :, :]))
            link(v.tensor_tensor(wsum[:, :], wk[:, :, 0], wk[:, :, 1], ALU.add))
            link(v.reciprocal(wsum[:, :], wsum[:, :]))
            link(v.tensor_tensor(wk[:, :, :], wk[:, :, :], wsum[:, :].unsqueeze(2).to_broadcast([P, NT, 2]), ALU.mult))
            link(v.tensor_tensor(tmpf, ohf, wk[:, :, :].rearrange("p t k -> p (t k)").unsqueeze(2)
                                 .to_broadcast([P, 2 * NT, NEX]), ALU.mult))
            v.tensor_tensor(cw[:, :, :], tmp[:, :, 0, :], tmp[:, :, 1, :], ALU.add).then_inc(s("cw_done"), 1)
            for n in range(-(-NPAD // 512)):
                c0, c1 = 512 * n, min(512 * n + 512, NPAD)
                for m in range(M):
                    k = M * n + m
                    v.wait_ge(s("pe_sh3"), k + 1)
                    v.wait_ge(s("act_sh"), k + 1)
                    v.scalar_tensor_tensor(out=hsT[:, m, c0:c1], in0=ps[:, 2 * (k % 2) + 1, 0:c1 - c0], scalar=sbias[:, 1, m:m + 1],
                                           in1=sil[:, 0:c1 - c0], op0=ALU.add, op1=ALU.mult).then_inc(s("hs_done"), 1)
            v.wait_ge(s("pe_cwT"), 1)
            v.wait_ge(s("cw_done"), 1)
            v.memset(cwT[NEX:NEX + 1, :], 1.0)
            for b in range(3):
                c0, c1 = 512 * b, min(512 * b + 512, NPAD)
                o = v.tensor_copy(cwT[0:NEX, c0:c1], ps[0:NEX, 4 + b, 0:c1 - c0])
            o.then_inc(s("cwT_done"), 1)
            for t in range(NT):
                v.wait_ge(s("pe_z"), t + 1)
                v.tensor_tensor(x_sb[:, t, :], ps[:, 4 + t % 2, :], x_sb[:, t, :], ALU.add).then_inc(s("z_added"), 1)

            def scale_in(u, e, bank, k, done):
                for a in range(A):
                    o = v.tensor_scalar(xgT[:, k, a, :], ps[:, bank, a * TS:(a + 1) * TS], gT[:, 0, a, e], gT[:, 1, a, e],
                                        ALU.mult, ALU.add)
                o.then_inc(s(done), 1)

            def hidden(e, bank, k, done):
                for m in range(M):
                    o = v.scalar_tensor_tensor(out=hT[:, k, m, :], in0=ps[:, bank, m * TS:(m + 1) * TS], scalar=bT[:, 1, m, e],
                                               in1=s1[:, k, m, :], op0=ALU.add, op1=ALU.mult)
                o.then_inc(s(done), 1)

            def experts(i, lo, last):
                for u in range(U):
                    e = U * i + u
                    if not (last and u == U - 1):
                        v.wait_ge(s("pe_xgT"), e + 2)
                        if U * lo + u >= 1:
                            v.wait_ge(s("pe_h3"), e)
                        scale_in(u, bass.ds(e + 1, 1), (u + 1) % 2, (u + 1) % 2, "xgT_done")
                    v.wait_ge(s("pe_h3"), e + 1)
                    v.wait_ge(s("act_s1"), e + 1)
                    if U * lo + u >= 2:
                        v.wait_ge(s("pe_y"), e - 1)
                    hidden(bass.ds(e, 1), 4 + u % 2, u % 2, "hT_done")

            v.wait_ge(s("pe_xgT"), 1)
            scale_in(0, slice(0, 1), 0, 0, "xgT_done")
            experts(0, 0, False)
            with v.Fori(1, NIT - 1) as i:
                experts(i, 1, False)
            experts(NIT - 1, NIT - 1, True)
            n = v.value_load(nover_i[0:1, 0:1], min_val=0, max_val=NOV)
            with v.If(n > 0):
                v.nop().then_inc(s("ov_end"), 1)
                with v.Fori(0, n) as j:
                    v.wait_ge(s("ov_step"), 7 * j + 1)
                    e = v.value_load(over_i[0:1, bass.ds(j, 1)], min_val=0, max_val=NEX - 1)
                    scale_in(0, bass.ds(e, 1), 0, 0, "ov_step")
                    v.wait_ge(s("ov_step"), 7 * j + 4)
                    hidden(bass.ds(e, 1), 4, 0, "ov_step")
            for t in range(NT):
                v.wait_ge(s(f"y_in{t % 4}"), 16 * (t // 4 + 1))
                rows = P if t < NT - 1 else LAST
                for k in range(2):
                    o = v.scalar_tensor_tensor(out=x_sb[0:rows, t, :], in0=yin[0:rows, t % 4, k, :], scalar=wk[0:rows, t, k:k + 1],
                                               in1=x_sb[0:rows, t, :], op0=ALU.mult, op1=ALU.add)
                    if k == 0:
                        link(o)
                o.then_inc(s("out_ready"), 1)


_INS = ['x', 'src', 'dst', 'edge_type_8', 'edge_weight', 'L0_gnn_W', 'L0_gnn_a_src', 'L0_gnn_a_dst', 'L0_gnn_et_emb',
        'L0_gnn_ln_gamma', 'L0_gnn_ln_beta', 'L0_ffn_Wg', 'L0_ffn_bg', 'L0_ffn_gamma', 'L0_ffn_beta', 'L0_ffn_W1',
        'L0_ffn_b1', 'L0_ffn_W3', 'L0_ffn_b3', 'L0_ffn_W2', 'L0_ffn_b2', 'L0_ffn_gs', 'L0_ffn_bs', 'L0_ffn_Ws1',
        'L0_ffn_bs1', 'L0_ffn_Ws3', 'L0_ffn_bs3', 'L0_ffn_Ws2', 'L0_ffn_bs2']


def kernel(**inputs):
    import numpy as _np
    import concourse.bacc as _bacc
    from concourse import mybir as _mybir
    from concourse.bass_utils import run_bass_kernel_spmd as _run

    nc = _bacc.Bacc("TRN2", target_bir_lowering=False, num_devices=1)
    arrays, args = {}, []
    for name in _INS:
        a = _np.ascontiguousarray(inputs[name])
        arrays[f"in_{name}_dram"] = a
        args.append(nc.dram_tensor(f"in_{name}_dram", a.shape, _mybir.dt.from_np(a.dtype), kind="ExternalInput").ap())
    out = nc.dram_tensor("out_0_dram", (1250, 512), _mybir.dt.float32, kind="ExternalOutput").ap()
    gnn_moe_kernel(nc, *args, out)
    r = _run(nc, [arrays], core_ids=[0])
    return r.results[0]["out_0_dram"]
```

```python
from contextlib import ExitStack

import concourse.bass as bass
from concourse import mybir

F32 = mybir.dt.float32
BF16 = mybir.dt.bfloat16
I32 = mybir.dt.int32
U32 = mybir.dt.uint32
ALU = mybir.AluOpType
ACT = mybir.ActivationFunctionType
AX_X = mybir.AxisListType.X

P = 128
EPS = 1e-5
TOKENS = 80


def gnn_moe_kernel(nc, x, src, dst, etype, eweight, W, a_src, a_dst, et_emb, ln_gamma, ln_beta,
                   Wg, bg, gamma, beta, W1, b1, W3, b3, W2, b2, gs, bs, Ws1, bs1, Ws3, bs3, Ws2, bs2, out):
    N, D = x.shape
    NE = src.shape[0]
    H, HD = a_src.shape
    TY = et_emb.shape[0]
    NT = -(-N // P)
    NPAD = NT * P
    LAST = N - (NT - 1) * P
    A = D // P
    GE = 2 * P
    NG = -(-NE // GE)
    NC = 2 * NG
    NX = NT - 1
    NI = NG + NX
    NCX = 2 * NI
    EPAD = NC * P
    PADNODE = NPAD - 1
    IB = 8
    SLOTS = 2 * IB
    ITER = NI // IB
    assert NI % IB == 0
    RW = GE + 2
    FULLC = NE // P
    REST = NE - FULLC * P

    NEX, _, HF = W1.shape
    M = HF // P
    TS = TOKENS
    NOV = (2 * N) // TS
    NTILE = NEX + NOV
    LNG = [(0, 3), (3, 6), (6, 8), (8, NT)]
    ROUND = 1.5 * 2 ** 23
    NSH = -(-NPAD // 512)
    U = 4
    NIT = NEX // U
    SKIP = 1 << 20
    assert NT + 1 < NIT - 1

    nx_d = nc.dram_tensor("nx_rows", [NPAD, D], F32).ap()
    y_d = nc.dram_tensor("y_rows", [2 * NPAD, D], F32).ap()
    h_d = nc.dram_tensor("h_rows", [NPAD, D], F32).ap()
    bkey_d = nc.dram_tensor("edge_keys", [3, EPAD], BF16).ap()

    with ExitStack() as ctx:
        ctx.enter_context(nc.allow_non_contiguous_dma(reason="a few hundred single elements of small inputs"))
        def sb(name, shape, dt=F32):
            return ctx.enter_context(nc.sbuf_tensor(name, shape, dt))

        def sem(name):
            return ctx.enter_context(nc.semaphore(name))

        arena = sb("arena", [P, 17500])

        class Carver:
            def __init__(self, buf, size):
                self.buf, self.size, self.at = buf, size, 0

            def __call__(self, shape, dt=F32):
                n = 1
                for d in shape[1:]:
                    n *= d
                words = (n * (2 if dt == BF16 else 4) + 3) // 4
                a = self.buf[0:shape[0], self.at:self.at + words]
                self.at += words
                assert self.at <= self.size, (self.at, self.size)
                if dt != F32:
                    a = a.bitcast(dt)[:, 0:n]
                if len(shape) > 2:
                    names = " ".join(f"d{k}" for k in range(1, len(shape)))
                    a = a.rearrange(f"p ({names}) -> p {names}", **{f"d{k}": shape[k] for k in range(1, len(shape))})
                return a

        first = Carver(arena, 17500)
        ps = ctx.enter_context(nc.psum_tensor("ps", [P, 8, 512], F32))

        ident = sb("ident", [P, P])
        ones = sb("ones", [P, P])
        iota_row = sb("iota_row", [P, P])
        spare = sb("spare", [P, 16])
        iota_p = sb("iota_p", [P, 1])
        x_sb = sb("x_sb", [P, NT, D])
        xn = sb("xn", [P, NT, D])
        xT = sb("xT", [P, A, NPAD])
        acc = sb("acc", [P, NT, D])
        accs = sb("accs", [P, NT, H])
        stats = sb("stats", [P, NT, 6])
        mv = sb("mv", [P, NT, 2])
        rstd = sb("rstd", [P, NT])
        ring = sb("ring", [P, SLOTS, D])
        W_sb = first([P, A, D])
        WT = first([P, A, D])
        attn = first([P, 2, A])
        ablk = first([P, A * 2 * H])
        V = first([P, A, 2 * H])
        tab = first([P, 2, NT * H])
        tabr = first([P, 2 * NT * H])
        tab3 = first([P, 3, 2, NT * H], BF16)
        emb = first([TY, H])
        embr = first([TY, H])
        emb3 = first([TY, 3, H], BF16)
        erow = first([P, 2, 4, P], I32)
        erowf = first([P, 2, 4, P])
        ecol = sb("ecol", [P, 4, NC])
        hi = first([P, 2, NC], I32)
        hif = first([P, 2, NC])
        sel_hi = first([P, 2, NC, NT])
        srcx = sb("srcx", [P, NCX], U32)
        dloc = sb("dloc", [P, NCX])
        e_c = sb("e_c", [P, NC, H])
        p_c = sb("p_c", [P, NCX, H])
        PIECE = 10
        keys = first([P, 2, 3, PIECE * P], BF16)
        prod = first([P, 5 * 2 * NT * H])
        S = sb("S", [P, 4, P])
        idx_stage = sb("idx_stage", [P, 2, IB], U32)
        low = first([1, NG], I32)
        lowf = first([1, NG])
        cnt = sb("cnt", [P, NX])
        cmp = first([P, NC])
        start_i = sb("start_i", [P, NX], I32)
        grp = sb("grp", [P, NX], I32)
        rem = sb("rem", [P, NX], I32)
        shift = sb("shift", [P, NX])
        witem = sb("witem", [1, NI], I32)
        kint = first([P, 3, 160], I32)
        kb = first([P, 3, 160], BF16)
        kpad = first([3, EPAD - NE], BF16)
        E1 = acc[0:NG, :, :].rearrange("p t d -> p (t d)")[:, 0:H * RW].rearrange("p (h k) -> p h k", h=H)
        E2 = acc[0:NG, :, :].rearrange("p t d -> p (t d)")[:, H * RW:2 * H * RW].rearrange("p (h k) -> p h k", h=H)
        F1 = xT[0:NG, :, :].rearrange("p t d -> p (t d)")[:, 0:H * RW].rearrange("p (h k) -> p h k", h=H)
        F2 = xT[0:NG, :, :].rearrange("p t d -> p (t d)")[:, H * RW:2 * H * RW].rearrange("p (h k) -> p h k", h=H)
        dx_i = first([NG, RW], I32)
        dx = first([NG, RW])
        eq = first([NG, RW])
        ends = sb("ends", [NG, 4, H])
        allsame = sb("allsame", [NG, 1])
        endsT = sb("endsT", [H, 4, NG])
        carry = sb("carry", [H, 2, NG + 1])
        router = Carver(acc[:, :, :].rearrange("p t d -> p (t d)"), NT * D)
        top = sb("top", [P, NT, 8])
        topi = sb("topi", [P, NT, 8], U32)
        wk = sb("wk", [P, NT, 2])
        wsum = sb("wsum", [P, NT])
        mean2 = sb("mean2", [P, NT])
        inv_r2 = sb("inv_r2", [P, NT])
        fac = sb("fac", [P, NT])
        slot_tab = sb("slot_tab", [TS, NTILE, 2], I32)
        payload = sb("payload", [P, NT, 2])
        vw = sb("vw", [P, 2, NT])
        rv = sb("rv", [P, 2, NT])
        far = sb("far", [P, 1])
        stage_g = sb("stage_g", [TS, U], U32)
        stage_s = sb("stage_s", [TS, U], U32)
        nover_i = sb("nover_i", [1, 1], I32)
        over_i = sb("over_i", [1, NOV], I32)
        later = Carver(arena, 17500)
        w13 = later([P, U, 2, A, HF])
        w2s = later([P, U, M, D])
        gam = later([NEX, D])
        bet = later([NEX, D])
        bb1 = later([NEX, 2, HF])
        wg = later([NEX, D])
        gT = later([P, 2, A, NEX])
        bT = later([P, 2, M, NEX])
        wgT = later([P, A, NEX])
        bg_b = later([P, NEX])
        shared = Carver(ring[:, :, :].rearrange("p k d -> p (k d)"), SLOTS * D)
        ws13 = shared([P, 2, A, HF])
        ws2 = shared([P, M, D])
        nxs = shared([P, A, 512])
        hsT = shared([P, M, NPAD])
        sil = shared([P, 512])
        zc = nxs[0:NEX + 1, 1, 0:P]
        yin = Carver(ring[:, :, :].rearrange("p k d -> p (k d)"), SLOTS * D)([P, 4, 2, D])
        lnp = later([P, 2, D])
        sg = later([P, 2, A])
        sbias = later([P, 2, M])
        b2a = later([NEX + 1, D])
        toks = Carver(xn[:, :, :].rearrange("p t d -> p (t d)"), NT * D)
        xg = toks([TS, U, D])
        yo = toks([TS, U, D])
        xgT = toks([P, 2, A, TS])
        onehots = Carver(xn[:, :, :].rearrange("p t d -> p (t d)"), NT * D)
        rank1h = onehots([P, 2 * NT, TS])
        tile1h = onehots([P, 2 * NT, NTILE])
        lg = router([P, NT, NEX])
        oh = router([P, NT, 2, NEX])
        tmp = router([P, NT, 2, NEX])
        hits = router([P, NT, NEX])
        before = router([P, NT + 1, NEX])
        eidx = sb("eidx", [P, NT, 2])
        gates = Carver(hits[:, :, :].rearrange("p t e -> p (t e)"), NT * NEX)
        s1 = gates([P, 2, M, TS])
        hT = gates([P, 2, M, TS])
        topf = sb("topf", [P, NT, 2])
        rnk = sb("rnk", [P, NT, 2])
        tens = sb("tens", [P, 2 * NT + NEX])
        slotf = sb("slotf", [TS, NTILE])
        obs = sb("obs", [P, NT, 2])
        real = sb("real", [P, 1])
        counts = sb("counts", [P, NEX])
        inc = sb("inc", [P, NEX])
        exc = sb("exc", [P, NEX])
        tri = sb("tri", [P, P])
        cw = lg
        cwT = tmp[0:NEX + 1, :, :, :].rearrange("p t k e -> p (t k e)")

        names = {}

        def s(name):
            if name not in names:
                names[name] = sem(name)
            return names[name]

        w_landed = [sem(f"w_landed{k}") for k in range(U)]
        xg_landed = [sem(f"xg_landed{k}") for k in range(U)]
        y_out = [sem(f"y_out{k}") for k in range(U)]
        landed = [sem(f"row_landed{k}") for k in range(SLOTS)]

        block = ctx.enter_context(nc.Block())

        ek = bkey_d
        x_main = x[0:(NT - 1) * P].rearrange("(t p) d -> p t d", p=P)
        PIECES = [(q * PIECE, min(PIECE, NC - q * PIECE)) for q in range(-(-NC // PIECE))]
        GROUPS = []
        for q, (c0, n) in enumerate(PIECES):
            for c in range(c0, c0 + n, 5):
                GROUPS.append((q, c, min(5, c0 + n - c)))
        KP = NE // 160

        @block.sync
        def _(sp):
            sp.wait_ge(s("erow_pad"), 1)
            for k, a in enumerate((src, dst, etype, eweight.bitcast(I32))):
                sp.dma_start(erow[:, 0, k, :], a[0:P * P].rearrange("(c e) -> c e", e=P)).then_inc(s("erow_in"), 16)
                sp.dma_start(erow[0:FULLC - P, 1, k, :],
                             a[P * P:FULLC * P].rearrange("(c e) -> c e", e=P)).then_inc(s("erow_in"), 16)
                sp.dma_start(erow[FULLC - P:FULLC - P + 1, 1, k, 0:REST],
                             a[FULLC * P:NE].rearrange("(a e) -> a e", a=1)).then_inc(s("erow_in"), 16)
            for k, a in enumerate((src, dst, etype)):
                sp.dma_start(kint[0:KP, k, :], a.rearrange("(p j) -> p j", j=160)).then_inc(s("key_in"), 16)
            sp.wait_ge(s("x_pad"), 1)
            for t in range(0, NT - 1, 3):
                sp.dma_start(x_sb[:, t:t + 3, :], x_main[:, t:t + 3, :]).then_inc(s("x_in"), 16)
            sp.dma_start(x_sb[0:LAST, NT - 1, :], x[(NT - 1) * P:N, :]).then_inc(s("x_in"), 16)
            sp.wait_ge(s("key_ready"), 3)
            for k in range(3):
                sp.dma_start(ek[k, 0:NE].rearrange("(p j) -> p j", j=160), kb[0:KP, k, :]).then_inc(s("key_out"), 16)
            sp.dma_start(ek[:, NE:EPAD], kpad[:, :]).then_inc(s("key_out"), 16)
            sp.wait_ge(s("key_out"), 64)
            for q, (c0, n) in enumerate(PIECES):
                if q >= 2:
                    sp.wait_ge(s("pe_sel"), sum(1 for g in GROUPS if g[0] <= q - 2))
                for k in range(3):
                    rows = P if k < 2 else TY
                    sp.dma_start(keys[0:rows, q % 2, k, 0:n * P],
                                 bass.AP(tensor=ek.tensor, offset=k * EPAD + c0 * P, ap=[[0, rows], [1, n * P]])
                                 ).then_inc(s(f"keys_landed{q % 2}"), 16)
            for t in range(NT):
                sp.wait_ge(s("act_h"), t + 1)
                sp.dma_start(h_d[t * P:(t + 1) * P, :], ring[:, t, :]).then_inc(s("h_out"), 16)
            sp.wait_ge(s("e_done"), 1)
            sp.wait_ge(s("dx_read"), 1)
            for o, i in ((gam[:, :], gamma[:, :]), (bet[:, :], beta[:, :]), (bb1[:, 0, :], b1[:, :]),
                         (bb1[:, 1, :], b3[:, :]), (wg[:, :], Wg[:, :]), (b2a[0:NEX, :], b2[:, :]),
                         (b2a[NEX:NEX + 1, :], bs2.rearrange("(a d) -> a d", a=1)),
                         (bg_b[:, :], bass.AP(tensor=bg.tensor, offset=0, ap=[[0, P], [1, NEX]])),
                         (lnp[:, 0, :], bass.AP(tensor=ln_gamma.tensor, offset=0, ap=[[0, P], [1, D]])),
                         (lnp[:, 1, :], bass.AP(tensor=ln_beta.tensor, offset=0, ap=[[0, P], [1, D]])),
                         (sg[:, 0, :], gs.rearrange("(p a) -> p a", a=A)), (sg[:, 1, :], bs.rearrange("(p a) -> p a", a=A)),
                         (sbias[:, 0, :], bs1.rearrange("(m p) -> p m", p=P)),
                         (sbias[:, 1, :], bs3.rearrange("(m p) -> p m", p=P))):
                sp.dma_start(o, i).then_inc(s("param_in"), 16)

            def load_expert(u, e):
                sp.dma_start(w13[:, u, 0, :, :].rearrange("p a h -> p (a h)"),
                             W1[e, :, :].rearrange("o (p a) h -> p (o a h)", a=A)).then_inc(w_landed[u], 16)
                sp.dma_start(w13[:, u, 1, :, :].rearrange("p a h -> p (a h)"),
                             W3[e, :, :].rearrange("o (p a) h -> p (o a h)", a=A)).then_inc(w_landed[u], 16)
                sp.dma_start(w2s[:, u, :, :], W2[e, :, :].rearrange("o (m p) d -> p (o m) d", p=P)).then_inc(w_landed[u], 16)

            for u in range(U):
                load_expert(u, bass.ds(u, 1))
            sp.wait_ge(s("p_done"), 1)
            for w in range(NX):
                g = sp.value_load(grp[0:1, w:w + 1], min_val=0, max_val=NG - 1)
                sp.dma_start(p_c[:, NC + 2 * w:NC + 2 * w + 2, :], p_c[:, bass.ds(2 * g, 2), :]).then_inc(s("px_in"), 16)
            sp.wait_ge(s("pe_item"), NI)
            for k, w in enumerate((Ws1, Ws3)):
                sp.dma_start(ws13[:, k, :, :].rearrange("p a h -> p (a h)"),
                             w.rearrange("(p a) h -> p (a h)", a=A)).then_inc(s("sh_in"), 16)
            sp.dma_start(ws2[:, :, :], Ws2.rearrange("(m p) d -> p m d", p=P)).then_inc(s("sh_in"), 16)
            for t in range(NT):
                sp.wait_ge(s("nx_done"), t + 1)
                sp.dma_start(nx_d[t * P:(t + 1) * P, :], xn[:, t, :]).then_inc(s("nx_out"), 16)
            with sp.Fori(1, NIT) as i:
                for u in range(U):
                    sp.wait_ge(s("pe_y"), U * (i - 1) + u + 1)
                    load_expert(u, bass.ds(U * i + u, 1))
            sp.wait_ge(s("over_done"), 1)
            sp.wait_ge(s("pe_y"), NEX)
            n = sp.value_load(nover_i[0:1, 0:1], min_val=0, max_val=NOV)
            with sp.If(n > 0):
                with sp.Fori(0, n) as j:
                    sp.wait_ge(s("ov_end"), j + 1)
                    e = sp.value_load(over_i[0:1, bass.ds(j, 1)], min_val=0, max_val=NEX - 1)
                    sp.dma_start(w13[:, 0, 0, :, :].rearrange("p a h -> p (a h)"),
                                 W1[bass.ds(e, 1), :, :].rearrange("o (p a) h -> p (o a h)", a=A)).then_inc(s("ov_w"), 16)
                    sp.dma_start(w13[:, 0, 1, :, :].rearrange("p a h -> p (a h)"),
                                 W3[bass.ds(e, 1), :, :].rearrange("o (p a) h -> p (o a h)", a=A)).then_inc(s("ov_w"), 16)
                    sp.dma_start(w2s[:, 0, :, :], W2[bass.ds(e, 1), :, :].rearrange("o (m p) d -> p (o m) d", p=P)
                                 ).then_inc(s("ov_w"), 16)
            sp.wait_ge(s("y_all"), 1)
            sp.wait_ge(s("z_added"), NT)
            yv = y_d.rearrange("(t p k) d -> t p (k d)", p=P, k=2)
            for t in range(NT):
                if t >= 4:
                    sp.wait_ge(s("out_ready"), t - 3)
                rows = P if t < NT - 1 else LAST
                sp.dma_start(yin[0:rows, t % 4, :, :].rearrange("p k d -> p (k d)"), yv[t, 0:rows, :]).then_inc(s(f"y_in{t % 4}"), 16)

        @block.gpsimd
        def _(pool):
            pool.memset(erow[0:32, 1, 0:2, :], PADNODE)
            pool.memset(erow[0:32, 1, 2:4, :], 0).then_inc(s("erow_pad"), 1)
            pool.memset(dx_i[:, :], PADNODE).then_inc(s("dx_pad"), 1)
            pool.memset(ident[:, :], 0.0).then_inc(s("poolc"), 1)
            pool.wait_ge(s("poolc"), 1)
            pool.affine_select(out=ident[:, :], in_=ident[:, :], compare_op=ALU.not_equal, fill=1.0, base=0,
                               pattern=[[-1, P]], channel_multiplier=1)
            pool.memset(ones[:, :], 1.0)
            pool.iota(iota_p[:, :], pattern=[[0, 1]], base=0, channel_multiplier=1,
                      allow_small_or_imprecise_dtypes=True)
            pool.iota(iota_row[:, :], pattern=[[1, P]], base=0, channel_multiplier=0,
                      allow_small_or_imprecise_dtypes=True).then_inc(s("const"), 1)
            pool.memset(tri[:, :], 1.0)
            pool.memset(real[:, :], 1.0).then_inc(s("tri_done"), 1)
            pool.memset(far[:, :], 0.0).then_inc(s("tri_done"), 1)
            pool.wait_ge(s("tri_done"), 2)
            pool.affine_select(out=tri[:, :], in_=tri[:, :], compare_op=ALU.is_gt, fill=0.0, base=0,
                               pattern=[[1, P]], channel_multiplier=-1).then_inc(s("tri_done"), 1)
            pool.affine_select(out=real[:, :], in_=real[:, :], compare_op=ALU.is_gt, fill=0.0, base=LAST,
                               pattern=[[0, 1]], channel_multiplier=-1).then_inc(s("tri_done"), 1)
            pool.affine_select(out=far[:, :], in_=far[:, :], compare_op=ALU.is_gt, fill=1.0e6, base=LAST,
                               pattern=[[0, 1]], channel_multiplier=-1).then_inc(s("tri_done"), 1)
            pool.iota(payload[:, :, :], pattern=[[2 * P, NT], [1, 2]], base=1, channel_multiplier=2,
                      allow_small_or_imprecise_dtypes=True).then_inc(s("tri_done"), 1)
            pool.wait_ge(s("srcx_done"), 1)
            pool.wait_ge(s("h_out"), 16 * NT)

            def settle(k):
                pool.tensor_tensor(spare[:, k:k + 1], iota_p[:, :], iota_p[:, :], ALU.add)

            def body(i, first):
                for half in range(2):
                    if not first:
                        for k in range(half * IB, (half + 1) * IB):
                            pool.wait_ge(landed[k], 16 * i)
                    if not first:
                        settle(12 + half)
                    pool.tensor_copy(idx_stage[:, half, :], srcx[:, bass.ds(SLOTS * i + IB * half, IB)]
                                     ).then_inc(s("stage"), 1)
                    pool.wait_ge(s("stage"), 2 * i + half + 1)
                    settle(14 + half)
                    for k in range(IB):
                        slot = half * IB + k
                        if not first and k % 4 == 0:
                            pool.wait_ge(s("pe_item"), IB * (i - 1) + slot // 2 + 2)
                            settle(slot // 4)
                        pool.indirect_dma_start(
                            out=ring[:, slot, :], out_offset=None, in_=h_d[:, :],
                            in_offset=bass.IndirectOffsetOnAxis(ap=idx_stage[:, half, k:k + 1], axis=0)
                        ).then_inc(landed[slot], 16)

            body(0, True)
            pool.wait_ge(s("pe_m"), 1)
            pool.memset(acc[:, :, :], 0.0).then_inc(s("acc_zero"), 1)
            with pool.Fori(1, ITER) as i:
                body(i, False)
            pool.wait_ge(s("param_in"), 16 * 14)
            for t in range(NT):
                o = pool.tensor_tensor(x_sb[:, t, :], x_sb[:, t, :], lnp[:, 1, :], ALU.add)
            o.then_inc(s("xb_done"), 1)

            def divide(g):
                for t in range(*LNG[g]):
                    o3 = acc[:, t, :].rearrange("p (h d) -> p h d", h=H)
                    pool.tensor_tensor(o3, o3, accs[:, t, :].unsqueeze(2).to_broadcast([P, H, HD]), ALU.mult
                                       ).then_inc(s("divided"), 1)

            def times_gamma(g):
                for t in range(*LNG[g]):
                    pool.wait_ge(s("gnn_norm"), t + 1)
                    pool.tensor_tensor(acc[:, t, :], acc[:, t, :], lnp[:, 0, :], ALU.mult).then_inc(s("gnn_gam"), 1)

            pool.wait_ge(s("accs_done"), 1)
            divide(1)
            for g in range(len(LNG)):
                times_gamma(g)
                if g + 2 < len(LNG):
                    divide(g + 2)
            pool.wait_ge(s("slots_done"), 1)
            pool.wait_ge(s("nx_out"), 16 * NT)

            def gather(u, sems):
                pool.indirect_dma_start(out=xg[:, u, :], out_offset=None, in_=nx_d[:, :],
                                        in_offset=bass.IndirectOffsetOnAxis(ap=stage_g[:, u:u + 1], axis=0),
                                        bounds_check=NPAD - 1, oob_is_err=False).then_inc(sems, 16)

            def scatter(u, y, sems):
                pool.indirect_dma_start(out=y_d[:, :], out_offset=bass.IndirectOffsetOnAxis(ap=stage_s[:, u:u + 1], axis=0),
                                        in_=yo[:, y, :], in_offset=None, bounds_check=2 * NPAD - 1,
                                        oob_is_err=False).then_inc(sems, 16)

            pool.tensor_copy(stage_g[:, :], slot_tab[:, 0:U, 0]).then_inc(s("stage_g"), 1)
            pool.wait_ge(s("stage_g"), 1)
            for u in range(U):
                gather(u, xg_landed[u])

            def experts(i, first, last):
                if not first:
                    for u in range(U):
                        pool.wait_ge(y_out[u], 16 * i)
                if not last:
                    for u in range(U):
                        pool.wait_ge(xg_landed[u], 16 * i + 16)
                    pool.tensor_tensor(spare[:, 0:1], iota_p[:, :], iota_p[:, :], ALU.add)
                    pool.tensor_copy(stage_g[:, :], slot_tab[:, bass.ds(U * i + U, U), 0])
                elif not first:
                    pool.tensor_tensor(spare[:, 0:1], iota_p[:, :], iota_p[:, :], ALU.add)
                pool.tensor_copy(stage_s[:, :], slot_tab[:, bass.ds(U * i, U), 1]).then_inc(s("stage_s"), 1)
                pool.wait_ge(s("stage_s"), i + 1)
                settle(1)
                for u in range(U):
                    if not last:
                        pool.wait_ge(s("pe_xgT"), U * i + u + 1)
                        settle(2 + 2 * u)
                        gather(u, xg_landed[u])
                    pool.wait_ge(s("y_ready"), U * i + u + 1)
                    settle(3 + 2 * u)
                    scatter(u, u, y_out[u])

            experts(0, True, False)
            with pool.Fori(1, NIT - 1) as i:
                experts(i, False, False)
            experts(NIT - 1, False, True)
            for u in range(U):
                pool.wait_ge(y_out[u], 16 * NIT)
            n = pool.value_load(nover_i[0:1, 0:1], min_val=0, max_val=NOV)
            with pool.If(n > 0):
                with pool.Fori(0, n) as j:
                    pool.wait_ge(s("ov_end"), j + 1)
                    settle(10)
                    pool.tensor_copy(stage_g[:, 0:1], slot_tab[:, bass.ds(NEX + j, 1), 0])
                    pool.tensor_copy(stage_s[:, 0:1], slot_tab[:, bass.ds(NEX + j, 1), 1]).then_inc(s("ov_stage"), 1)
                    pool.wait_ge(s("ov_stage"), j + 1)
                    settle(11)
                    gather(0, s("ov_g"))
                    pool.wait_ge(s("ov_step"), 7 * j + 7)
                    settle(12)
                    scatter(0, 0, s("ov_s"))
                    pool.wait_ge(s("ov_s"), 16 * j + 16)
                    pool.tensor_tensor(spare[:, 13:14], iota_p[:, :], iota_p[:, :], ALU.add).then_inc(s("ov_end"), 1)
            pool.nop().then_inc(s("y_all"), 1)

        @block.scalar
        def _(act):
            act.dma_start(W_sb[:, :, :], W.rearrange("(t p) d -> p t d", p=P)).then_inc(s("w_in"), 16)
            act.dma_start(attn[:, 0, :], a_src.rearrange("h d -> (h d)").rearrange("(t p) -> p t", p=P)).then_inc(s("small_in"), 16)
            act.dma_start(attn[:, 1, :], a_dst.rearrange("h d -> (h d)").rearrange("(t p) -> p t", p=P)).then_inc(s("small_in"), 16)
            act.dma_start(emb[:, :], et_emb[:, :]).then_inc(s("small_in"), 16)
            act.dma_start(low[:, :], bass.AP(tensor=dst.tensor, offset=0, ap=[[0, 1], [GE, NG]])).then_inc(s("small_in"), 16)
            act.wait_ge(s("dx_pad"), 1)
            act.dma_start(dx_i[1:NG - 1, :], bass.AP(tensor=dst.tensor, offset=GE - 1, ap=[[GE, NG - 2], [1, RW]])).then_inc(s("dx_in"), 16)
            act.dma_start(dx_i[0:1, 1:RW], dst[0:RW - 1].rearrange("(a e) -> a e", a=1)).then_inc(s("dx_in"), 16)
            act.dma_start(dx_i[NG - 1:NG, 0:NE - (NG - 1) * GE + 1],
                          dst[(NG - 1) * GE - 1:NE].rearrange("(a e) -> a e", a=1)).then_inc(s("dx_in"), 16)
            act.wait_ge(s("ln_scr"), 1)
            act.activation(rstd[:, :], rstd[:, :], ACT.Sqrt).then_inc(s("ln1_std"), 1)
            for a in range(A):
                act.wait_ge(s("pe_wt"), a + 1)
                act.copy(WT[:, a, :], ps[:, 6 + a % 2, :]).then_inc(s("act_wt"), 1)
            act.wait_ge(s("pe_v"), 1)
            act.copy(V[:, :, :].rearrange("p a h -> p (a h)"), ps[:, 3, 0:A * 2 * H]).then_inc(s("v_done"), 1)
            for t in range(NT):
                act.wait_ge(s("pe_xt"), t + 1)
                act.copy(xT[:, :, t * P:(t + 1) * P],
                         ps[:, t % 2, :].rearrange("p (a n) -> p a n", a=A)).then_inc(s("act_xt"), 1)
            for t in range(NT):
                act.wait_ge(s("pe_h"), t + 1)
                act.copy(ring[:, t, :], ps[:, 7, :]).then_inc(s("act_h"), 1)
            for b in range(4):
                act.wait_ge(s("pe_er"), b + 1)
                for k in range(4):
                    h, q = (4 * b + k) // 2, (4 * b + k) % 2
                    act.copy(E1[:, h, 1 + q * P:1 + (q + 1) * P], ps[0:NG, b, k * P:(k + 1) * P]).then_inc(s("act_er"), 1)
            act.wait_ge(s("dve_d"), 1)
            act.activation(p_c[:, 0:NC, :], e_c[:, :, :], ACT.Exp).then_inc(s("p_done"), 1)
            act.wait_ge(s("p_done"), 1)

            def body(i, first):
                for k in range(SLOTS):
                    act.wait_ge(landed[k], 16 * i + 16)
                    for h in (H - 2, H - 1):
                        o = act.activation(ring[:, k, h * HD:(h + 1) * HD], ring[:, k, h * HD:(h + 1) * HD], ACT.Copy,
                                           scale=p_c[:, bass.ds(SLOTS * i + k, 1), h:h + 1].rearrange("p a b -> p (a b)"))
                    o.then_inc(s("act_msg"), 1)

            body(0, True)
            act.wait_ge(s("px_in"), 16 * NX)
            with act.Fori(1, ITER) as i:
                body(i, False)

            def root(g):
                act.wait_ge(s("gnn_var"), g + 1)
                b = slice(*LNG[g])
                act.activation(rstd[:, b], rstd[:, b], ACT.Sqrt).then_inc(s("gnn_std"), 1)

            def gnn_normalise(g):
                act.wait_ge(s("gnn_off"), g + 1)
                for t in range(*LNG[g]):
                    act.activation(acc[:, t, :], acc[:, t, :], ACT.Identity, bias=mean2[:, t:t + 1],
                                   scale=rstd[:, t:t + 1]).then_inc(s("gnn_norm"), 1)

            def x1_roots(g):
                act.wait_ge(s("x1_var"), g + 1)
                b = slice(*LNG[g])
                act.activation(vw[:, :, b], vw[:, :, b], ACT.Sqrt).then_inc(s("x1_std"), 1)

            def x1_normalise(g):
                act.wait_ge(s("nx_ready"), g + 1)
                for t in range(*LNG[g]):
                    act.activation(xn[:, t, :], x_sb[:, t, :], ACT.Identity, bias=mean2[:, t:t + 1],
                                   scale=rv[:, 1, t:t + 1]).then_inc(s("nx_done"), 1)
                for t in range(*LNG[g]):
                    act.wait_ge(s("pe_nxT"), t + 1)
                    act.copy(xT[:, :, t * P:(t + 1) * P],
                             ps[:, t % 2, :].rearrange("p (a n) -> p a n", a=A)).then_inc(s("act_nxT"), 1)

            def shared_in(n):
                c0, c1 = 512 * n, min(512 * n + 512, NPAD)
                if n:
                    act.wait_ge(s("pe_sh3"), M * n)
                act.wait_ge(s("act_nxT"), c1 // P)
                for a in range(A):
                    act.activation(nxs[:, a, 0:c1 - c0], xT[:, a, c0:c1], ACT.Identity, bias=sg[:, 1, a:a + 1],
                                   scale=sg[:, 0, a:a + 1]).then_inc(s("nxs_done"), 1)

            def shared_gate(k):
                n, m = k // M, k % M
                c = min(512, NPAD - 512 * n)
                act.wait_ge(s("pe_sh1"), k + 1)
                if k:
                    act.wait_ge(s("hs_done"), k)
                act.activation(sil[:, 0:c], ps[:, 4, 0:c], ACT.Silu, bias=sbias[:, 0, m:m + 1]).then_inc(s("act_sh"), 1)

            G = len(LNG)
            for step in range(G + 3):
                if step < G:
                    root(step)
                if 0 <= step - 1 < G:
                    gnn_normalise(step - 1)
                if 0 <= step - 2 < G:
                    x1_roots(step - 2)
                if 0 <= step - 3 < G:
                    x1_normalise(step - 3)
                if step - 3 == G - 2:
                    shared_in(0)
            for n in range(NSH):
                if n:
                    shared_in(n)
                if n == NSH - 1:
                    act.wait_ge(s("top_done"), 1)
                    act.activation(wk[:, :, :], topf[:, :, :], ACT.Exp, scale=-1.0).then_inc(s("exp_top"), 1)
                for m in range(M):
                    shared_gate(M * n + m)

            def gate(u, e, k, done, bank):
                for m in range(M):
                    o = act.activation(s1[:, k, m, :], ps[:, bank, m * TS:(m + 1) * TS], ACT.Silu,
                                       bias=bT[:, 0, m, e])
                o.then_inc(s(done), 1)

            def out_rows(y, bank, done):
                act.copy(yo[:, y, :], ps[0:TS, bank, :]).then_inc(s(done), 1)

            def experts(i, lo, cw_in=False, z=False):
                for u in range(U):
                    act.wait_ge(s("pe_h1"), U * i + u + 1)
                    if U * lo + u >= 2:
                        act.wait_ge(s("hT_done"), U * i + u - 1)
                    gate(u, bass.ds(U * i + u, 1), u % 2, "act_s1", 2 + u % 2)
                    if U * lo + u >= 1:
                        act.wait_ge(s("pe_y"), U * i + u)
                        if U * lo + u - 1 >= U:
                            act.wait_ge(y_out[(u - 1) % U], 16 * i if u else 16 * i - 16)
                        out_rows((u - 1) % U, 6 + (u - 1) % 2, "y_ready")
                    if cw_in and u >= 1:
                        act.wait_ge(s("pe_cwT"), u)
                        c0, c1 = 512 * (u - 1), min(512 * u, NPAD)
                        act.copy(cwT[0:NEX, c0:c1], ps[0:NEX, 1, 0:c1 - c0]).then_inc(s("cwT_done"), 1)
                    if z and u == 0:
                        if lo >= 2:
                            act.wait_ge(s("z_added"), i - 1)
                        act.wait_ge(s("cwT_done"), NSH)
                        act.wait_ge(s("cwT_one"), 1)
                        act.copy(zc[:, :], cwT[:, bass.ds(P * i - P, P)]).then_inc(s("z_staged"), 1)

            experts(0, 0, cw_in=True)
            experts(1, 1, z=True)
            with act.Fori(2, NT + 1) as i:
                experts(i, 2, z=True)
            with act.Fori(NT + 1, NIT) as i:
                experts(i, 2)
            act.wait_ge(s("pe_y"), NEX)
            act.wait_ge(y_out[U - 1], 16 * (NIT - 1))
            out_rows(U - 1, 6 + (U - 1) % 2, "y_ready")
            act.wait_ge(s("over_done"), 1)
            n = act.value_load(nover_i[0:1, 0:1], min_val=0, max_val=NOV)
            with act.If(n > 0):
                with act.Fori(0, n) as j:
                    act.wait_ge(s("ov_step"), 7 * j + 3)
                    e = act.value_load(over_i[0:1, bass.ds(j, 1)], min_val=0, max_val=NEX - 1)
                    gate(0, bass.ds(e, 1), 0, "ov_step", 2)
                    act.wait_ge(s("ov_step"), 7 * j + 6)
                    out_rows(0, 6, "ov_step")
            for t in range(NT):
                act.wait_ge(s("out_ready"), t + 1)
                rows = P if t < NT - 1 else LAST
                act.dma_start(out[t * P:t * P + rows, :], x_sb[0:rows, t, :]).then_inc(s("stored"), 16)
            act.wait_ge(s("stored"), 16 * NT)

        @block.tensor
        def _(pe):
            def T(o, i, n=P):
                return pe.transpose(o, i, ident[0:n, 0:n])

            pe.wait_ge(s("const"), 1)
            pe.wait_ge(s("erow_f"), 1)
            for k in range(4):
                b, col = 4 + k // 2, (k % 2) * NC
                T(ps[:, b, col:col + P], erowf[:, 0, k, :])
                o = T(ps[:, b, col + P:col + NC], erowf[0:NC - P, 1, k, :], NC - P)
            o.then_inc(s("pe_erow"), 1)
            pe.wait_ge(s("w_in"), 16)
            for a in range(A):
                if a >= 2:
                    pe.wait_ge(s("act_wt"), a - 1)
                for t in range(A):
                    o = T(ps[:, 6 + a % 2, t * P:(t + 1) * P], W_sb[:, t, a * P:(a + 1) * P])
                o.then_inc(s("pe_wt"), 1)
            pe.wait_ge(s("ablk_done"), 1)
            for a in range(A):
                for t in range(A):
                    o = pe.matmul(ps[:, 3, a * 2 * H:(a + 1) * 2 * H], W_sb[:, t, a * P:(a + 1) * P],
                                  ablk[:, t * 2 * H:(t + 1) * 2 * H], start=(t == 0), stop=(t == A - 1))
            o.then_inc(s("pe_v"), 1)
            for t in range(NT):
                pe.wait_ge(s("ln1"), t + 1)
                if t >= 2:
                    pe.wait_ge(s("act_xt"), t - 1)
                for a in range(A):
                    o = T(ps[:, t % 2, a * P:(a + 1) * P], xn[:, t, a * P:(a + 1) * P])
                o.then_inc(s("pe_xt"), 1)
            pe.wait_ge(s("srcx_done"), 1)
            pe.matmul(ps[:, 6, 0:NX], ones[:, :], cnt[:, :], start=True, stop=True)
            pe.matmul(ps[:, 6, 64:64 + NG], ones[0:1, :], lowf[:, :], start=True, stop=True).then_inc(s("pe_low"), 1)
            pe.wait_ge(s("v_done"), 1)
            for t in range(NT):
                pe.wait_ge(s("act_xt"), t + 1)
                for a in range(A):
                    o = pe.matmul(ps[:, 2, t * 2 * H:(t + 1) * 2 * H], xT[:, a, t * P:(t + 1) * P], V[:, a, :],
                                  start=(a == 0), stop=(a == A - 1))
            o.then_inc(s("pe_tab"), 1)
            def h_tile(t):
                if t == 0:
                    pe.wait_ge(s("act_wt"), A)
                else:
                    pe.wait_ge(s("act_h"), t)
                for a in range(A):
                    o = pe.matmul(ps[:, 7, :], xT[:, a, t * P:(t + 1) * P], WT[:, a, :],
                                  start=(a == 0), stop=(a == A - 1))
                o.then_inc(s("pe_h"), 1)

            pe.wait_ge(s("tab_done"), 1)
            pe.wait_ge(s("emb_done"), 1)
            pe.wait_ge(s("dve_low"), 1)
            for g, (q, c0, n) in enumerate(GROUPS):
                if g == 0 or GROUPS[g - 1][0] != q:
                    pe.wait_ge(s("hot"), q + 1)
                if g >= 2:
                    pe.wait_ge(s("sel_read"), g - 1)
                for side in range(2):
                    for c in range(c0, c0 + n):
                        oh = keys[:, q % 2, side, (c - PIECES[q][0]) * P:(c - PIECES[q][0] + 1) * P]
                        for r in range(3):
                            o = pe.matmul(ps[:, 2 * (g % 2) + side, (c - c0) * NT * H:(c - c0 + 1) * NT * H], oh,
                                          tab3[:, r, side, :], start=(r == 0), stop=(r == 2))
                for c in range(c0, c0 + n):
                    oh = keys[0:TY, q % 2, 2, (c - PIECES[q][0]) * P:(c - PIECES[q][0] + 1) * P]
                    for r in range(3):
                        o = pe.matmul(ps[:, 4 + c // 64, (c % 64) * H:(c % 64 + 1) * H], oh, emb3[:, r, :],
                                      start=(r == 0), stop=(r == 2))
                o.then_inc(s("pe_sel"), 1)
                if g % 3 == 2 and g // 3 < NT:
                    h_tile(g // 3)
            pe.wait_ge(s("e_done"), 1)
            for b in range(4):
                for k in range(4):
                    h, q = (4 * b + k) // 2, (4 * b + k) % 2
                    o = T(ps[0:NG, b, k * P:(k + 1) * P], e_c[:, q::2, h])
                o.then_inc(s("pe_er"), 1)
            pe.wait_ge(s("ends_done"), 1)
            for k in range(4):
                o = T(ps[0:H, 4, k * NG:(k + 1) * NG], ends[:, k, :], NG)
            o.then_inc(s("pe_ends"), 1)
            pe.wait_ge(s("carry_done"), 1)
            T(ps[0:NG, 5, 0:H], carry[:, 0, 0:NG], H)
            T(ps[0:NG, 5, H:2 * H], carry[:, 1, 1:NG + 1], H).then_inc(s("pe_carry"), 1)
            pe.wait_ge(s("m_done"), 1)
            for k in range(2 * H):
                h, q = k // 2, k % 2
                o = T(ps[:, k // 6, (k % 6) * NG:(k % 6 + 1) * NG], E1[:, h, 1 + q * P:1 + (q + 1) * P], NG)
            o.then_inc(s("pe_m"), 1)

            def body(i, first):
                for j in range(IB):
                    if not (first and j < 4):
                        pe.wait_ge(s("acc_done"), IB * i + j - 3)
                    for u in range(2):
                        k = 2 * j + u
                        pe.wait_ge(s("dve_msg"), SLOTS * i + k + 1)
                        pe.wait_ge(s("act_msg"), SLOTS * i + k + 1)
                        pe.matmul(ps[:, j % 4, :], S[:, k % 4, :], ring[:, k, :], start=(u == 0), stop=(u == 1))
                    for u in range(2):
                        k = 2 * j + u
                        o = pe.matmul(ps[:, 4 + j % 4, 0:H], S[:, k % 4, :],
                                      p_c[:, bass.ds(SLOTS * i + k, 1), :].rearrange("p a h -> p (a h)"),
                                      start=(u == 0), stop=(u == 1))
                    o.then_inc(s("pe_item"), 1)

            body(0, True)
            pe.wait_ge(s("px_in"), 16 * NX)
            with pe.Fori(1, ITER) as i:
                body(i, False)
            LGB = (2, 3, 6, 7)
            pe.wait_ge(s("param_in"), 16 * 14)
            pe.wait_ge(s("acc_done"), NI)
            for a in range(A):
                T(ps[:, 4, a * NEX:(a + 1) * NEX], gam[:, a::A], NEX)
                T(ps[:, 4, (A + a) * NEX:(A + a + 1) * NEX], bet[:, a::A], NEX)
                T(ps[:, 5, (A + a) * NEX:(A + a + 1) * NEX], wg[:, a::A], NEX)
            for k in range(2):
                for m in range(M):
                    o = T(ps[:, 5, (k * M + m) * NEX:(k * M + m + 1) * NEX], bb1[:, k, m * P:(m + 1) * P], NEX)
            o.then_inc(s("pe_param"), 1)

            def nx_turn(t):
                pe.wait_ge(s("nx_done"), t + 1)
                if t >= 2:
                    pe.wait_ge(s("act_nxT"), t - 1)
                for a in range(A):
                    o = T(ps[:, t % 2, a * P:(a + 1) * P], xn[:, t, a::A])
                o.then_inc(s("pe_nxT"), 1)

            def logits(t):
                pe.wait_ge(s("act_nxT"), t + 1)
                if t >= 4:
                    pe.wait_ge(s("lg_read"), t - 3)
                for a in range(A):
                    o = pe.matmul(ps[:, LGB[t % 4], 0:NEX], xT[:, a, t * P:(t + 1) * P], wgT[:, a, :],
                                  start=(a == 0), stop=(a == A - 1))
                o.then_inc(s("pe_lg"), 1)

            def shared_up(k):
                n, m = k // M, k % M
                c = min(512, NPAD - 512 * n)
                pe.wait_ge(s("nxs_done"), A * (n + 1))
                for w, read in ((0, "act_sh"), (1, "hs_done")):
                    if k:
                        pe.wait_ge(s(read), k)
                    for a in range(A):
                        o = pe.matmul(ps[:, 4 + w, 0:c], ws13[:, w, a, m * P:(m + 1) * P],
                                      nxs[:, a, 0:c], start=(a == 0), stop=(a == A - 1))
                    o.then_inc(s("pe_sh1" if w == 0 else "pe_sh3"), 1)

            pe.wait_ge(s("param_done"), 1)
            late = LNG[-1][0]
            nx_turn(0)
            for t in range(1, late):
                nx_turn(t)
                logits(t - 1)
            logits(late - 1)
            nx_turn(late)
            for t in range(late + 1, NT):
                nx_turn(t)
                logits(t - 1)
            logits(NT - 1)
            pe.wait_ge(s("sh_in"), 48)
            shared_up(0)
            pe.wait_ge(s("before_done"), 1)
            for t0, t1 in ((0, 8), (8, NT)):
                o = ps[:, 6 + t0 // 8, 0:(t1 - t0) * NEX]
                pe.matmul(o, tri[:, :], hits[:, t0:t1, :].rearrange("p t e -> p (t e)"), start=True, stop=False)
                pe.matmul(o, ones[:, :], before[:, t0:t1, :].rearrange("p t e -> p (t e)"), start=False, stop=True)
            pe.matmul(ps[:, 7, 2 * NEX:3 * NEX], ones[:, :], before[:, NT, :], start=True, stop=True).then_inc(s("pe_rank"), 1)
            shared_up(1)
            shared_up(2)
            pe.wait_ge(s("onehots"), 1)
            for k in range(2 * NT):
                o = pe.matmul(ps[0:TS, 0, 0:NTILE], rank1h[:, k, :], tile1h[:, k, :], start=(k == 0), stop=(k == 2 * NT - 1))
            o.then_inc(s("pe_slots"), 1)
            for k in range(3, M * NSH):
                shared_up(k)

            def shared_down(t):
                if t >= 3:
                    pe.wait_ge(s("zh_added"), t - 2)
                for m in range(M):
                    o = pe.matmul(ps[:, (1, 6, 7)[t % 3], :], hsT[:, m, t * P:(t + 1) * P], ws2[:, m, :],
                                  start=(m == 0), stop=(m == M - 1))
                o.then_inc(s("pe_zh"), 1)

            def turn(u, bank, done):
                for a in range(A):
                    o = T(ps[:, bank, a * TS:(a + 1) * TS], xg[:, u, a::A], TS)
                o.then_inc(s(done), 1)

            def up(u, k, bank, done1, done3):
                for w, done in ((0, done1), (1, done3)):
                    for m in range(M):
                        for a in range(A):
                            o = pe.matmul(ps[:, bank + 2 * w, m * TS:(m + 1) * TS], w13[:, u, w, a, m * P:(m + 1) * P],
                                          xgT[:, k, a, :], start=(a == 0), stop=(a == A - 1))
                    if done:
                        o.then_inc(s(done), 1)

            def down(u, k, bank, done):
                for m in range(M):
                    o = pe.matmul(ps[0:TS, bank, :], hT[:, k, m, :], w2s[:, u, m, :], start=(m == 0), stop=(m == M - 1))
                o.then_inc(s(done), 1)

            def experts(i, lo, last, cw_out=False, z=False):
                for u in range(U):
                    e = U * i + u
                    pe.wait_ge(w_landed[u], 48 * i + 48)
                    pe.wait_ge(s("xgT_done"), e + 1)
                    if U * lo + u >= 2:
                        pe.wait_ge(s("act_s1"), e - 1)
                        pe.wait_ge(s("hT_done"), e - 1)
                    up(u, u % 2, 2 + u % 2, "pe_h1", "pe_h3")
                    if not (last and u == U - 1):
                        v_ = (u + 1) % U
                        pe.wait_ge(xg_landed[v_], 16 * i + (16 if v_ else 32))
                        turn(v_, 0, "pe_xgT")
                    if U * lo + u >= 1:
                        pe.wait_ge(s("hT_done"), e)
                        if U * lo + u >= 3:
                            pe.wait_ge(s("y_ready"), e - 2)
                        down((u - 1) % U, (u - 1) % 2, 6 + (u - 1) % 2, "pe_y")
                    if cw_out and u >= 1:
                        if u == 1:
                            pe.wait_ge(s("cw_done"), 1)
                        else:
                            pe.wait_ge(s("cwT_done"), u - 1)
                        for t in range(4 * (u - 1), min(4 * u, NT)):
                            o = T(ps[0:NEX, 1, (t % 4) * P:(t % 4 + 1) * P], cw[:, t, :])
                        o.then_inc(s("pe_cwT"), 1)
                    if z and u == 1:
                        pe.wait_ge(s("z_staged"), i)
                        pe.matmul(ps[:, 1, :], zc[:, :], b2a[:, :], start=True, stop=True).then_inc(s("pe_z"), 1)

            for t in range(4):
                shared_down(t)
            pe.wait_ge(xg_landed[0], 16)
            turn(0, 0, "pe_xgT")
            pe.wait_ge(s("hs_done"), M * NSH)
            for t in range(4, NT):
                shared_down(t)
            pe.wait_ge(s("zh_added"), NT)
            experts(0, 0, False, cw_out=True)
            with pe.Fori(1, NT + 1) as i:
                experts(i, 1, False, z=True)
            with pe.Fori(NT + 1, NIT - 1) as i:
                experts(i, 1, False)
            experts(NIT - 1, NIT - 1, True)
            pe.wait_ge(s("hT_done"), NEX)
            pe.wait_ge(s("y_ready"), NEX - 2)
            down(U - 1, (U - 1) % 2, 6 + (U - 1) % 2, "pe_y")
            pe.wait_ge(s("over_done"), 1)
            pe.wait_ge(s("y_ready"), NEX)
            n = pe.value_load(nover_i[0:1, 0:1], min_val=0, max_val=NOV)
            with pe.If(n > 0):
                with pe.Fori(0, n) as j:
                    pe.wait_ge(s("ov_g"), 16 * j + 16)
                    turn(0, 0, "ov_step")
                    pe.wait_ge(s("ov_step"), 7 * j + 2)
                    pe.wait_ge(s("ov_w"), 48 * j + 48)
                    up(0, 0, 2, None, "ov_step")
                    pe.wait_ge(s("ov_step"), 7 * j + 5)
                    down(0, 0, 6, "ov_step")

        @block.vector
        def _(v):
            chain = [0]

            def link(ins):
                chain[0] += 1
                ins.then_inc(s("dve"), 1)
                v.wait_ge(s("dve"), chain[0])

            v.memset(x_sb[96:P, NT - 1, :], 0.0).then_inc(s("x_pad"), 1)
            v.wait_ge(s("key_in"), 48)
            v.tensor_single_scalar(kint[0:KP, 0, :], kint[0:KP, 0, :], P - 1, op=ALU.bitwise_and)
            link(v.tensor_single_scalar(kint[0:KP, 1, :], kint[0:KP, 1, :], P - 1, op=ALU.bitwise_and))
            v.tensor_copy(kb[0:KP, :, :], kint[0:KP, :, :]).then_inc(s("key_ready"), 1)
            v.memset(kpad[:, :], float(PADNODE % P)).then_inc(s("key_ready"), 1)
            v.nop().then_inc(s("key_ready"), 1)
            v.wait_ge(s("erow_in"), 16 * 12)
            v.tensor_copy(erowf[:, 0, 0:3, :], erow[:, 0, 0:3, :])
            v.tensor_copy(erowf[:, 0, 3, :], erow[:, 0, 3, :].bitcast(F32))
            v.tensor_copy(erowf[0:32, 1, 0:3, :], erow[0:32, 1, 0:3, :])
            v.tensor_copy(erowf[0:32, 1, 3, :], erow[0:32, 1, 3, :].bitcast(F32)).then_inc(s("erow_f"), 1)
            v.wait_ge(s("small_in"), 64)
            link(v.memset(ablk[:, :], 0.0))
            for side in range(2):
                for half in range(2):
                    rows = slice(64 * half, 64 * half + 64)
                    o = side * H + half
                    last = v.tensor_copy(ablk[rows, o:o + 3 * (2 * H + 2) + 1:2 * H + 2], attn[rows, side, :])
            last.then_inc(s("ablk_done"), 1)

            def split(parts, value, rest):
                link(v.tensor_copy(parts[0], value))
                link(v.tensor_tensor(rest, value, parts[0], ALU.subtract))
                link(v.tensor_copy(parts[1], rest))
                link(v.tensor_tensor(rest, rest, parts[1], ALU.subtract))
                link(v.tensor_copy(parts[2], rest))

            link(v.tensor_scalar(emb[:, :], emb[:, :], 1.0, None, ALU.add))
            split([emb3[:, r, :] for r in range(3)], emb[:, :], embr[:, :])
            v.nop().then_inc(s("emb_done"), 1)
            v.wait_ge(s("x_in"), 64)
            for t in range(NT):
                o = v.bn_stats(stats[:, t, :], x_sb[:, t, :])
            link(o)
            for t in range(NT):
                o = v.bn_aggr(mv[:, t, :], stats[:, t, :])
            link(o)
            v.tensor_scalar(rstd[:, :], mv[:, :, 1], EPS, None, ALU.add).then_inc(s("ln_scr"), 1)
            v.wait_ge(s("ln1_std"), 1)
            link(v.reciprocal(rstd[:, :], rstd[:, :]))
            for t in range(NT):
                v.tensor_scalar(xn[:, t, :], x_sb[:, t, :], mv[:, t, 0:1], rstd[:, t:t + 1],
                                ALU.subtract, ALU.mult).then_inc(s("ln1"), 1)
            v.wait_ge(s("pe_erow"), 1)
            v.tensor_copy(ecol[:, 0:2, :], ps[:, 4, 0:2 * NC].rearrange("p (k c) -> p k c", k=2))
            link(v.tensor_copy(ecol[:, 2:4, :], ps[:, 5, 0:2 * NC].rearrange("p (k c) -> p k c", k=2)))
            v.wait_ge(s("const"), 1)
            link(v.tensor_single_scalar(low[:, :], low[:, :], 7, op=ALU.arith_shift_right))
            v.tensor_copy(lowf[:, :], low[:, :])
            v.tensor_copy(witem[:, 0:NG], low[:, :])
            for w in range(NX):
                v.memset(witem[:, NG + w:NG + w + 1], w + 1)
                link(v.tensor_scalar(cmp[:, :], ecol[:, 1, :], float(P * (w + 1)), 0.0, ALU.is_lt, ALU.add,
                                     accum_out=cnt[:, w:w + 1]))
            v.tensor_copy(srcx[:, 0:NC], ecol[:, 0, :])
            link(v.tensor_copy(hi[:, :, :], ecol[:, 0:2, :]))
            link(v.tensor_single_scalar(hi[:, :, :], hi[:, :, :], 7, op=ALU.arith_shift_right))
            link(v.tensor_copy(hif[:, :, :], hi[:, :, :]))
            v.nop().then_inc(s("srcx_done"), 1)
            ib = iota_row[:, 0:NT].unsqueeze(1).to_broadcast([P, 2 * NC, NT])
            v.tensor_tensor(sel_hi[:, :, :, :].rearrange("p s c a -> p (s c) a"),
                            hif[:, :, :].rearrange("p s c -> p (s c)").unsqueeze(2).to_broadcast([P, 2 * NC, NT]), ib, ALU.is_equal)
            v.wait_ge(s("pe_low"), 1)
            link(v.tensor_copy(start_i[:, :], ps[:, 6, 0:NX]))
            v.tensor_single_scalar(grp[:, :], start_i[:, :], 8, op=ALU.arith_shift_right)
            link(v.tensor_single_scalar(rem[:, :], start_i[:, :], GE - 1, op=ALU.bitwise_and))
            link(v.tensor_scalar(shift[:, :], rem[:, :], 0.0, 1.0e6, ALU.is_equal, ALU.mult))
            for w in range(NX):
                o = v.tensor_scalar(shift[:, w:w + 1], shift[:, w:w + 1], float(P * (w + 1)), None, ALU.add)
            link(o)
            lo2 = ps[:, 6, 64:64 + NG].unsqueeze(2).to_broadcast([P, NG, 2])
            v.scalar_tensor_tensor(out=dloc[:, 0:NC].rearrange("p (g u) -> p g u", u=2), in0=lo2, scalar=-float(P),
                                   in1=ecol[:, 1, :].rearrange("p (g u) -> p g u", u=2), op0=ALU.mult,
                                   op1=ALU.add).then_inc(s("dve_low"), 1)
            for w in range(NX):
                g = v.value_load(grp[0:1, w:w + 1], min_val=0, max_val=NG - 1)
                c = NC + 2 * w
                v.tensor_copy(srcx[:, c:c + 2], ecol[:, 0, bass.ds(2 * g, 2)])
                v.tensor_scalar(dloc[:, c:c + 2], ecol[:, 1, bass.ds(2 * g, 2)], shift[:, w:w + 1], None, ALU.subtract)
            v.nop().then_inc(s("srcx_done"), 1)
            v.wait_ge(s("dx_in"), 48)
            link(v.tensor_copy(dx[:, :], dx_i[:, :]))
            link(v.tensor_tensor(eq[:, 1:RW], dx[:, 1:RW], dx[:, 0:RW - 1], ALU.is_equal))
            link(v.tensor_reduce(allsame[:, :], eq[:, 2:GE + 1], AX_X, ALU.min))
            for h in range(H):
                v.tensor_scalar(ends[:, 2, h:h + 1], eq[:, 1:2], allsame[:, 0:1], None, ALU.mult)
                v.tensor_scalar(ends[:, 3, h:h + 1], eq[:, RW - 1:RW], allsame[:, 0:1], None, ALU.mult)

            v.wait_ge(s("pe_tab"), 1)
            pt = ps[:, 2, 0:NT * 2 * H].rearrange("p (a s h) -> p s a h", a=NT, s=2)
            link(v.tensor_copy(tab[:, :, :].rearrange("p s (a h) -> p s a h", a=NT), pt))
            tf = tab[:, :, :].rearrange("p s k -> p (s k)")
            split([tab3[:, r, :, :].rearrange("p s k -> p (s k)") for r in range(3)], tf, tabr[:, :])
            v.nop().then_inc(s("tab_done"), 1)

            def hot(q):
                c0, n = PIECES[q]
                v.wait_ge(s(f"keys_landed{q % 2}"), 48 * (q // 2 + 1))
                v.tensor_scalar(keys[:, q % 2, 0:2, 0:n * P], keys[:, q % 2, 0:2, 0:n * P], iota_p[:, 0:1], None, ALU.is_equal)
                v.tensor_scalar(keys[0:TY, q % 2, 2, 0:n * P], keys[0:TY, q % 2, 2, 0:n * P], iota_p[0:TY, 0:1], None,
                                ALU.is_equal).then_inc(s("hot"), 1)

            hot(0)
            for g, (q, c0, n) in enumerate(GROUPS):
                if g + 1 < len(GROUPS) and GROUPS[g + 1][0] != q:
                    hot(q + 1)
                v.wait_ge(s("pe_sel"), g + 1)
                pr = prod[:, 0:n * 2 * NT * H].rearrange("p (c s a h) -> p s c a h", c=n, s=2, a=NT)
                for side in range(2):
                    o = v.tensor_tensor(pr[:, side, :, :, :],
                                        ps[:, 2 * (g % 2) + side, 0:n * NT * H].rearrange("p (c a h) -> p c a h", c=n, a=NT),
                                        sel_hi[:, side, c0:c0 + n, :].unsqueeze(3).to_broadcast([P, n, NT, H]), ALU.mult)
                    o.then_inc(s("dve"), 1)
                    chain[0] += 1
                v.wait_ge(s("dve"), chain[0])
                v.nop().then_inc(s("sel_read"), 1)
                link(v.tensor_reduce(e_c[:, c0:c0 + n, :],
                                     prod[:, 0:n * 2 * NT * H].rearrange("p (c k h) -> p c h k", c=n, h=H), AX_X, ALU.add))
            ef = e_c[:, :, :].rearrange("p c h -> p (c h)")
            link(v.scalar_tensor_tensor(out=ef, in0=ef, scalar=0.2, in1=ef, op0=ALU.mult, op1=ALU.max))
            for b in range(3):
                c0, c1 = 64 * b, min(64 * b + 64, NC)
                o = v.tensor_tensor(e_c[:, c0:c1, :].rearrange("p c h -> p (c h)"),
                                    ps[:, 4 + b, 0:(c1 - c0) * H], e_c[:, c0:c1, :].rearrange("p c h -> p (c h)"), ALU.mult)
            link(o)
            v.tensor_tensor(e_c[:, :, :], e_c[:, :, :], ecol[:, 3, :].unsqueeze(2).to_broadcast([P, NC, H]),
                            ALU.mult).then_inc(s("e_done"), 1)
            v.wait_ge(s("act_h"), NT)
            v.memset(E1[:, :, 0:1], 0.0)
            v.memset(E1[:, :, RW - 1:RW], 0.0)
            v.memset(F1[:, :, 0:1], 0.0)
            v.memset(F1[:, :, RW - 1:RW], 0.0)
            v.memset(F2[:, :, 0:1], 0.0)
            v.memset(F2[:, :, RW - 1:RW], 0.0)
            v.tensor_copy(F1[:, :, 1:GE + 1], eq[:, 1:GE + 1].unsqueeze(1).to_broadcast([NG, H, GE]))
            link(v.tensor_copy(F2[:, :, 1:GE + 1], eq[:, 2:GE + 2].unsqueeze(1).to_broadcast([NG, H, GE])))
            v.nop().then_inc(s("dx_read"), 1)
            e1, e2, f1, f2 = (z.rearrange("p h k -> p (h k)") for z in (E1, E2, F1, F2))

            def segment_max():
                link(v.tensor_tensor_scan(e2, f1, e1, 0.0, ALU.mult, ALU.max))
                link(v.tensor_tensor_scan(e1[:, ::-1], f2[:, ::-1], e2[:, ::-1], 0.0, ALU.mult, ALU.max))

            v.wait_ge(s("act_er"), 16)
            segment_max()
            v.tensor_copy(ends[:, 0, :], E1[:, :, GE])
            v.tensor_copy(ends[:, 1, :], E1[:, :, 1]).then_inc(s("ends_done"), 1)
            v.wait_ge(s("pe_ends"), 1)
            link(v.tensor_copy(endsT[:, :, :].rearrange("h k g -> h (k g)"), ps[0:H, 4, 0:4 * NG]))
            v.memset(carry[:, 0, 0:1], 0.0)
            v.memset(carry[:, 1, NG:NG + 1], 0.0)
            v.tensor_tensor_scan(carry[:, 0, 1:NG + 1], endsT[:, 2, :], endsT[:, 0, :], 0.0, ALU.mult, ALU.max)
            v.tensor_tensor_scan(carry[:, 1, 0:NG][:, ::-1], endsT[:, 3, ::-1], endsT[:, 1, ::-1], 0.0, ALU.mult,
                                 ALU.max).then_inc(s("carry_done"), 1)
            v.wait_ge(s("pe_carry"), 1)
            v.tensor_copy(E1[:, :, 0], ps[0:NG, 5, 0:H])
            link(v.tensor_copy(E1[:, :, RW - 1], ps[0:NG, 5, H:2 * H]))
            segment_max()
            v.nop().then_inc(s("m_done"), 1)
            v.wait_ge(s("pe_m"), 1)
            for k in range(2 * H):
                h, q = k // 2, k % 2
                o = v.tensor_tensor(e_c[:, q::2, h], e_c[:, q::2, h], ps[:, k // 6, (k % 6) * NG:(k % 6 + 1) * NG], ALU.subtract)
            o.then_inc(s("dve_d"), 1)
            v.memset(accs[:, :, :], 0.0)
            v.memset(ps[:, 3, :], 0.0)
            link(v.memset(ps[:, 7, 0:H], 0.0))
            v.wait_ge(s("p_done"), 1)

            def add_item(it, j, number):
                w = v.value_load(witem[0:1, it], min_val=0, max_val=NT - 1)
                a = acc[:, bass.ds(w, 1), :].rearrange("p a d -> p (a d)")
                b = accs[:, bass.ds(w, 1), :].rearrange("p a d -> p (a d)")
                v.tensor_tensor(b, ps[:, 4 + j % 4, 0:H], b, ALU.add)
                v.tensor_tensor(a, ps[:, j % 4, :], a, ALU.add).then_inc(s("acc_done"), 1)

            def body(i, first):
                for j in range(IB):
                    for u in range(2):
                        k = 2 * j + u
                        if not (first and j < 2):
                            v.wait_ge(s("pe_item"), IB * i + j - 1)
                        v.tensor_scalar(S[:, k % 4, :], iota_row[:, :],
                                        dloc[:, bass.ds(SLOTS * i + k, 1)], None, ALU.is_equal)
                        v.wait_ge(landed[k], 16 * i + 16)
                        n = (H - 2) * HD
                        v.tensor_tensor(ring[:, k, 0:n].rearrange("p (h d) -> p h d", d=HD),
                                        ring[:, k, 0:n].rearrange("p (h d) -> p h d", d=HD),
                                        p_c[:, bass.ds(SLOTS * i + k, 1), 0:H - 2].rearrange("p a h -> p (a h)")
                                        .unsqueeze(2).to_broadcast([P, H - 2, HD]), ALU.mult).then_inc(s("dve_msg"), 1)
                    if not (first and j == 0):
                        v.wait_ge(s("pe_item"), IB * i + j)
                        if not (first and j == 1):
                            v.wait_ge(s("acc_done"), IB * i + j - 1)
                        add_item(bass.ds(IB * i + j - 1, 1), j - 1, None)

            v.wait_ge(s("acc_zero"), 1)
            body(0, True)
            v.wait_ge(s("px_in"), 16 * NX)
            with v.Fori(1, ITER) as i:
                body(i, False)
            v.wait_ge(s("pe_item"), NI)
            v.wait_ge(s("acc_done"), NI - 1)
            add_item(slice(NI - 1, NI), IB - 1, None)
            v.wait_ge(s("acc_done"), NI)
            link(v.tensor_scalar(accs[:, :, :], accs[:, :, :], 1e-10, None, ALU.add))
            v.reciprocal(accs[:, :, :], accs[:, :, :]).then_inc(s("accs_done"), 1)
            v.wait_ge(s("pe_param"), 1)
            v.tensor_copy(gT[:, :, :, :].rearrange("p k a e -> p (k a e)"), ps[:, 4, 0:2 * A * NEX])
            v.tensor_copy(bT[:, :, :, :].rearrange("p k m e -> p (k m e)"), ps[:, 5, 0:2 * M * NEX])
            v.tensor_copy(wgT[:, :, :].rearrange("p a e -> p (a e)"), ps[:, 5, A * NEX:2 * A * NEX]).then_inc(s("param_done"), 1)

            def issue(ins):
                chain[0] += 1
                ins.then_inc(s("dve"), 1)
                return chain[0]

            def add_and_stats(g, out, extra, ready, t0=0):
                tiles = range(*LNG[g])
                added = []
                for t in tiles:
                    v.wait_ge(s(ready), t + 1 - t0)
                    added.append(issue(v.tensor_tensor(out[:, t, :], extra[:, t, :], out[:, t, :], ALU.add)))
                for t, n in zip(tiles, added):
                    v.wait_ge(s("dve"), n)
                    o = v.bn_stats(stats[:, t, :], out[:, t, :])
                link(o)
                for t in tiles:
                    o = v.bn_aggr(mv[:, t, :], stats[:, t, :])
                link(o)

            def gnn_sum(g):
                add_and_stats(g, acc, xn, "divided" if g else "divided0", LNG[0][1] if g else 0)
                b = slice(*LNG[g])
                v.tensor_scalar(rstd[:, b], mv[:, b, 1], EPS, None, ALU.add).then_inc(s("gnn_var"), 1)

            def gnn_scale(g):
                b = slice(*LNG[g])
                v.wait_ge(s("gnn_std"), g + 1)
                link(v.reciprocal(rstd[:, b], rstd[:, b]))
                v.scalar_tensor_tensor(out=mean2[:, b], in0=mv[:, b, 0], scalar=-1.0, in1=rstd[:, b], op0=ALU.mult,
                                       op1=ALU.mult).then_inc(s("gnn_off"), 1)

            def x1_sum(g):
                add_and_stats(g, x_sb, acc, "gnn_gam")
                b = slice(*LNG[g])
                v.tensor_scalar(vw[:, 0, b], mv[:, b, 1], EPS, None, ALU.add)
                v.tensor_scalar(vw[:, 1, b], mv[:, b, 1], 1.0 + EPS, EPS * EPS, ALU.mult, ALU.add).then_inc(s("x1_var"), 1)

            def x1_scale(g):
                b = slice(*LNG[g])
                v.wait_ge(s("x1_std"), g + 1)
                link(v.reciprocal(rv[:, :, b], vw[:, :, b]))
                v.tensor_tensor(inv_r2[:, b], vw[:, 1, b], rv[:, 0, b], ALU.mult)
                v.scalar_tensor_tensor(out=mean2[:, b], in0=mv[:, b, 0], scalar=-1.0, in1=rv[:, 1, b], op0=ALU.mult,
                                       op1=ALU.mult).then_inc(s("nx_ready"), 1)

            def best_two(g):
                tiles = range(*LNG[g])
                for t in tiles:
                    v.wait_ge(s("pe_lg"), t + 1)
                    v.scalar_tensor_tensor(out=lg[:, t, :], in0=ps[:, (2, 3, 6, 7)[t % 4], 0:NEX], scalar=inv_r2[:, t:t + 1],
                                           in1=bg_b[:, :], op0=ALU.mult, op1=ALU.add).then_inc(s("lg_read"), 1)
                found = []
                for t in tiles:
                    v.wait_ge(s("lg_read"), t + 1)
                    found.append(issue(v.max(top[:, t, :], lg[:, t, :])))
                for t, n in zip(tiles, found):
                    v.wait_ge(s("dve"), n)
                    o = v.max_index(topi[:, t, :], top[:, t, :], lg[:, t, :])
                return o

            def shared_hidden(k):
                n, m = k // M, k % M
                c0, c1 = 512 * n, min(512 * n + 512, NPAD)
                v.wait_ge(s("pe_sh3"), k + 1)
                v.wait_ge(s("act_sh"), k + 1)
                v.scalar_tensor_tensor(out=hsT[:, m, c0:c1], in0=ps[:, 5, 0:c1 - c0], scalar=sbias[:, 1, m:m + 1],
                                       in1=sil[:, 0:c1 - c0], op0=ALU.add, op1=ALU.mult).then_inc(s("hs_done"), 1)

            v.wait_ge(s("accs_done"), 1)
            for t in range(*LNG[0]):
                o3 = acc[:, t, :].rearrange("p (h d) -> p h d", h=H)
                v.tensor_tensor(o3, o3, accs[:, t, :].unsqueeze(2).to_broadcast([P, H, HD]), ALU.mult
                                ).then_inc(s("divided0"), 1)
            v.wait_ge(s("xb_done"), 1)
            G = len(LNG)
            for step in range(G + 4):
                if step < G:
                    gnn_sum(step)
                if 0 <= step - 1 < G:
                    gnn_scale(step - 1)
                if 0 <= step - 2 < G:
                    x1_sum(step - 2)
                if 0 <= step - 3 < G:
                    x1_scale(step - 3)
                if 0 <= step - 4 < G:
                    o = best_two(step - 4)
            link(o)
            v.tensor_copy(topf[:, :, :], top[:, :, 0:2]).then_inc(s("top_done"), 1)
            link(v.tensor_copy(eidx[:, :, :], topi[:, :, 0:2]))
            erow2 = iota_row[:, 0:NEX].unsqueeze(1).to_broadcast([P, 2 * NT, NEX])
            ohf, tmpf = (z[:, :, :, :].rearrange("p t k e -> p (t k) e") for z in (oh, tmp))
            link(v.tensor_tensor(ohf, erow2, eidx[:, :, :].rearrange("p t k -> p (t k)").unsqueeze(2).to_broadcast([P, 2 * NT, NEX]),
                                 ALU.is_equal))
            v.wait_ge(s("tri_done"), 5)
            link(v.tensor_scalar(oh[:, NT - 1, :, :], oh[:, NT - 1, :, :], real[:, 0:1], None, ALU.mult))
            v.memset(before[:, 0, :], 0.0)
            link(v.tensor_tensor(hits[:, :, :], oh[:, :, 0, :], oh[:, :, 1, :], ALU.add))
            for t in range(NT):
                link(v.tensor_tensor(before[:, t + 1, :], before[:, t, :], hits[:, t, :], ALU.add))
            v.nop().then_inc(s("before_done"), 1)
            shared_hidden(0)
            v.wait_ge(s("pe_rank"), 1)
            v.tensor_tensor(tmp[:, 0:8, :, :], oh[:, 0:8, :, :],
                            ps[:, 6, :].rearrange("p (t e) -> p t e", t=8).unsqueeze(2).to_broadcast([P, 8, 2, NEX]), ALU.mult)
            rf, of, ef_ = (z[:, :, :].rearrange("p t k -> p (t k)") for z in (rnk, obs, eidx))
            tf_, kf, nov = tens[:, :], tens[:, 0:2 * NT], tens[:, 2 * NT:2 * NT + NEX]
            v.tensor_scalar(nov, ps[:, 7, 2 * NEX:3 * NEX], 1.0 / TS, -0.5 / TS - 0.5, ALU.mult, ALU.add)
            link(v.tensor_tensor(tmp[:, 8:NT, :, :], oh[:, 8:NT, :, :],
                                 ps[:, 7, 0:(NT - 8) * NEX].rearrange("p (t e) -> p t e", e=NEX).unsqueeze(2)
                                 .to_broadcast([P, NT - 8, 2, NEX]), ALU.mult))
            link(v.tensor_reduce(rf, tmpf, AX_X, ALU.add))
            link(v.tensor_scalar(kf, rf, 1.0 / TS, 0.5 / TS - 0.5, ALU.mult, ALU.add))
            link(v.tensor_scalar(tf_, tf_, ROUND, None, ALU.add))
            link(v.tensor_scalar(tf_, tf_, -ROUND, 0.0, ALU.add, ALU.max))
            link(v.tensor_tensor_scan(inc[:, :], ones[:, 0:NEX], nov, 0.0, ALU.mult, ALU.add))
            link(v.tensor_tensor(exc[:, :], inc[:, :], nov, ALU.subtract))
            link(v.tensor_tensor(tmpf, ohf, exc[:, :].unsqueeze(1).to_broadcast([P, 2 * NT, NEX]), ALU.mult))
            link(v.tensor_reduce(of, tmpf, AX_X, ALU.add))
            v.scalar_tensor_tensor(out=rf, in0=kf, scalar=-float(TS), in1=rf, op0=ALU.mult, op1=ALU.add)
            link(v.scalar_tensor_tensor(out=of, in0=of, scalar=float(NEX - 1), in1=kf, op0=ALU.add, op1=ALU.add))
            v.tensor_scalar(rnk[:, NT - 1, :], rnk[:, NT - 1, :], far[:, 0:1], None, ALU.add)
            link(v.tensor_tensor(of, of, ef_, ALU.subtract))
            link(v.scalar_tensor_tensor(out=of, in0=kf, scalar=1.0, in1=of, op0=ALU.min, op1=ALU.mult))
            link(v.tensor_tensor(of, of, ef_, ALU.add))
            shared_hidden(1)
            v.wait_ge(s("nx_out"), 16 * NT)
            v.wait_ge(s("pe_nxT"), NT)
            v.tensor_tensor(rank1h[:, :, :], iota_row[:, 0:TS].unsqueeze(1).to_broadcast([P, 2 * NT, TS]),
                            rf.unsqueeze(2).to_broadcast([P, 2 * NT, TS]), ALU.is_equal)
            link(v.tensor_tensor(tile1h[:, :, :], iota_row[:, 0:NTILE].unsqueeze(1).to_broadcast([P, 2 * NT, NTILE]),
                                 of.unsqueeze(2).to_broadcast([P, 2 * NT, NTILE]), ALU.is_equal))
            v.tensor_tensor(tile1h[:, :, :], tile1h[:, :, :], payload[:, :, :].rearrange("p t k -> p (t k)").unsqueeze(2)
                            .to_broadcast([P, 2 * NT, NTILE]), ALU.mult).then_inc(s("onehots"), 1)
            shared_hidden(2)
            v.wait_ge(s("pe_slots"), 1)
            link(v.tensor_scalar(slotf[:, :], ps[0:TS, 0, 0:NTILE], 0.0, float(SKIP), ALU.is_equal, ALU.mult))
            link(v.scalar_tensor_tensor(out=slotf[:, :], in0=ps[0:TS, 0, 0:NTILE], scalar=-1.0, in1=slotf[:, :],
                                        op0=ALU.add, op1=ALU.add))
            link(v.tensor_copy(slot_tab[:, :, 1], slotf[:, :]))
            v.tensor_single_scalar(slot_tab[:, :, 0], slot_tab[:, :, 1], 1, op=ALU.arith_shift_right).then_inc(s("slots_done"), 1)
            for j0 in range(0, NOV, 16):
                n = min(16, NOV - j0)
                c3 = tmpf[0:1, 0:n, :]
                link(v.tensor_tensor(c3, inc[0:1, :].unsqueeze(1).to_broadcast([1, n, NEX]),
                                     iota_row[0:1, j0:j0 + n].unsqueeze(2).to_broadcast([1, n, NEX]), ALU.is_le))
                link(v.tensor_reduce(counts[0:1, j0:j0 + n], c3, AX_X, ALU.add))
            v.tensor_copy(over_i[:, :], counts[0:1, 0:NOV])
            v.tensor_copy(nover_i[:, :], inc[0:1, NEX - 1:NEX]).then_inc(s("over_done"), 1)
            v.wait_ge(s("exp_top"), 1)
            link(v.tensor_scalar(wk[:, :, :], wk[:, :, :], 1.0, None, ALU.add))
            link(v.reciprocal(wk[:, :, :], wk[:, :, :]))
            link(v.tensor_tensor(wsum[:, :], wk[:, :, 0], wk[:, :, 1], ALU.add))
            link(v.reciprocal(wsum[:, :], wsum[:, :]))
            link(v.tensor_tensor(wk[:, :, :], wk[:, :, :], wsum[:, :].unsqueeze(2).to_broadcast([P, NT, 2]), ALU.mult))
            link(v.tensor_tensor(tmpf, ohf, wk[:, :, :].rearrange("p t k -> p (t k)").unsqueeze(2)
                                 .to_broadcast([P, 2 * NT, NEX]), ALU.mult))
            v.tensor_tensor(cw[:, :, :], tmp[:, :, 0, :], tmp[:, :, 1, :], ALU.add).then_inc(s("cw_done"), 1)
            v.wait_ge(s("cw_done"), 1)
            v.memset(cwT[NEX:NEX + 1, :], 1.0).then_inc(s("cwT_one"), 1)
            for k in range(3, M * NSH):
                shared_hidden(k)

            def scale_in(u, e, bank, k, done):
                for a in range(A):
                    o = v.tensor_scalar(xgT[:, k, a, :], ps[:, bank, a * TS:(a + 1) * TS], gT[:, 0, a, e], gT[:, 1, a, e],
                                        ALU.mult, ALU.add)
                o.then_inc(s(done), 1)

            def hidden(e, bank, k, done):
                for m in range(M):
                    o = v.scalar_tensor_tensor(out=hT[:, k, m, :], in0=ps[:, bank, m * TS:(m + 1) * TS], scalar=bT[:, 1, m, e],
                                               in1=s1[:, k, m, :], op0=ALU.add, op1=ALU.mult)
                o.then_inc(s(done), 1)

            def experts(i, lo, last, z=False):
                for u in range(U):
                    e = U * i + u
                    if z and u == 2:
                        v.wait_ge(s("pe_z"), i)
                        zt = x_sb[:, bass.ds(i - 1, 1), :].rearrange("p a d -> p (a d)")
                        v.tensor_tensor(zt, ps[:, 1, :], zt, ALU.add).then_inc(s("z_added"), 1)
                    if not (last and u == U - 1):
                        v.wait_ge(s("pe_xgT"), e + 2)
                        if U * lo + u >= 1:
                            v.wait_ge(s("pe_h3"), e)
                        scale_in(u, bass.ds(e + 1, 1), 0, (u + 1) % 2, "xgT_done")
                    v.wait_ge(s("pe_h3"), e + 1)
                    v.wait_ge(s("act_s1"), e + 1)
                    if U * lo + u >= 2:
                        v.wait_ge(s("pe_y"), e - 1)
                    hidden(bass.ds(e, 1), 4 + u % 2, u % 2, "hT_done")

            def shared_add(t):
                v.wait_ge(s("pe_zh"), t + 1)
                v.tensor_tensor(x_sb[:, t, :], ps[:, (1, 6, 7)[t % 3], :], x_sb[:, t, :], ALU.add).then_inc(s("zh_added"), 1)

            for t in range(4):
                shared_add(t)
            v.wait_ge(s("pe_xgT"), 1)
            scale_in(0, slice(0, 1), 0, 0, "xgT_done")
            for t in range(4, NT):
                shared_add(t)
            v.wait_ge(s("zh_added"), NT)
            experts(0, 0, False)
            with v.Fori(1, NT + 1) as i:
                experts(i, 1, False, z=True)
            with v.Fori(NT + 1, NIT - 1) as i:
                experts(i, 1, False)
            experts(NIT - 1, NIT - 1, True)
            n = v.value_load(nover_i[0:1, 0:1], min_val=0, max_val=NOV)
            with v.If(n > 0):
                v.nop().then_inc(s("ov_end"), 1)
                with v.Fori(0, n) as j:
                    v.wait_ge(s("ov_step"), 7 * j + 1)
                    e = v.value_load(over_i[0:1, bass.ds(j, 1)], min_val=0, max_val=NEX - 1)
                    scale_in(0, bass.ds(e, 1), 0, 0, "ov_step")
                    v.wait_ge(s("ov_step"), 7 * j + 4)
                    hidden(bass.ds(e, 1), 4, 0, "ov_step")
            for t in range(NT):
                v.wait_ge(s(f"y_in{t % 4}"), 16 * (t // 4 + 1))
                rows = P if t < NT - 1 else LAST
                for k in range(2):
                    o = v.scalar_tensor_tensor(out=x_sb[0:rows, t, :], in0=yin[0:rows, t % 4, k, :], scalar=wk[0:rows, t, k:k + 1],
                                               in1=x_sb[0:rows, t, :], op0=ALU.mult, op1=ALU.add)
                    if k == 0:
                        link(o)
                o.then_inc(s("out_ready"), 1)


_INS = ['x', 'src', 'dst', 'edge_type_8', 'edge_weight', 'L0_gnn_W', 'L0_gnn_a_src', 'L0_gnn_a_dst', 'L0_gnn_et_emb',
        'L0_gnn_ln_gamma', 'L0_gnn_ln_beta', 'L0_ffn_Wg', 'L0_ffn_bg', 'L0_ffn_gamma', 'L0_ffn_beta', 'L0_ffn_W1',
        'L0_ffn_b1', 'L0_ffn_W3', 'L0_ffn_b3', 'L0_ffn_W2', 'L0_ffn_b2', 'L0_ffn_gs', 'L0_ffn_bs', 'L0_ffn_Ws1',
        'L0_ffn_bs1', 'L0_ffn_Ws3', 'L0_ffn_bs3', 'L0_ffn_Ws2', 'L0_ffn_bs2']


def kernel(**inputs):
    import numpy as _np
    import concourse.bacc as _bacc
    from concourse import mybir as _mybir
    from concourse.bass_utils import run_bass_kernel_spmd as _run

    nc = _bacc.Bacc("TRN2", target_bir_lowering=False, num_devices=1)
    arrays, args = {}, []
    for name in _INS:
        a = _np.ascontiguousarray(inputs[name])
        arrays[f"in_{name}_dram"] = a
        args.append(nc.dram_tensor(f"in_{name}_dram", a.shape, _mybir.dt.from_np(a.dtype), kind="ExternalInput").ap())
    out = nc.dram_tensor("out_0_dram", (1250, 512), _mybir.dt.float32, kind="ExternalOutput").ap()
    gnn_moe_kernel(nc, *args, out)
    r = _run(nc, [arrays], core_ids=[0])
    return r.results[0]["out_0_dram"]
```

```python
from contextlib import ExitStack

import concourse.bass as bass
from concourse import mybir

F32 = mybir.dt.float32
BF16 = mybir.dt.bfloat16
I32 = mybir.dt.int32
U32 = mybir.dt.uint32
ALU = mybir.AluOpType
ACT = mybir.ActivationFunctionType
AX_X = mybir.AxisListType.X

P = 128
EPS = 1e-5
TOKENS = 80


def gnn_moe_kernel(nc, x, src, dst, etype, eweight, W, a_src, a_dst, et_emb, ln_gamma, ln_beta,
                   Wg, bg, gamma, beta, W1, b1, W3, b3, W2, b2, gs, bs, Ws1, bs1, Ws3, bs3, Ws2, bs2, out):
    N, D = x.shape
    NE = src.shape[0]
    H, HD = a_src.shape
    TY = et_emb.shape[0]
    NT = -(-N // P)
    NPAD = NT * P
    LAST = N - (NT - 1) * P
    A = D // P
    GE = 2 * P
    NG = -(-NE // GE)
    NC = 2 * NG
    NX = NT - 1
    NI = NG + NX
    NCX = 2 * NI
    EPAD = NC * P
    PADNODE = NPAD - 1
    IB = 8
    SLOTS = 2 * IB
    ITER = NI // IB
    assert NI % IB == 0
    RW = GE + 2
    FULLC = NE // P
    REST = NE - FULLC * P

    NEX, _, HF = W1.shape
    M = HF // P
    TS = TOKENS
    NOV = (2 * N) // TS
    NTILE = NEX + NOV
    LNG = [(0, 2), (2, 4), (4, 7), (7, NT)]
    ROUND = 1.5 * 2 ** 23
    HV = H - 3
    NSH = -(-NPAD // 512)
    U = 4
    NIT = NEX // U
    SKIP = 1 << 20
    assert NT + 2 < NIT - 1
    BESIDE = {0: (("down", 3),), 1: (("up", 4),), 2: (("up", 5),), 3: (("down", 4), ("down", 5)),
              4: (("cw", 0), ("cw", 1)), 5: (("cw", 2), ("down", 6)), 6: (("down", 7), ("down", 8)), 7: (("down", 9),)}
    DOWN0 = 3
    SPARE = (1, 7)

    def beside(e, kind):
        return sum(1 for g in range(e) for k, _ in BESIDE.get(g, ()) if k == kind)


    nx_d = nc.dram_tensor("nx_rows", [NPAD, D], F32).ap()
    y_d = nc.dram_tensor("y_rows", [2 * NPAD, D], F32).ap()
    h_d = nc.dram_tensor("h_rows", [NPAD, D], F32).ap()
    bkey_d = nc.dram_tensor("edge_keys", [3, EPAD], BF16).ap()

    with ExitStack() as ctx:
        ctx.enter_context(nc.allow_non_contiguous_dma(reason="a few hundred single elements of small inputs"))
        def sb(name, shape, dt=F32):
            return ctx.enter_context(nc.sbuf_tensor(name, shape, dt))

        def sem(name):
            return ctx.enter_context(nc.semaphore(name))

        arena = sb("arena", [P, 17500])

        class Carver:
            def __init__(self, buf, size):
                self.buf, self.size, self.at = buf, size, 0

            def __call__(self, shape, dt=F32):
                n = 1
                for d in shape[1:]:
                    n *= d
                words = (n * (2 if dt == BF16 else 4) + 3) // 4
                a = self.buf[0:shape[0], self.at:self.at + words]
                self.at += words
                assert self.at <= self.size, (self.at, self.size)
                if dt != F32:
                    a = a.bitcast(dt)[:, 0:n]
                if len(shape) > 2:
                    names = " ".join(f"d{k}" for k in range(1, len(shape)))
                    a = a.rearrange(f"p ({names}) -> p {names}", **{f"d{k}": shape[k] for k in range(1, len(shape))})
                return a

        first = Carver(arena, 17500)
        ps = ctx.enter_context(nc.psum_tensor("ps", [P, 8, 512], F32))

        ident = sb("ident", [P, P])
        ones = sb("ones", [P, P])
        iota_row = sb("iota_row", [P, P])
        spare = sb("spare", [P, 16])
        iota_p = sb("iota_p", [P, 1])
        iota_m = sb("iota_m", [P, 1])
        x_sb = sb("x_sb", [P, NT, D])
        xn = sb("xn", [P, NT, D])
        xT = sb("xT", [P, A, NPAD])
        acc = sb("acc", [P, NT, D])
        accs = sb("accs", [P, NT, H])
        stats = sb("stats", [P, NT, 6])
        mv = sb("mv", [P, NT, 2])
        rstd = sb("rstd", [P, NT])
        ring = sb("ring", [P, SLOTS, D])
        ring2 = arena[:, 0:SLOTS * D].rearrange("p (k d) -> p k d", k=SLOTS)
        W_sb = first([P, A, D])
        WT = first([P, A, D])
        attn = first([P, 2, A])
        ablk = first([P, A * 2 * H])
        V = first([P, A, 2 * H])
        tab = first([P, 2, NT * H])
        tabr = first([P, 2 * NT * H])
        tab3 = first([P, 3, 2, NT * H], BF16)
        emb = first([3 * TY, H])
        embr = first([3 * TY, H])
        emb3 = first([3 * TY, 3, H], BF16)
        embp = first([3 * TY, H], BF16)
        place = first([3 * TY, 3])
        beyond = first([3 * TY, 2])
        type_p = first([3 * TY, 1])
        erow = first([P, 2, 4, P], I32)
        erowf = first([P, 2, 4, P])
        ecol = sb("ecol", [P, 4, NC])
        hi = first([P, 2, NC], I32)
        hif = first([P, 2, NC])
        sel_hi = first([P, 2, NC, NT])
        srcx = sb("srcx", [P, NCX], U32)
        dloc = sb("dloc", [P, NCX])
        e_c = sb("e_c", [P, NC, H])
        p_c = sb("p_c", [P, NCX, H])
        PIECE = 10
        keys = [first([P, 3, PIECE * P], BF16) for _ in range(2)]
        keys.append(Carver(ring[:, NT:, :].rearrange("p k d -> p (k d)"), (SLOTS - NT) * D)([P, 3, PIECE * P], BF16))
        prod = first([P, 5 * 2 * NT * H])
        S = sb("S", [P, 4, P])
        idx_stage = sb("idx_stage", [P, 2, IB], U32)
        low = first([1, NG], I32)
        lowf = first([1, NG])
        cnt = sb("cnt", [P, NX])
        cmp = first([P, NC])
        start_i = sb("start_i", [P, NX], I32)
        grp = sb("grp", [P, NX], I32)
        rem = sb("rem", [P, NX], I32)
        shift = sb("shift", [P, NX])
        witem = sb("witem", [1, NI], I32)
        kint = first([P, 3, 160], I32)
        kb = first([P, 3, 160], BF16)
        kpad = first([3, EPAD - NE], BF16)
        E1, E2 = (arena[0:NG, SLOTS * D + k * H * RW:SLOTS * D + (k + 1) * H * RW].rearrange("p (h k) -> p h k", h=H)
                  for k in range(2))
        F1 = xT[0:NG, :, :].rearrange("p t d -> p (t d)")[:, 0:H * RW].rearrange("p (h k) -> p h k", h=H)
        F2 = xT[0:NG, :, :].rearrange("p t d -> p (t d)")[:, H * RW:2 * H * RW].rearrange("p (h k) -> p h k", h=H)
        dx_i = first([NG, RW], I32)
        dx = first([NG, RW])
        eq = first([NG, RW])
        ends = sb("ends", [NG, 4, H])
        allsame = sb("allsame", [NG, 1])
        endsT = sb("endsT", [H, 4, NG])
        carry = sb("carry", [H, 2, NG + 1])
        router = Carver(acc[:, :, :].rearrange("p t d -> p (t d)"), NT * D)
        top = sb("top", [P, NT, 8])
        topi = sb("topi", [P, NT, 8], U32)
        wk = sb("wk", [P, NT, 2])
        wsum = sb("wsum", [P, NT])
        mean2 = sb("mean2", [P, NT])
        inv_r2 = sb("inv_r2", [P, NT])
        slot_tab = sb("slot_tab", [TS, NTILE, 2], I32)
        payload = sb("payload", [P, NT, 2])
        vw = sb("vw", [P, 2, NT])
        rv = sb("rv", [P, 2, NT])
        far = sb("far", [P, 1])
        stage_g = sb("stage_g", [TS, U], U32)
        stage_s = sb("stage_s", [TS, U], U32)
        nover_i = sb("nover_i", [1, 1], I32)
        over_i = sb("over_i", [1, NOV], I32)
        later = Carver(arena, 17500)
        w13 = later([P, U, 2, A, HF])
        w2s = later([P, U, M, D])
        gam = later([NEX, D])
        bet = later([NEX, D])
        bb1 = later([NEX, 2, HF])
        wg = later([NEX, D])
        gT = later([P, 2, A, NEX])
        bT = later([P, 2, M, NEX])
        wgT = later([P, A, NEX])
        bg_b = later([P, NEX])
        shared = Carver(ring[:, :, :].rearrange("p k d -> p (k d)"), SLOTS * D)
        ws13 = shared([P, 2, A, HF])
        ws2 = shared([P, M, D])
        zc = shared([NEX + 1, P])
        hsT = shared([P, M, NPAD])
        sil = shared([P, 512])
        yin = Carver(ring[:, :, :].rearrange("p k d -> p (k d)"), SLOTS * D)([P, 4, 2, D])
        lnp = later([P, 2, D])
        sg = later([P, 2, A])
        sbias = later([P, 2, M])
        b2a = later([NEX + 1, D])
        toks = Carver(xn[:, :, :].rearrange("p t d -> p (t d)"), NT * D)
        xg = toks([TS, U, D])
        yo = toks([TS, U, D])
        xgT = toks([P, 2, A, TS])
        onehots = Carver(xn[:, :, :].rearrange("p t d -> p (t d)"), NT * D)
        rank1h = onehots([P, 2 * NT, TS])
        tile1h = onehots([P, 2 * NT, NTILE])
        lg = router([P, NT, NEX])
        oh = router([P, NT, 2, NEX])
        tmp = router([P, NT, 2, NEX])
        hits = router([P, NT, NEX])
        before = router([P, NT + 1, NEX])
        eidx = sb("eidx", [P, NT, 2])
        gates = Carver(hits[:, :, :].rearrange("p t e -> p (t e)"), NT * NEX)
        s1 = gates([P, 2, M, TS])
        hT = gates([P, 2, M, TS])
        topf = sb("topf", [P, NT, 2])
        rnk = sb("rnk", [P, NT, 2])
        tens = sb("tens", [P, 2 * NT + NEX])
        slotf = sb("slotf", [TS, NTILE])
        obs = sb("obs", [P, NT, 2])
        real = sb("real", [P, 1])
        counts = sb("counts", [P, NEX])
        inc = sb("inc", [P, NEX])
        exc = sb("exc", [P, NEX])
        tri = sb("tri", [P, P])
        cw = lg
        cwT = tmp[0:NEX + 1, :, :, :].rearrange("p t k e -> p (t k e)")

        names = {}

        def s(name):
            if name not in names:
                names[name] = sem(name)
            return names[name]

        w_landed = [sem(f"w_landed{k}") for k in range(U)]
        xg_landed = [sem(f"xg_landed{k}") for k in range(U)]
        y_out = [sem(f"y_out{k}") for k in range(U)]
        landed = [sem(f"row_landed{k}") for k in range(SLOTS)]

        block = ctx.enter_context(nc.Block())

        ek = bkey_d
        x_main = x[0:(NT - 1) * P].rearrange("(t p) d -> p t d", p=P)
        PIECES = [(q * PIECE, min(PIECE, NC - q * PIECE)) for q in range(-(-NC // PIECE))]
        GROUPS = []
        for q, (c0, n) in enumerate(PIECES):
            for c in range(c0, c0 + n, 5):
                GROUPS.append((q, c, min(5, c0 + n - c)))
        KP = NE // 160

        @block.sync
        def _(sp):
            sp.wait_ge(s("x_pad"), 1)
            for t in range(0, NT - 1, 3):
                sp.dma_start(x_sb[:, t:t + 3, :], x_main[:, t:t + 3, :]).then_inc(s("x_in"), 16)
            sp.dma_start(x_sb[0:LAST, NT - 1, :], x[(NT - 1) * P:N, :]).then_inc(s("x_in"), 16)
            sp.wait_ge(s("erow_pad"), 1)
            for k, a in enumerate((src, dst, etype, eweight.bitcast(I32))):
                sp.dma_start(erow[:, 0, k, :], a[0:P * P].rearrange("(c e) -> c e", e=P)).then_inc(s("erow_in"), 16)
                sp.dma_start(erow[0:FULLC - P, 1, k, :],
                             a[P * P:FULLC * P].rearrange("(c e) -> c e", e=P)).then_inc(s("erow_in"), 16)
                sp.dma_start(erow[FULLC - P:FULLC - P + 1, 1, k, 0:REST],
                             a[FULLC * P:NE].rearrange("(a e) -> a e", a=1)).then_inc(s("erow_in"), 16)
            for k, a in enumerate((src, dst, etype)):
                sp.dma_start(kint[0:KP, k, :], a.rearrange("(p j) -> p j", j=160)).then_inc(s("key_in"), 16)
            sp.wait_ge(s("key_ready"), 3)
            for k in range(3):
                sp.dma_start(ek[k, 0:NE].rearrange("(p j) -> p j", j=160), kb[0:KP, k, :]).then_inc(s("key_out"), 16)
            sp.dma_start(ek[:, NE:EPAD], kpad[:, :]).then_inc(s("key_out"), 16)
            sp.wait_ge(s("key_out"), 64)
            for q, (c0, n) in enumerate(PIECES):
                if q >= 3:
                    sp.wait_ge(s("pe_sel"), sum(1 for g in GROUPS if g[0] <= q - 3))
                for k in range(3):
                    rows = P if k < 2 else 3 * TY
                    sp.dma_start(keys[q % 3][0:rows, k, 0:n * P],
                                 bass.AP(tensor=ek.tensor, offset=k * EPAD + c0 * P, ap=[[0, rows], [1, n * P]])
                                 ).then_inc(s(f"keys_landed{q % 3}"), 16)
            for t in range(NT):
                sp.wait_ge(s("act_h"), t + 1)
                sp.dma_start(h_d[t * P:(t + 1) * P, :], ring[:, t, :]).then_inc(s("h_out"), 16)
            sp.wait_ge(s("dve_low"), 1)
            groups = [sp.value_load(grp[0:1, w:w + 1], min_val=0, max_val=NG - 1) for w in range(NX)]
            for w, g in enumerate(groups):
                at = slice(NC + 2 * w, NC + 2 * w + 2)
                sp.dma_start(srcx[:, at], srcx[:, bass.ds(2 * g, 2)]).then_inc(s("ex_in"), 16)
                sp.dma_start(dloc[:, at], ecol[:, 1, bass.ds(2 * g, 2)]).then_inc(s("ex_in"), 16)
            sp.wait_ge(s("p_done"), 1)
            for w, g in enumerate(groups):
                sp.dma_start(p_c[:, NC + 2 * w:NC + 2 * w + 2, :], p_c[:, bass.ds(2 * g, 2), :]).then_inc(s("px_in"), 16)
            for o, i in ((gam[:, :], gamma[:, :]), (bet[:, :], beta[:, :]), (bb1[:, 0, :], b1[:, :]),
                         (bb1[:, 1, :], b3[:, :]), (wg[:, :], Wg[:, :]), (b2a[0:NEX, :], b2[:, :]),
                         (b2a[NEX:NEX + 1, :], bs2.rearrange("(a d) -> a d", a=1)),
                         (bg_b[:, :], bass.AP(tensor=bg.tensor, offset=0, ap=[[0, P], [1, NEX]])),
                         (lnp[:, 0, :], bass.AP(tensor=ln_gamma.tensor, offset=0, ap=[[0, P], [1, D]])),
                         (lnp[:, 1, :], bass.AP(tensor=ln_beta.tensor, offset=0, ap=[[0, P], [1, D]])),
                         (sg[:, 0, :], gs.rearrange("(p a) -> p a", a=A)), (sg[:, 1, :], bs.rearrange("(p a) -> p a", a=A)),
                         (sbias[:, 0, :], bs1.rearrange("(m p) -> p m", p=P)),
                         (sbias[:, 1, :], bs3.rearrange("(m p) -> p m", p=P))):
                sp.dma_start(o, i).then_inc(s("param_in"), 16)

            def load_expert(u, e):
                sp.dma_start(w13[:, u, 0, :, :].rearrange("p a h -> p (a h)"),
                             W1[e, :, :].rearrange("o (p a) h -> p (o a h)", a=A)).then_inc(w_landed[u], 16)
                sp.dma_start(w13[:, u, 1, :, :].rearrange("p a h -> p (a h)"),
                             W3[e, :, :].rearrange("o (p a) h -> p (o a h)", a=A)).then_inc(w_landed[u], 16)
                sp.dma_start(w2s[:, u, :, :], W2[e, :, :].rearrange("o (m p) d -> p (o m) d", p=P)).then_inc(w_landed[u], 16)

            for u in range(U):
                sp.wait_ge(s("pe_item"), 2 * IB * (u + 1))
                load_expert(u, bass.ds(u, 1))
            sp.wait_ge(s("pe_item"), NI)
            for k, w in enumerate((Ws1, Ws3)):
                sp.dma_start(ws13[:, k, :, :].rearrange("p a h -> p (a h)"),
                             w.rearrange("(p a) h -> p (a h)", a=A)).then_inc(s("sh_in"), 16)
            sp.dma_start(ws2[:, :, :], Ws2.rearrange("(m p) d -> p m d", p=P)).then_inc(s("sh_in"), 16)
            for t in range(NT):
                sp.wait_ge(s("nx_done"), t + 1)
                sp.dma_start(nx_d[t * P:(t + 1) * P, :], xn[:, t, :]).then_inc(s("nx_out"), 16)
            with sp.Fori(1, NIT) as i:
                for u in range(U):
                    sp.wait_ge(s("pe_y"), U * (i - 1) + u + 1)
                    load_expert(u, bass.ds(U * i + u, 1))
            sp.wait_ge(s("over_done"), 1)
            sp.wait_ge(s("pe_y"), NEX)
            n = sp.value_load(nover_i[0:1, 0:1], min_val=0, max_val=NOV)
            with sp.If(n > 0):
                with sp.Fori(0, n) as j:
                    sp.wait_ge(s("ov_end"), j + 1)
                    e = sp.value_load(over_i[0:1, bass.ds(j, 1)], min_val=0, max_val=NEX - 1)
                    sp.dma_start(w13[:, 0, 0, :, :].rearrange("p a h -> p (a h)"),
                                 W1[bass.ds(e, 1), :, :].rearrange("o (p a) h -> p (o a h)", a=A)).then_inc(s("ov_w"), 16)
                    sp.dma_start(w13[:, 0, 1, :, :].rearrange("p a h -> p (a h)"),
                                 W3[bass.ds(e, 1), :, :].rearrange("o (p a) h -> p (o a h)", a=A)).then_inc(s("ov_w"), 16)
                    sp.dma_start(w2s[:, 0, :, :], W2[bass.ds(e, 1), :, :].rearrange("o (m p) d -> p (o m) d", p=P)
                                 ).then_inc(s("ov_w"), 16)
            sp.wait_ge(s("y_all"), 1)
            sp.wait_ge(s("z_added"), NT)
            yv = y_d.rearrange("(t p k) d -> t p (k d)", p=P, k=2)
            for t in range(NT):
                if t >= 4:
                    sp.wait_ge(s("out_ready"), t - 3)
                rows = P if t < NT - 1 else LAST
                sp.dma_start(yin[0:rows, t % 4, :, :].rearrange("p k d -> p (k d)"), yv[t, 0:rows, :]).then_inc(s(f"y_in{t % 4}"), 16)

        @block.gpsimd
        def _(pool):
            pool.memset(erow[0:32, 1, 0:2, :], PADNODE)
            pool.memset(erow[0:32, 1, 2:4, :], 0).then_inc(s("erow_pad"), 1)
            pool.memset(dx_i[:, :], PADNODE).then_inc(s("dx_pad"), 1)
            pool.memset(ident[:, :], 0.0).then_inc(s("poolc"), 1)
            pool.wait_ge(s("poolc"), 1)
            pool.affine_select(out=ident[:, :], in_=ident[:, :], compare_op=ALU.not_equal, fill=1.0, base=0,
                               pattern=[[-1, P]], channel_multiplier=1)
            pool.memset(ones[:, :], 1.0)
            pool.iota(iota_p[:, :], pattern=[[0, 1]], base=0, channel_multiplier=1,
                      allow_small_or_imprecise_dtypes=True)
            pool.iota(iota_row[:, :], pattern=[[1, P]], base=0, channel_multiplier=0,
                      allow_small_or_imprecise_dtypes=True).then_inc(s("const"), 1)
            pool.memset(tri[:, :], 1.0)
            pool.memset(real[:, :], 1.0).then_inc(s("tri_done"), 1)
            pool.memset(far[:, :], 0.0).then_inc(s("tri_done"), 1)
            pool.wait_ge(s("tri_done"), 2)
            pool.affine_select(out=tri[:, :], in_=tri[:, :], compare_op=ALU.is_gt, fill=0.0, base=0,
                               pattern=[[1, P]], channel_multiplier=-1).then_inc(s("tri_done"), 1)
            pool.affine_select(out=real[:, :], in_=real[:, :], compare_op=ALU.is_gt, fill=0.0, base=LAST,
                               pattern=[[0, 1]], channel_multiplier=-1).then_inc(s("tri_done"), 1)
            pool.affine_select(out=far[:, :], in_=far[:, :], compare_op=ALU.is_gt, fill=1.0e6, base=LAST,
                               pattern=[[0, 1]], channel_multiplier=-1).then_inc(s("tri_done"), 1)
            pool.iota(payload[:, :, :], pattern=[[2 * P, NT], [1, 2]], base=1, channel_multiplier=2,
                      allow_small_or_imprecise_dtypes=True).then_inc(s("tri_done"), 1)
            pool.memset(acc[:, :, :], 0.0).then_inc(s("acc_zero"), 1)
            pool.wait_ge(s("emb_done"), 1)
            for q, (c0, n) in enumerate(PIECES):
                pool.wait_ge(s(f"keys_landed{q % 3}"), 48 * (q // 3 + 1))
                pool.tensor_scalar(keys[q % 3][0:3 * TY, 2, 0:n * P], keys[q % 3][0:3 * TY, 2, 0:n * P], type_p[:, 0:1], None,
                                   ALU.is_equal).then_inc(s("hot_type"), 1)
            pool.wait_ge(s("pe_sel"), len(GROUPS))
            pool.wait_ge(s("srcx_done"), 1)
            pool.wait_ge(s("h_out"), 16 * NT)

            def settle(k):
                pool.tensor_tensor(spare[:, k:k + 1], iota_p[:, :], iota_p[:, :], ALU.add)

            def body(i, lo):
                for half in range(2):
                    used = IB * (i - 2 if lo == 2 else i - 1) + half * IB // 2
                    if lo >= 1:
                        for k in range(half * IB, (half + 1) * IB):
                            pool.wait_ge(landed[k], 16 * i)
                    if lo >= 2:
                        pool.wait_ge(s("pe_item"), used + 2)
                    if lo >= 1:
                        settle(12 + half)
                    pool.tensor_copy(idx_stage[:, half, :], srcx[:, bass.ds(SLOTS * i + IB * half, IB)]
                                     ).then_inc(s("stage"), 1)
                    pool.wait_ge(s("stage"), 2 * i + half + 1)
                    settle(14 + half)
                    for k in range(IB):
                        slot = half * IB + k
                        if lo >= 2 and k == 4:
                            pool.wait_ge(s("pe_item"), used + 4)
                            settle(slot // 4)
                        pool.indirect_dma_start(
                            out=(ring2 if lo == 1 else ring)[:, slot, :], out_offset=None, in_=h_d[:, :],
                            in_offset=bass.IndirectOffsetOnAxis(ap=idx_stage[:, half, k:k + 1], axis=0)
                        ).then_inc(landed[slot], 16)

            body(0, 0)
            pool.wait_ge(s("e_done"), 1)
            pool.wait_ge(s("dx_read"), 1)
            body(1, 1)
            pool.wait_ge(s("ex_in"), 32 * NX)
            body(2, 2)
            with pool.Fori(3, ITER) as i:
                body(i, 3)
            pool.wait_ge(s("param_in"), 16 * 14)
            for t in range(NT):
                pool.tensor_tensor(x_sb[:, t, :], x_sb[:, t, :], lnp[:, 1, :], ALU.add)

            def divide(g):
                for t in range(*LNG[g]):
                    o3 = acc[:, t, :].rearrange("p (h d) -> p h d", h=H)
                    pool.tensor_tensor(o3, o3, accs[:, t, :].unsqueeze(2).to_broadcast([P, H, HD]), ALU.mult
                                       ).then_inc(s("divided"), 1)

            def times_gamma(g):
                for t in range(*LNG[g]):
                    pool.wait_ge(s("gnn_norm"), t + 1)
                    pool.tensor_tensor(acc[:, t, :], acc[:, t, :], lnp[:, 0, :], ALU.mult).then_inc(s("gnn_gam"), 1)

            pool.wait_ge(s("accs_done"), 1)
            divide(1)
            divide(2)
            for g in range(len(LNG)):
                times_gamma(g)
                if g + 3 < len(LNG):
                    divide(g + 3)
            pool.wait_ge(s("slots_done"), 1)
            pool.wait_ge(s("nx_out"), 16 * NT)

            def gather(u, sems):
                pool.indirect_dma_start(out=xg[:, u, :], out_offset=None, in_=nx_d[:, :],
                                        in_offset=bass.IndirectOffsetOnAxis(ap=stage_g[:, u:u + 1], axis=0),
                                        bounds_check=NPAD - 1, oob_is_err=False).then_inc(sems, 16)

            def scatter(u, y, sems):
                pool.indirect_dma_start(out=y_d[:, :], out_offset=bass.IndirectOffsetOnAxis(ap=stage_s[:, u:u + 1], axis=0),
                                        in_=yo[:, y, :], in_offset=None, bounds_check=2 * NPAD - 1,
                                        oob_is_err=False).then_inc(sems, 16)

            pool.tensor_copy(stage_g[:, :], slot_tab[:, 0:U, 0]).then_inc(s("stage_g"), 1)
            pool.wait_ge(s("stage_g"), 1)
            for u in range(U):
                gather(u, xg_landed[u])

            def experts(i, first, last):
                if not first:
                    for u in range(U):
                        pool.wait_ge(y_out[u], 16 * i)
                if not last:
                    for u in range(U):
                        pool.wait_ge(xg_landed[u], 16 * i + 16)
                    pool.tensor_tensor(spare[:, 0:1], iota_p[:, :], iota_p[:, :], ALU.add)
                    pool.tensor_copy(stage_g[:, :], slot_tab[:, bass.ds(U * i + U, U), 0])
                elif not first:
                    pool.tensor_tensor(spare[:, 0:1], iota_p[:, :], iota_p[:, :], ALU.add)
                pool.tensor_copy(stage_s[:, :], slot_tab[:, bass.ds(U * i, U), 1]).then_inc(s("stage_s"), 1)
                pool.wait_ge(s("stage_s"), i + 1)
                settle(1)
                for u in range(U):
                    if not last:
                        pool.wait_ge(s("pe_xgT"), U * i + u + 1)
                        settle(2 + 2 * u)
                        gather(u, xg_landed[u])
                    pool.wait_ge(s("y_ready"), U * i + u + 1)
                    settle(3 + 2 * u)
                    scatter(u, u, y_out[u])

            experts(0, True, False)
            with pool.Fori(1, NIT - 1) as i:
                experts(i, False, False)
            experts(NIT - 1, False, True)
            for u in range(U):
                pool.wait_ge(y_out[u], 16 * NIT)
            n = pool.value_load(nover_i[0:1, 0:1], min_val=0, max_val=NOV)
            with pool.If(n > 0):
                with pool.Fori(0, n) as j:
                    pool.wait_ge(s("ov_end"), j + 1)
                    settle(10)
                    pool.tensor_copy(stage_g[:, 0:1], slot_tab[:, bass.ds(NEX + j, 1), 0])
                    pool.tensor_copy(stage_s[:, 0:1], slot_tab[:, bass.ds(NEX + j, 1), 1]).then_inc(s("ov_stage"), 1)
                    pool.wait_ge(s("ov_stage"), j + 1)
                    settle(11)
                    gather(0, s("ov_g"))
                    pool.wait_ge(s("ov_step"), 7 * j + 7)
                    settle(12)
                    scatter(0, 0, s("ov_s"))
                    pool.wait_ge(s("ov_s"), 16 * j + 16)
                    pool.tensor_tensor(spare[:, 13:14], iota_p[:, :], iota_p[:, :], ALU.add).then_inc(s("ov_end"), 1)
            pool.nop().then_inc(s("y_all"), 1)

        @block.scalar
        def _(act):
            act.dma_start(W_sb[:, :, :], W.rearrange("(t p) d -> p t d", p=P)).then_inc(s("w_in"), 16)
            act.dma_start(attn[:, 0, :], a_src.rearrange("h d -> (h d)").rearrange("(t p) -> p t", p=P)).then_inc(s("small_in"), 16)
            act.dma_start(attn[:, 1, :], a_dst.rearrange("h d -> (h d)").rearrange("(t p) -> p t", p=P)).then_inc(s("small_in"), 16)
            for r in range(3):
                act.dma_start(emb[r * TY:(r + 1) * TY, :], et_emb[:, :]).then_inc(s("small_in"), 16)
            act.dma_start(low[:, :], bass.AP(tensor=dst.tensor, offset=0, ap=[[0, 1], [GE, NG]])).then_inc(s("small_in"), 16)
            act.wait_ge(s("dx_pad"), 1)
            act.dma_start(dx_i[1:NG - 1, :], bass.AP(tensor=dst.tensor, offset=GE - 1, ap=[[GE, NG - 2], [1, RW]])).then_inc(s("dx_in"), 16)
            act.dma_start(dx_i[0:1, 1:RW], dst[0:RW - 1].rearrange("(a e) -> a e", a=1)).then_inc(s("dx_in"), 16)
            act.dma_start(dx_i[NG - 1:NG, 0:NE - (NG - 1) * GE + 1],
                          dst[(NG - 1) * GE - 1:NE].rearrange("(a e) -> a e", a=1)).then_inc(s("dx_in"), 16)
            act.wait_ge(s("ln_scr"), 1)
            act.activation(rstd[:, :], rstd[:, :], ACT.Sqrt).then_inc(s("ln1_std"), 1)
            for a in range(A):
                act.wait_ge(s("pe_wt"), a + 1)
                act.copy(WT[:, a, :], ps[:, 6 + a % 2, :]).then_inc(s("act_wt"), 1)
            act.wait_ge(s("pe_v"), 1)
            act.copy(V[:, :, :].rearrange("p a h -> p (a h)"), ps[:, 3, 0:A * 2 * H]).then_inc(s("v_done"), 1)
            for t in range(NT):
                act.wait_ge(s("pe_xt"), t + 1)
                act.copy(xT[:, :, t * P:(t + 1) * P],
                         ps[:, t % 2, :].rearrange("p (a n) -> p a n", a=A)).then_inc(s("act_xt"), 1)

            def hot_dst(q):
                c0, n = PIECES[q]
                k = keys[q % 3][:, 1, 0:n * P]
                act.wait_ge(s(f"keys_landed{q % 3}"), 48 * (q // 3 + 1))
                act.activation(k, k, ACT.Abs, bias=iota_m[:, 0:1]).then_inc(s("hot_dst"), 1)
                act.wait_ge(s("hot_dst"), 2 * q + 1)
                act.activation(k, k, ACT.Relu, bias=ones[:, 0:1], scale=-1.0).then_inc(s("hot_dst"), 1)

            act.wait_ge(s("emb_done"), 1)
            hot_dst(0)
            hot_dst(1)
            for g, (q, c0, n) in enumerate(GROUPS):
                if g + 1 < len(GROUPS) and GROUPS[g + 1][0] != q and q + 2 < len(PIECES):
                    hot_dst(q + 2)
                if g % 3 == 2 and g // 3 < NT:
                    t = g // 3
                    act.wait_ge(s("pe_h"), t + 1)
                    act.copy(ring[:, t, :], ps[:, 7, :]).then_inc(s("act_h"), 1)
            act.wait_ge(s("dx_read"), 1)
            for b in range(4):
                act.wait_ge(s("pe_er"), b + 1)
                for k in range(4):
                    h, q = (4 * b + k) // 2, (4 * b + k) % 2
                    act.copy(E1[:, h, 1 + q * P:1 + (q + 1) * P], ps[0:NG, b, k * P:(k + 1) * P]).then_inc(s("act_er"), 1)
            act.wait_ge(s("dve_d"), 1)
            act.activation(p_c[:, 0:NC, :], e_c[:, :, :], ACT.Exp).then_inc(s("p_done"), 1)
            act.wait_ge(s("p_done"), 1)

            def body(i, rows):
                for k in range(SLOTS):
                    act.wait_ge(landed[k], 16 * i + 16)
                    for h in range(HV, H):
                        o = act.activation(rows[:, k, h * HD:(h + 1) * HD], rows[:, k, h * HD:(h + 1) * HD], ACT.Copy,
                                           scale=p_c[:, bass.ds(SLOTS * i + k, 1), h:h + 1].rearrange("p a b -> p (a b)"))
                    o.then_inc(s("act_msg"), 1)

            body(0, ring)
            act.wait_ge(s("px_in"), 16 * NX)
            body(1, ring2)
            with act.Fori(2, ITER) as i:
                body(i, ring)

            def root(g):
                act.wait_ge(s("gnn_var"), g + 1)
                b = slice(*LNG[g])
                act.activation(rstd[:, b], rstd[:, b], ACT.Sqrt).then_inc(s("gnn_std"), 1)

            def gnn_normalise(g):
                act.wait_ge(s("gnn_off"), g + 1)
                for t in range(*LNG[g]):
                    act.activation(acc[:, t, :], acc[:, t, :], ACT.Identity, bias=mean2[:, t:t + 1],
                                   scale=rstd[:, t:t + 1]).then_inc(s("gnn_norm"), 1)

            def x1_roots(g):
                act.wait_ge(s("x1_var"), g + 1)
                b = slice(*LNG[g])
                act.activation(vw[:, :, b], vw[:, :, b], ACT.Sqrt).then_inc(s("x1_std"), 1)

            def x1_normalise(g):
                act.wait_ge(s("nx_ready"), g + 1)
                for t in range(*LNG[g]):
                    act.activation(xn[:, t, :], x_sb[:, t, :], ACT.Identity, bias=mean2[:, t:t + 1],
                                   scale=rv[:, 1, t:t + 1]).then_inc(s("nx_done"), 1)
                for t in range(*LNG[g]):
                    act.wait_ge(s("pe_nxT"), t + 1)
                    act.copy(xT[:, :, t * P:(t + 1) * P],
                             ps[:, t % 2, :].rearrange("p (a n) -> p a n", a=A)).then_inc(s("act_nxT"), 1)

            def shared_in(n):
                c0, c1 = 512 * n, min(512 * n + 512, NPAD)
                act.wait_ge(s("pe_lg"), c1 // P)
                act.wait_ge(s("act_nxT"), c1 // P)
                for a in range(A):
                    act.activation(xT[:, a, c0:c1], xT[:, a, c0:c1], ACT.Identity, bias=sg[:, 1, a:a + 1],
                                   scale=sg[:, 0, a:a + 1]).then_inc(s("nxs_done"), 1)

            def shared_gate(k):
                n, m = k // M, k % M
                c = min(512, NPAD - 512 * n)
                act.wait_ge(s("pe_sh1"), k + 1)
                if k:
                    act.wait_ge(s("hs_done"), k)
                act.activation(sil[:, 0:c], ps[:, 4 if k < 4 else SPARE[0], 0:c], ACT.Silu, bias=sbias[:, 0, m:m + 1]).then_inc(s("act_sh"), 1)

            G = len(LNG)
            for step in range(G + 3):
                if step < G:
                    root(step)
                if 0 <= step - 1 < G:
                    gnn_normalise(step - 1)
                if 0 <= step - 2 < G:
                    x1_roots(step - 2)
                if 0 <= step - 3 < G:
                    x1_normalise(step - 3)
                if step - 3 == G - 2:
                    shared_in(0)
            shared_in(1)
            for n in range(NSH):
                if 1 < n + 1 < NSH:
                    shared_in(n + 1)
                if n == NSH - 1:
                    act.wait_ge(s("top_done"), 1)
                    act.activation(wk[:, :, :], topf[:, :, :], ACT.Exp, scale=-1.0).then_inc(s("exp_top"), 1)
                else:
                    for m in range(M):
                        shared_gate(M * n + m)

            def gate(u, e, k, done, bank):
                for m in range(M):
                    o = act.activation(s1[:, k, m, :], ps[:, bank, m * TS:(m + 1) * TS], ACT.Silu,
                                       bias=bT[:, 0, m, e])
                o.then_inc(s(done), 1)

            def out_rows(y, bank, done):
                act.copy(yo[:, y, :], ps[0:TS, bank, :]).then_inc(s(done), 1)

            def experts(i, lo, z=False):
                for u in range(U):
                    act.wait_ge(s("pe_h1"), U * i + u + 1)
                    if U * lo + u >= 2:
                        act.wait_ge(s("hT_done"), U * i + u - 1)
                    gate(u, bass.ds(U * i + u, 1), u % 2, "act_s1", 2 + u % 2)
                    if U * lo + u >= 1:
                        act.wait_ge(s("pe_y"), U * i + u)
                        if U * lo + u - 1 >= U:
                            act.wait_ge(y_out[(u - 1) % U], 16 * i if u else 16 * i - 16)
                        out_rows((u - 1) % U, 6, "y_ready")
                    if lo < 2:
                        for n, (kind, k) in enumerate(BESIDE[U * lo + u]):
                            if kind == "up":
                                shared_gate(k)
                            elif kind == "cw":
                                act.wait_ge(s("pe_cwT"), k + 1)
                                c0, c1 = 512 * k, min(512 * k + 512, NPAD)
                                act.copy(cwT[0:NEX, c0:c1], ps[0:NEX, SPARE[n], 0:c1 - c0]).then_inc(s("cwT_done"), 1)
                    if z and u == 0:
                        if lo >= 3:
                            act.wait_ge(s("z_added"), i - 2)
                        act.wait_ge(s("cwT_done"), NSH)
                        act.wait_ge(s("cw_done"), 2)
                        act.copy(zc[:, :], cwT[:, bass.ds(P * i - 2 * P, P)]).then_inc(s("z_staged"), 1)

            experts(0, 0)
            experts(1, 1)
            experts(2, 2, z=True)
            with act.Fori(3, NT + 2) as i:
                experts(i, 3, z=True)
            with act.Fori(NT + 2, NIT) as i:
                experts(i, 3)
            act.wait_ge(s("pe_y"), NEX)
            act.wait_ge(y_out[U - 1], 16 * (NIT - 1))
            out_rows(U - 1, 6, "y_ready")
            act.wait_ge(s("over_done"), 1)
            n = act.value_load(nover_i[0:1, 0:1], min_val=0, max_val=NOV)
            with act.If(n > 0):
                with act.Fori(0, n) as j:
                    act.wait_ge(s("ov_step"), 7 * j + 3)
                    e = act.value_load(over_i[0:1, bass.ds(j, 1)], min_val=0, max_val=NEX - 1)
                    gate(0, bass.ds(e, 1), 0, "ov_step", 2)
                    act.wait_ge(s("ov_step"), 7 * j + 6)
                    out_rows(0, 6, "ov_step")
            for t in range(NT):
                act.wait_ge(s("out_ready"), t + 1)
                rows = P if t < NT - 1 else LAST
                act.dma_start(out[t * P:t * P + rows, :], x_sb[0:rows, t, :]).then_inc(s("stored"), 16)
            act.wait_ge(s("stored"), 16 * NT)

        @block.tensor
        def _(pe):
            def T(o, i, n=P):
                return pe.transpose(o, i, ident[0:n, 0:n])

            pe.wait_ge(s("const"), 1)
            pe.wait_ge(s("erow_f"), 1)
            for k in range(4):
                b, col = 4 + k // 2, (k % 2) * NC
                T(ps[:, b, col:col + P], erowf[:, 0, k, :])
                o = T(ps[:, b, col + P:col + NC], erowf[0:NC - P, 1, k, :], NC - P)
            o.then_inc(s("pe_erow"), 1)
            pe.wait_ge(s("w_in"), 16)
            for a in range(A):
                if a >= 2:
                    pe.wait_ge(s("act_wt"), a - 1)
                for t in range(A):
                    o = T(ps[:, 6 + a % 2, t * P:(t + 1) * P], W_sb[:, t, a * P:(a + 1) * P])
                o.then_inc(s("pe_wt"), 1)
            pe.wait_ge(s("ablk_done"), 1)
            for a in range(A):
                for t in range(A):
                    o = pe.matmul(ps[:, 3, a * 2 * H:(a + 1) * 2 * H], W_sb[:, t, a * P:(a + 1) * P],
                                  ablk[:, t * 2 * H:(t + 1) * 2 * H], start=(t == 0), stop=(t == A - 1))
            o.then_inc(s("pe_v"), 1)

            def turn_x(t):
                pe.wait_ge(s("ln1"), t + 1)
                if t >= 2:
                    pe.wait_ge(s("act_xt"), t - 1)
                for a in range(A):
                    o = T(ps[:, t % 2, a * P:(a + 1) * P], xn[:, t, a * P:(a + 1) * P])
                o.then_inc(s("pe_xt"), 1)

            def table(t):
                pe.wait_ge(s("act_xt"), t + 1)
                for a in range(A):
                    o = pe.matmul(ps[:, 2, t * 2 * H:(t + 1) * 2 * H], xT[:, a, t * P:(t + 1) * P], V[:, a, :],
                                  start=(a == 0), stop=(a == A - 1))
                return o

            turn_x(0)
            turn_x(1)
            pe.wait_ge(s("v_done"), 1)
            for t in range(NT):
                if t + 2 < NT:
                    turn_x(t + 2)
                o = table(t)
                if t == 5:
                    pe.wait_ge(s("srcx_done"), 1)
                    pe.matmul(ps[:, 6, 0:NX], ones[:, :], cnt[:, :], start=True, stop=True)
                    pe.matmul(ps[:, 6, 64:64 + NG], ones[0:1, :], lowf[:, :], start=True, stop=True).then_inc(s("pe_low"), 1)
            o.then_inc(s("pe_tab"), 1)

            def h_tile(t):
                if t == 0:
                    pe.wait_ge(s("act_wt"), A)
                else:
                    pe.wait_ge(s("act_h"), t)
                for a in range(A):
                    o = pe.matmul(ps[:, 7, :], xT[:, a, t * P:(t + 1) * P], WT[:, a, :],
                                  start=(a == 0), stop=(a == A - 1))
                o.then_inc(s("pe_h"), 1)

            pe.wait_ge(s("tab_done"), 1)
            pe.wait_ge(s("emb_done"), 1)
            pe.wait_ge(s("dve_low"), 1)
            for g, (q, c0, n) in enumerate(GROUPS):
                if g == 0 or GROUPS[g - 1][0] != q:
                    pe.wait_ge(s("hot_src"), q + 1)
                    pe.wait_ge(s("hot_dst"), 2 * q + 2)
                    pe.wait_ge(s("hot_type"), q + 1)
                if g >= 2:
                    pe.wait_ge(s("sel_read"), g - 1)
                for side in range(2):
                    for c in range(c0, c0 + n):
                        oh = keys[q % 3][:, side, (c - PIECES[q][0]) * P:(c - PIECES[q][0] + 1) * P]
                        for r in range(3):
                            o = pe.matmul(ps[:, 2 * (g % 2) + side, (c - c0) * NT * H:(c - c0 + 1) * NT * H], oh,
                                          tab3[:, r, side, :], start=(r == 0), stop=(r == 2))
                for c in range(c0, c0 + n):
                    oh = keys[q % 3][0:3 * TY, 2, (c - PIECES[q][0]) * P:(c - PIECES[q][0] + 1) * P]
                    o = pe.matmul(ps[:, 4 + c // 64, (c % 64) * H:(c % 64 + 1) * H], oh, embp[:, :], start=True, stop=True)
                o.then_inc(s("pe_sel"), 1)
                if g % 3 == 2 and g // 3 < NT:
                    h_tile(g // 3)
            pe.wait_ge(s("e_done"), 1)
            for b in range(4):
                for k in range(4):
                    h, q = (4 * b + k) // 2, (4 * b + k) % 2
                    o = T(ps[0:NG, b, k * P:(k + 1) * P], e_c[:, q::2, h])
                o.then_inc(s("pe_er"), 1)
            pe.wait_ge(s("ends_done"), 1)
            for k in range(4):
                o = T(ps[0:H, 4, k * NG:(k + 1) * NG], ends[:, k, :], NG)
            o.then_inc(s("pe_ends"), 1)
            pe.wait_ge(s("carry_done"), 1)
            T(ps[0:NG, 5, 0:H], carry[:, 0, 0:NG], H)
            T(ps[0:NG, 5, H:2 * H], carry[:, 1, 1:NG + 1], H).then_inc(s("pe_carry"), 1)
            pe.wait_ge(s("m_done"), 1)
            for k in range(2 * H):
                h, q = k // 2, k % 2
                o = T(ps[:, k // 6, (k % 6) * NG:(k % 6 + 1) * NG], E1[:, h, 1 + q * P:1 + (q + 1) * P], NG)
            o.then_inc(s("pe_m"), 1)

            def body(i, first, rows):
                for j in range(IB):
                    if not (first and j < 4):
                        pe.wait_ge(s("acc_done"), IB * i + j - 3)
                    for u in range(2):
                        k = 2 * j + u
                        pe.wait_ge(s("dve_msg"), SLOTS * i + k + 1)
                        pe.wait_ge(s("act_msg"), SLOTS * i + k + 1)
                        pe.matmul(ps[:, j % 4, :], S[:, k % 4, :], rows[:, k, :], start=(u == 0), stop=(u == 1))
                    for u in range(2):
                        k = 2 * j + u
                        o = pe.matmul(ps[:, 4 + j % 4, 0:H], S[:, k % 4, :],
                                      p_c[:, bass.ds(SLOTS * i + k, 1), :].rearrange("p a h -> p (a h)"),
                                      start=(u == 0), stop=(u == 1))
                    o.then_inc(s("pe_item"), 1)

            body(0, True, ring)
            pe.wait_ge(s("px_in"), 16 * NX)
            body(1, False, ring2)
            with pe.Fori(2, ITER) as i:
                body(i, False, ring)
            LGB = (2, 3, 6, 7)
            pe.wait_ge(s("param_in"), 16 * 14)
            pe.wait_ge(s("acc_done"), NI)
            for a in range(A):
                T(ps[:, 4, a * NEX:(a + 1) * NEX], gam[:, a::A], NEX)
                T(ps[:, 4, (A + a) * NEX:(A + a + 1) * NEX], bet[:, a::A], NEX)
                T(ps[:, 5, (A + a) * NEX:(A + a + 1) * NEX], wg[:, a::A], NEX)
            for k in range(2):
                for m in range(M):
                    o = T(ps[:, 5, (k * M + m) * NEX:(k * M + m + 1) * NEX], bb1[:, k, m * P:(m + 1) * P], NEX)
            o.then_inc(s("pe_param"), 1)

            def nx_turn(t):
                pe.wait_ge(s("nx_done"), t + 1)
                if t >= 2:
                    pe.wait_ge(s("act_nxT"), t - 1)
                for a in range(A):
                    o = T(ps[:, t % 2, a * P:(a + 1) * P], xn[:, t, a::A])
                o.then_inc(s("pe_nxT"), 1)

            def logits(t):
                pe.wait_ge(s("act_nxT"), t + 1)
                if t >= 4:
                    pe.wait_ge(s("lg_read"), t - 3)
                for a in range(A):
                    o = pe.matmul(ps[:, LGB[t % 4], 0:NEX], xT[:, a, t * P:(t + 1) * P], wgT[:, a, :],
                                  start=(a == 0), stop=(a == A - 1))
                o.then_inc(s("pe_lg"), 1)

            def shared_up(k):
                n, m = k // M, k % M
                c0, c1 = 512 * n, min(512 * n + 512, NPAD)
                c = c1 - c0
                pe.wait_ge(s("nxs_done"), A * (n + 1))
                for w, read in ((0, "act_sh"), (1, "hs_done")):
                    if k:
                        pe.wait_ge(s(read), k)
                    for a in range(A):
                        o = pe.matmul(ps[:, 4 + w if k < 4 else SPARE[w], 0:c], ws13[:, w, a, m * P:(m + 1) * P],
                                      xT[:, a, c0:c1], start=(a == 0), stop=(a == A - 1))
                    o.then_inc(s("pe_sh1" if w == 0 else "pe_sh3"), 1)

            def shared_down(t, bank):
                for m in range(M):
                    o = pe.matmul(ps[:, bank, :], hsT[:, m, t * P:(t + 1) * P], ws2[:, m, :],
                                  start=(m == 0), stop=(m == M - 1))
                o.then_inc(s("pe_zh"), 1)

            pe.wait_ge(s("param_done"), 1)
            for t0, t1 in LNG:
                for t in range(t0, t1):
                    nx_turn(t)
                for t in range(t0, t1):
                    logits(t)
            pe.wait_ge(s("sh_in"), 48)
            shared_up(0)
            pe.wait_ge(s("before_done"), 1)
            for t0, t1 in ((0, 8), (8, NT)):
                o = ps[:, 6 + t0 // 8, 0:(t1 - t0) * NEX]
                pe.matmul(o, tri[:, :], hits[:, t0:t1, :].rearrange("p t e -> p (t e)"), start=True, stop=False)
                pe.matmul(o, ones[:, :], before[:, t0:t1, :].rearrange("p t e -> p (t e)"), start=False, stop=True)
            pe.matmul(ps[:, 7, 2 * NEX:3 * NEX], ones[:, :], before[:, NT, :], start=True, stop=True).then_inc(s("pe_rank"), 1)
            shared_up(1)
            shared_up(2)
            pe.wait_ge(s("lg_read"), NT)
            pe.wait_ge(s("hs_done"), M)
            shared_down(0, SPARE[1])
            shared_down(1, SPARE[0])
            pe.wait_ge(s("onehots"), 1)
            for k in range(2 * NT):
                o = pe.matmul(ps[0:TS, 0, 0:NTILE], rank1h[:, k, :], tile1h[:, k, :], start=(k == 0), stop=(k == 2 * NT - 1))
            o.then_inc(s("pe_slots"), 1)
            shared_up(3)

            def aside(e):
                for name, count in (("zh_added", DOWN0 + beside(e, "down")), ("hs_done", 4 + beside(e, "up")),
                                    ("cwT_done", beside(e, "cw"))):
                    if count:
                        pe.wait_ge(s(name), count)
                for n, (kind, k) in enumerate(BESIDE[e]):
                    if kind == "up":
                        shared_up(k)
                    elif kind == "down":
                        shared_down(k, SPARE[n])
                    else:
                        pe.wait_ge(s("cw_done"), 1)
                        for t in range(4 * k, min(4 * k + 4, NT)):
                            o = T(ps[0:NEX, SPARE[n], (t % 4) * P:(t % 4 + 1) * P], cw[:, t, :])
                        o.then_inc(s("pe_cwT"), 1)

            def turn(u, bank, done):
                for a in range(A):
                    o = T(ps[:, bank, a * TS:(a + 1) * TS], xg[:, u, a::A], TS)
                o.then_inc(s(done), 1)

            def up(u, k, bank, done1, done3):
                for w, done in ((0, done1), (1, done3)):
                    for m in range(M):
                        for a in range(A):
                            o = pe.matmul(ps[:, bank + 2 * w, m * TS:(m + 1) * TS], w13[:, u, w, a, m * P:(m + 1) * P],
                                          xgT[:, k, a, :], start=(a == 0), stop=(a == A - 1))
                    if done:
                        o.then_inc(s(done), 1)

            def down(u, k, bank, done):
                for m in range(M):
                    o = pe.matmul(ps[0:TS, bank, :], hT[:, k, m, :], w2s[:, u, m, :], start=(m == 0), stop=(m == M - 1))
                o.then_inc(s(done), 1)

            def experts(i, lo, last, z=False):
                for u in range(U):
                    e = U * i + u
                    pe.wait_ge(w_landed[u], 48 * i + 48)
                    pe.wait_ge(s("xgT_done"), e + 1)
                    if U * lo + u >= 2:
                        pe.wait_ge(s("act_s1"), e - 1)
                        pe.wait_ge(s("hT_done"), e - 1)
                    up(u, u % 2, 2 + u % 2, "pe_h1", "pe_h3")
                    if not (last and u == U - 1):
                        v_ = (u + 1) % U
                        pe.wait_ge(xg_landed[v_], 16 * i + (16 if v_ else 32))
                        turn(v_, 0, "pe_xgT")
                    if U * lo + u >= 1:
                        pe.wait_ge(s("hT_done"), e)
                        if U * lo + u >= 2:
                            pe.wait_ge(s("y_ready"), e - 1)
                        down((u - 1) % U, (u - 1) % 2, 6, "pe_y")
                    if lo < 2:
                        aside(e)
                    if z and u == 1:
                        pe.wait_ge(s("z_staged"), i - 1)
                        pe.matmul(ps[:, 1, :], zc[:, :], b2a[:, :], start=True, stop=True).then_inc(s("pe_z"), 1)

            pe.wait_ge(xg_landed[0], 16)
            turn(0, 0, "pe_xgT")
            pe.wait_ge(s("zh_added"), 1)
            shared_down(2, SPARE[1])
            experts(0, 0, False)
            experts(1, 1, False)
            with pe.Fori(2, NT + 2) as i:
                experts(i, 2, False, z=True)
            with pe.Fori(NT + 2, NIT - 1) as i:
                experts(i, 2, False)
            experts(NIT - 1, NIT - 1, True)
            pe.wait_ge(s("hT_done"), NEX)
            pe.wait_ge(s("y_ready"), NEX - 1)
            down(U - 1, (U - 1) % 2, 6, "pe_y")
            pe.wait_ge(s("over_done"), 1)
            pe.wait_ge(s("y_ready"), NEX)
            n = pe.value_load(nover_i[0:1, 0:1], min_val=0, max_val=NOV)
            with pe.If(n > 0):
                with pe.Fori(0, n) as j:
                    pe.wait_ge(s("ov_g"), 16 * j + 16)
                    turn(0, 0, "ov_step")
                    pe.wait_ge(s("ov_step"), 7 * j + 2)
                    pe.wait_ge(s("ov_w"), 48 * j + 48)
                    up(0, 0, 2, None, "ov_step")
                    pe.wait_ge(s("ov_step"), 7 * j + 5)
                    down(0, 0, 6, "ov_step")

        @block.vector
        def _(v):
            chain = [0]

            def link(ins):
                chain[0] += 1
                ins.then_inc(s("dve"), 1)
                v.wait_ge(s("dve"), chain[0])

            v.memset(x_sb[96:P, NT - 1, :], 0.0).then_inc(s("x_pad"), 1)
            v.wait_ge(s("x_in"), 64)
            for t in range(NT):
                o = v.bn_stats(stats[:, t, :], x_sb[:, t, :])
            link(o)
            for t in range(NT):
                o = v.bn_aggr(mv[:, t, :], stats[:, t, :])
            link(o)
            v.tensor_scalar(rstd[:, :], mv[:, :, 1], EPS, None, ALU.add).then_inc(s("ln_scr"), 1)
            v.wait_ge(s("key_in"), 48)
            v.tensor_single_scalar(kint[0:KP, 0, :], kint[0:KP, 0, :], P - 1, op=ALU.bitwise_and)
            link(v.tensor_single_scalar(kint[0:KP, 1, :], kint[0:KP, 1, :], P - 1, op=ALU.bitwise_and))
            v.tensor_copy(kb[0:KP, :, :], kint[0:KP, :, :]).then_inc(s("key_ready"), 1)
            v.memset(kpad[:, :], float(PADNODE % P)).then_inc(s("key_ready"), 1)
            v.nop().then_inc(s("key_ready"), 1)
            v.wait_ge(s("erow_in"), 16 * 12)
            v.tensor_copy(erowf[:, 0, 0:3, :], erow[:, 0, 0:3, :])
            v.tensor_copy(erowf[:, 0, 3, :], erow[:, 0, 3, :].bitcast(F32))
            v.tensor_copy(erowf[0:32, 1, 0:3, :], erow[0:32, 1, 0:3, :])
            v.tensor_copy(erowf[0:32, 1, 3, :], erow[0:32, 1, 3, :].bitcast(F32)).then_inc(s("erow_f"), 1)
            v.wait_ge(s("small_in"), 96)
            link(v.memset(ablk[:, :], 0.0))
            for side in range(2):
                for half in range(2):
                    rows = slice(64 * half, 64 * half + 64)
                    o = side * H + half
                    last = v.tensor_copy(ablk[rows, o:o + 3 * (2 * H + 2) + 1:2 * H + 2], attn[rows, side, :])
            last.then_inc(s("ablk_done"), 1)

            def split(parts, value, rest):
                link(v.tensor_copy(parts[0], value))
                link(v.tensor_tensor(rest, value, parts[0], ALU.subtract))
                link(v.tensor_copy(parts[1], rest))
                link(v.tensor_tensor(rest, rest, parts[1], ALU.subtract))
                link(v.tensor_copy(parts[2], rest))

            link(v.tensor_scalar(emb[:, :], emb[:, :], 1.0, None, ALU.add))
            split([emb3[:, r, :] for r in range(3)], emb[:, :], embr[:, :])
            v.wait_ge(s("const"), 1)
            p24 = iota_p[0:3 * TY, :]
            v.tensor_scalar(iota_m[:, :], iota_p[:, :], -1.0, None, ALU.mult)
            v.tensor_scalar(beyond[:, 0:1], p24, float(TY), None, ALU.is_ge)
            link(v.tensor_scalar(beyond[:, 1:2], p24, float(2 * TY), None, ALU.is_ge))
            link(v.scalar_tensor_tensor(out=type_p[:, :], in0=beyond[:, 0:1], scalar=-float(TY), in1=p24, op0=ALU.mult, op1=ALU.add))
            v.tensor_scalar(place[:, 0:1], beyond[:, 0:1], -1.0, 1.0, ALU.mult, ALU.add)
            v.tensor_tensor(place[:, 1:2], beyond[:, 0:1], beyond[:, 1:2], ALU.subtract)
            v.tensor_copy(place[:, 2:3], beyond[:, 1:2])
            link(v.scalar_tensor_tensor(out=type_p[:, :], in0=beyond[:, 1:2], scalar=-float(TY), in1=type_p[:, :], op0=ALU.mult,
                                        op1=ALU.add))
            link(v.tensor_scalar(embp[:, :], emb3[:, 0, :], place[:, 0:1], None, ALU.mult))
            for r in (1, 2):
                link(v.scalar_tensor_tensor(out=embp[:, :], in0=emb3[:, r, :], scalar=place[:, r:r + 1], in1=embp[:, :],
                                            op0=ALU.mult, op1=ALU.add))
            v.nop().then_inc(s("emb_done"), 1)
            v.wait_ge(s("ln1_std"), 1)
            link(v.reciprocal(rstd[:, :], rstd[:, :]))
            for t in range(NT):
                v.tensor_scalar(xn[:, t, :], x_sb[:, t, :], mv[:, t, 0:1], rstd[:, t:t + 1],
                                ALU.subtract, ALU.mult).then_inc(s("ln1"), 1)
            v.wait_ge(s("pe_erow"), 1)
            v.tensor_copy(ecol[:, 0:2, :], ps[:, 4, 0:2 * NC].rearrange("p (k c) -> p k c", k=2))
            link(v.tensor_copy(ecol[:, 2:4, :], ps[:, 5, 0:2 * NC].rearrange("p (k c) -> p k c", k=2)))
            v.wait_ge(s("const"), 1)
            link(v.tensor_single_scalar(low[:, :], low[:, :], 7, op=ALU.arith_shift_right))
            v.tensor_copy(lowf[:, :], low[:, :])
            v.tensor_copy(witem[:, 0:NG], low[:, :])
            for w in range(NX):
                v.memset(witem[:, NG + w:NG + w + 1], w + 1)
                link(v.tensor_scalar(cmp[:, :], ecol[:, 1, :], float(P * (w + 1)), 0.0, ALU.is_lt, ALU.add,
                                     accum_out=cnt[:, w:w + 1]))
            v.tensor_copy(srcx[:, 0:NC], ecol[:, 0, :])
            link(v.tensor_copy(hi[:, :, :], ecol[:, 0:2, :]))
            link(v.tensor_single_scalar(hi[:, :, :], hi[:, :, :], 7, op=ALU.arith_shift_right))
            link(v.tensor_copy(hif[:, :, :], hi[:, :, :]))
            v.nop().then_inc(s("srcx_done"), 1)
            ib = iota_row[:, 0:NT].unsqueeze(1).to_broadcast([P, 2 * NC, NT])
            v.tensor_tensor(sel_hi[:, :, :, :].rearrange("p s c a -> p (s c) a"),
                            hif[:, :, :].rearrange("p s c -> p (s c)").unsqueeze(2).to_broadcast([P, 2 * NC, NT]), ib,
                               ALU.is_equal)
            v.wait_ge(s("pe_low"), 1)
            link(v.tensor_copy(start_i[:, :], ps[:, 6, 0:NX]))
            v.tensor_single_scalar(grp[:, :], start_i[:, :], 8, op=ALU.arith_shift_right)
            link(v.tensor_single_scalar(rem[:, :], start_i[:, :], GE - 1, op=ALU.bitwise_and))
            link(v.tensor_scalar(shift[:, :], rem[:, :], 0.0, 1.0e6, ALU.is_equal, ALU.mult))
            for w in range(NX):
                o = v.tensor_scalar(shift[:, w:w + 1], shift[:, w:w + 1], float(P * (w + 1)), None, ALU.add)
            link(o)
            lo2 = ps[:, 6, 64:64 + NG].unsqueeze(2).to_broadcast([P, NG, 2])
            v.scalar_tensor_tensor(out=dloc[:, 0:NC].rearrange("p (g u) -> p g u", u=2), in0=lo2, scalar=-float(P),
                                   in1=ecol[:, 1, :].rearrange("p (g u) -> p g u", u=2), op0=ALU.mult,
                                   op1=ALU.add).then_inc(s("dve_low"), 1)
            v.wait_ge(s("dx_in"), 48)
            link(v.tensor_copy(dx[:, :], dx_i[:, :]))
            link(v.tensor_tensor(eq[:, 1:RW], dx[:, 1:RW], dx[:, 0:RW - 1], ALU.is_equal))
            link(v.tensor_reduce(allsame[:, :], eq[:, 2:GE + 1], AX_X, ALU.min))
            for h in range(H):
                v.tensor_scalar(ends[:, 2, h:h + 1], eq[:, 1:2], allsame[:, 0:1], None, ALU.mult)
                v.tensor_scalar(ends[:, 3, h:h + 1], eq[:, RW - 1:RW], allsame[:, 0:1], None, ALU.mult)

            v.wait_ge(s("pe_tab"), 1)
            pt = ps[:, 2, 0:NT * 2 * H].rearrange("p (a s h) -> p s a h", a=NT, s=2)
            link(v.tensor_copy(tab[:, :, :].rearrange("p s (a h) -> p s a h", a=NT), pt))
            tf = tab[:, :, :].rearrange("p s k -> p (s k)")
            split([tab3[:, r, :, :].rearrange("p s k -> p (s k)") for r in range(3)], tf, tabr[:, :])
            v.nop().then_inc(s("tab_done"), 1)


            def hot_src(q):
                c0, n = PIECES[q]
                v.wait_ge(s(f"keys_landed{q % 3}"), 48 * (q // 3 + 1))
                v.tensor_scalar(keys[q % 3][:, 0, 0:n * P], keys[q % 3][:, 0, 0:n * P], iota_p[:, 0:1], None, ALU.is_equal
                                ).then_inc(s("hot_src"), 1)

            hot_src(0)
            hot_src(1)
            for g, (q, c0, n) in enumerate(GROUPS):
                if g + 1 < len(GROUPS) and GROUPS[g + 1][0] != q and q + 2 < len(PIECES):
                    hot_src(q + 2)
                v.wait_ge(s("pe_sel"), g + 1)
                pr = prod[:, 0:n * 2 * NT * H].rearrange("p (c s a h) -> p s c a h", c=n, s=2, a=NT)
                for side in range(2):
                    o = v.tensor_tensor(pr[:, side, :, :, :],
                                        ps[:, 2 * (g % 2) + side, 0:n * NT * H].rearrange("p (c a h) -> p c a h", c=n, a=NT),
                                        sel_hi[:, side, c0:c0 + n, :].unsqueeze(3).to_broadcast([P, n, NT, H]), ALU.mult)
                    o.then_inc(s("dve"), 1)
                    chain[0] += 1
                v.wait_ge(s("dve"), chain[0])
                v.nop().then_inc(s("sel_read"), 1)
                link(v.tensor_reduce(e_c[:, c0:c0 + n, :],
                                     prod[:, 0:n * 2 * NT * H].rearrange("p (c k h) -> p c h k", c=n, h=H), AX_X, ALU.add))
            ef = e_c[:, :, :].rearrange("p c h -> p (c h)")
            link(v.scalar_tensor_tensor(out=ef, in0=ef, scalar=0.2, in1=ef, op0=ALU.mult, op1=ALU.max))
            for b in range(3):
                c0, c1 = 64 * b, min(64 * b + 64, NC)
                o = v.tensor_tensor(e_c[:, c0:c1, :].rearrange("p c h -> p (c h)"),
                                    ps[:, 4 + b, 0:(c1 - c0) * H], e_c[:, c0:c1, :].rearrange("p c h -> p (c h)"), ALU.mult)
            link(o)
            v.tensor_tensor(e_c[:, :, :], e_c[:, :, :], ecol[:, 3, :].unsqueeze(2).to_broadcast([P, NC, H]),
                            ALU.mult).then_inc(s("e_done"), 1)
            v.wait_ge(s("act_h"), NT)
            v.memset(F1[:, :, 0:1], 0.0)
            v.memset(F1[:, :, RW - 1:RW], 0.0)
            v.memset(F2[:, :, 0:1], 0.0)
            v.memset(F2[:, :, RW - 1:RW], 0.0)
            v.tensor_copy(F1[:, :, 1:GE + 1], eq[:, 1:GE + 1].unsqueeze(1).to_broadcast([NG, H, GE]))
            link(v.tensor_copy(F2[:, :, 1:GE + 1], eq[:, 2:GE + 2].unsqueeze(1).to_broadcast([NG, H, GE])))
            v.nop().then_inc(s("dx_read"), 1)
            v.memset(E1[:, :, 0:1], 0.0)
            link(v.memset(E1[:, :, RW - 1:RW], 0.0))
            e1, e2, f1, f2 = (z.rearrange("p h k -> p (h k)") for z in (E1, E2, F1, F2))

            def segment_max():
                link(v.tensor_tensor_scan(e2, f1, e1, 0.0, ALU.mult, ALU.max))
                link(v.tensor_tensor_scan(e1[:, ::-1], f2[:, ::-1], e2[:, ::-1], 0.0, ALU.mult, ALU.max))

            v.wait_ge(s("act_er"), 16)
            segment_max()
            v.tensor_copy(ends[:, 0, :], E1[:, :, GE])
            v.tensor_copy(ends[:, 1, :], E1[:, :, 1]).then_inc(s("ends_done"), 1)
            v.wait_ge(s("pe_ends"), 1)
            link(v.tensor_copy(endsT[:, :, :].rearrange("h k g -> h (k g)"), ps[0:H, 4, 0:4 * NG]))
            v.memset(carry[:, 0, 0:1], 0.0)
            v.memset(carry[:, 1, NG:NG + 1], 0.0)
            v.tensor_tensor_scan(carry[:, 0, 1:NG + 1], endsT[:, 2, :], endsT[:, 0, :], 0.0, ALU.mult, ALU.max)
            v.tensor_tensor_scan(carry[:, 1, 0:NG][:, ::-1], endsT[:, 3, ::-1], endsT[:, 1, ::-1], 0.0, ALU.mult,
                                 ALU.max).then_inc(s("carry_done"), 1)
            v.wait_ge(s("pe_carry"), 1)
            v.tensor_copy(E1[:, :, 0], ps[0:NG, 5, 0:H])
            link(v.tensor_copy(E1[:, :, RW - 1], ps[0:NG, 5, H:2 * H]))
            segment_max()
            v.nop().then_inc(s("m_done"), 1)
            v.wait_ge(s("pe_m"), 1)
            for k in range(2 * H):
                h, q = k // 2, k % 2
                o = v.tensor_tensor(e_c[:, q::2, h], e_c[:, q::2, h], ps[:, k // 6, (k % 6) * NG:(k % 6 + 1) * NG], ALU.subtract)
            o.then_inc(s("dve_d"), 1)
            v.memset(accs[:, :, :], 0.0)
            v.memset(ps[:, 3, :], 0.0)
            link(v.memset(ps[:, 7, 0:H], 0.0))
            v.wait_ge(s("p_done"), 1)

            def add_item(it, j):
                w = v.value_load(witem[0:1, it], min_val=0, max_val=NT - 1)
                a = acc[:, bass.ds(w, 1), :].rearrange("p a d -> p (a d)")
                b = accs[:, bass.ds(w, 1), :].rearrange("p a d -> p (a d)")
                v.tensor_tensor(b, ps[:, 4 + j % 4, 0:H], b, ALU.add)
                v.tensor_tensor(a, ps[:, j % 4, :], a, ALU.add).then_inc(s("acc_done"), 1)

            def body(i, first, rows):
                for j in range(IB):
                    for u in range(2):
                        k = 2 * j + u
                        if not (first and j < 2):
                            v.wait_ge(s("pe_item"), IB * i + j - 1)
                        v.tensor_scalar(S[:, k % 4, :], iota_row[:, :],
                                        dloc[:, bass.ds(SLOTS * i + k, 1)], None, ALU.is_equal)
                        v.wait_ge(landed[k], 16 * i + 16)
                        n = HV * HD
                        v.tensor_tensor(rows[:, k, 0:n].rearrange("p (h d) -> p h d", d=HD),
                                        rows[:, k, 0:n].rearrange("p (h d) -> p h d", d=HD),
                                        p_c[:, bass.ds(SLOTS * i + k, 1), 0:HV].rearrange("p a h -> p (a h)")
                                        .unsqueeze(2).to_broadcast([P, HV, HD]), ALU.mult).then_inc(s("dve_msg"), 1)
                    if not (first and j < 2):
                        v.wait_ge(s("pe_item"), IB * i + j - 1)
                        if not (first and j == 2):
                            v.wait_ge(s("acc_done"), IB * i + j - 2)
                        add_item(bass.ds(IB * i + j - 2, 1), j - 2)

            v.wait_ge(s("acc_zero"), 1)
            body(0, True, ring)
            v.wait_ge(s("ex_in"), 32 * NX)
            v.wait_ge(s("px_in"), 16 * NX)
            dx2 = dloc[:, NC:NCX].rearrange("p (w u) -> p w u", u=2)
            link(v.tensor_tensor(dx2, dx2, shift[:, :].unsqueeze(2).to_broadcast([P, NX, 2]), ALU.subtract))
            body(1, False, ring2)
            with v.Fori(2, ITER) as i:
                body(i, False, ring)
            for k in (2, 1):
                v.wait_ge(s("pe_item"), NI + 1 - k)
                v.wait_ge(s("acc_done"), NI - k)
                add_item(slice(NI - k, NI - k + 1), IB - k)
            v.wait_ge(s("acc_done"), NI)
            link(v.tensor_scalar(accs[:, :, :], accs[:, :, :], 1e-10, None, ALU.add))
            v.reciprocal(accs[:, :, :], accs[:, :, :]).then_inc(s("accs_done"), 1)
            def params_by_row():
                v.wait_ge(s("pe_param"), 1)
                v.tensor_copy(gT[:, :, :, :].rearrange("p k a e -> p (k a e)"), ps[:, 4, 0:2 * A * NEX])
                v.tensor_copy(bT[:, :, :, :].rearrange("p k m e -> p (k m e)"), ps[:, 5, 0:2 * M * NEX])
                v.tensor_copy(wgT[:, :, :].rearrange("p a e -> p (a e)"), ps[:, 5, A * NEX:2 * A * NEX]).then_inc(s("param_done"), 1)

            def issue(ins):
                chain[0] += 1
                ins.then_inc(s("dve"), 1)
                return chain[0]

            def add_and_stats(g, out, extra, ready, t0=0):
                tiles = range(*LNG[g])
                added = []
                for t in tiles:
                    v.wait_ge(s(ready), t + 1 - t0)
                    added.append(issue(v.tensor_tensor(out[:, t, :], extra[:, t, :], out[:, t, :], ALU.add)))
                for t, n in zip(tiles, added):
                    v.wait_ge(s("dve"), n)
                    o = v.bn_stats(stats[:, t, :], out[:, t, :])
                link(o)
                for t in tiles:
                    o = v.bn_aggr(mv[:, t, :], stats[:, t, :])
                link(o)

            def gnn_sum(g):
                add_and_stats(g, acc, xn, "divided" if g else "divided0", LNG[0][1] if g else 0)
                b = slice(*LNG[g])
                v.tensor_scalar(rstd[:, b], mv[:, b, 1], EPS, None, ALU.add).then_inc(s("gnn_var"), 1)

            def gnn_scale(g):
                b = slice(*LNG[g])
                v.wait_ge(s("gnn_std"), g + 1)
                link(v.reciprocal(rstd[:, b], rstd[:, b]))
                v.scalar_tensor_tensor(out=mean2[:, b], in0=mv[:, b, 0], scalar=-1.0, in1=rstd[:, b], op0=ALU.mult,
                                       op1=ALU.mult).then_inc(s("gnn_off"), 1)

            def x1_sum(g):
                add_and_stats(g, x_sb, acc, "gnn_gam")
                b = slice(*LNG[g])
                v.tensor_scalar(vw[:, 0, b], mv[:, b, 1], EPS, None, ALU.add)
                v.tensor_scalar(vw[:, 1, b], mv[:, b, 1], 1.0 + EPS, EPS * EPS, ALU.mult, ALU.add).then_inc(s("x1_var"), 1)

            def x1_scale(g):
                b = slice(*LNG[g])
                v.wait_ge(s("x1_std"), g + 1)
                link(v.reciprocal(rv[:, :, b], vw[:, :, b]))
                v.tensor_tensor(inv_r2[:, b], vw[:, 1, b], rv[:, 0, b], ALU.mult)
                v.scalar_tensor_tensor(out=mean2[:, b], in0=mv[:, b, 0], scalar=-1.0, in1=rv[:, 1, b], op0=ALU.mult,
                                       op1=ALU.mult).then_inc(s("nx_ready"), 1)

            def best_two(g):
                tiles = range(*LNG[g])
                for t in tiles:
                    v.wait_ge(s("pe_lg"), t + 1)
                    v.scalar_tensor_tensor(out=lg[:, t, :], in0=ps[:, (2, 3, 6, 7)[t % 4], 0:NEX], scalar=inv_r2[:, t:t + 1],
                                           in1=bg_b[:, :], op0=ALU.mult, op1=ALU.add).then_inc(s("lg_read"), 1)
                found = []
                for t in tiles:
                    v.wait_ge(s("lg_read"), t + 1)
                    found.append(issue(v.max(top[:, t, :], lg[:, t, :])))
                for t, n in zip(tiles, found):
                    v.wait_ge(s("dve"), n)
                    o = v.max_index(topi[:, t, :], top[:, t, :], lg[:, t, :])
                return o

            def shared_add(t, bank):
                v.wait_ge(s("pe_zh"), t + 1)
                v.tensor_tensor(x_sb[:, t, :], ps[:, bank, :], x_sb[:, t, :], ALU.add).then_inc(s("zh_added"), 1)

            def shared_hidden(k):
                n, m = k // M, k % M
                c0, c1 = 512 * n, min(512 * n + 512, NPAD)
                v.wait_ge(s("pe_sh3"), k + 1)
                v.wait_ge(s("act_sh"), k + 1)
                v.scalar_tensor_tensor(out=hsT[:, m, c0:c1], in0=ps[:, 5 if k < 4 else SPARE[1], 0:c1 - c0], scalar=sbias[:, 1, m:m + 1],
                                       in1=sil[:, 0:c1 - c0], op0=ALU.add, op1=ALU.mult).then_inc(s("hs_done"), 1)

            v.wait_ge(s("accs_done"), 1)
            for t in range(*LNG[0]):
                o3 = acc[:, t, :].rearrange("p (h d) -> p h d", h=H)
                v.tensor_tensor(o3, o3, accs[:, t, :].unsqueeze(2).to_broadcast([P, H, HD]), ALU.mult
                                ).then_inc(s("divided0"), 1)
            G = len(LNG)
            for step in range(G + 5):
                if step < G:
                    gnn_sum(step)
                if step == 1:
                    params_by_row()
                if 0 <= step - 1 < G:
                    gnn_scale(step - 1)
                if 0 <= step - 2 < G:
                    x1_sum(step - 2)
                if 0 <= step - 3 < G:
                    x1_scale(step - 3)
                if 0 <= step - 5 < G:
                    o = best_two(step - 5)
            link(o)
            v.tensor_copy(topf[:, :, :], top[:, :, 0:2]).then_inc(s("top_done"), 1)
            link(v.tensor_copy(eidx[:, :, :], topi[:, :, 0:2]))
            erow2 = iota_row[:, 0:NEX].unsqueeze(1).to_broadcast([P, 2 * NT, NEX])
            ohf, tmpf = (z[:, :, :, :].rearrange("p t k e -> p (t k) e") for z in (oh, tmp))
            link(v.tensor_tensor(ohf, erow2, eidx[:, :, :].rearrange("p t k -> p (t k)").unsqueeze(2).to_broadcast([P, 2 * NT, NEX]),
                                 ALU.is_equal))
            v.wait_ge(s("tri_done"), 5)
            link(v.tensor_scalar(oh[:, NT - 1, :, :], oh[:, NT - 1, :, :], real[:, 0:1], None, ALU.mult))
            v.memset(before[:, 0, :], 0.0)
            link(v.tensor_tensor(hits[:, :, :], oh[:, :, 0, :], oh[:, :, 1, :], ALU.add))
            for t in range(NT):
                link(v.tensor_tensor(before[:, t + 1, :], before[:, t, :], hits[:, t, :], ALU.add))
            v.nop().then_inc(s("before_done"), 1)
            shared_hidden(0)
            v.wait_ge(s("pe_rank"), 1)
            v.tensor_tensor(tmp[:, 0:8, :, :], oh[:, 0:8, :, :],
                            ps[:, 6, :].rearrange("p (t e) -> p t e", t=8).unsqueeze(2).to_broadcast([P, 8, 2, NEX]), ALU.mult)
            rf, of, ef_ = (z[:, :, :].rearrange("p t k -> p (t k)") for z in (rnk, obs, eidx))
            tf_, kf, nov = tens[:, :], tens[:, 0:2 * NT], tens[:, 2 * NT:2 * NT + NEX]
            v.tensor_scalar(nov, ps[:, 7, 2 * NEX:3 * NEX], 1.0 / TS, -0.5 / TS - 0.5, ALU.mult, ALU.add)
            link(v.tensor_tensor(tmp[:, 8:NT, :, :], oh[:, 8:NT, :, :],
                                 ps[:, 7, 0:(NT - 8) * NEX].rearrange("p (t e) -> p t e", e=NEX).unsqueeze(2)
                                 .to_broadcast([P, NT - 8, 2, NEX]), ALU.mult))
            link(v.tensor_reduce(rf, tmpf, AX_X, ALU.add))
            link(v.tensor_scalar(kf, rf, 1.0 / TS, 0.5 / TS - 0.5, ALU.mult, ALU.add))
            link(v.tensor_scalar(tf_, tf_, ROUND, None, ALU.add))
            link(v.tensor_scalar(tf_, tf_, -ROUND, 0.0, ALU.add, ALU.max))
            link(v.tensor_tensor_scan(inc[:, :], ones[:, 0:NEX], nov, 0.0, ALU.mult, ALU.add))
            link(v.tensor_tensor(exc[:, :], inc[:, :], nov, ALU.subtract))
            link(v.tensor_tensor(tmpf, ohf, exc[:, :].unsqueeze(1).to_broadcast([P, 2 * NT, NEX]), ALU.mult))
            link(v.tensor_reduce(of, tmpf, AX_X, ALU.add))
            v.scalar_tensor_tensor(out=rf, in0=kf, scalar=-float(TS), in1=rf, op0=ALU.mult, op1=ALU.add)
            link(v.scalar_tensor_tensor(out=of, in0=of, scalar=float(NEX - 1), in1=kf, op0=ALU.add, op1=ALU.add))
            v.tensor_scalar(rnk[:, NT - 1, :], rnk[:, NT - 1, :], far[:, 0:1], None, ALU.add)
            link(v.tensor_tensor(of, of, ef_, ALU.subtract))
            link(v.scalar_tensor_tensor(out=of, in0=kf, scalar=1.0, in1=of, op0=ALU.min, op1=ALU.mult))
            link(v.tensor_tensor(of, of, ef_, ALU.add))
            shared_hidden(1)
            v.wait_ge(s("nx_out"), 16 * NT)
            v.wait_ge(s("pe_nxT"), NT)
            v.tensor_tensor(rank1h[:, :, :], iota_row[:, 0:TS].unsqueeze(1).to_broadcast([P, 2 * NT, TS]),
                            rf.unsqueeze(2).to_broadcast([P, 2 * NT, TS]), ALU.is_equal)
            link(v.tensor_tensor(tile1h[:, :, :], iota_row[:, 0:NTILE].unsqueeze(1).to_broadcast([P, 2 * NT, NTILE]),
                                 of.unsqueeze(2).to_broadcast([P, 2 * NT, NTILE]), ALU.is_equal))
            v.tensor_tensor(tile1h[:, :, :], tile1h[:, :, :], payload[:, :, :].rearrange("p t k -> p (t k)").unsqueeze(2)
                            .to_broadcast([P, 2 * NT, NTILE]), ALU.mult).then_inc(s("onehots"), 1)
            shared_add(0, SPARE[1])
            shared_add(1, SPARE[0])
            shared_hidden(2)
            v.wait_ge(s("pe_slots"), 1)
            link(v.tensor_scalar(slotf[:, :], ps[0:TS, 0, 0:NTILE], 0.0, float(SKIP), ALU.is_equal, ALU.mult))
            link(v.scalar_tensor_tensor(out=slotf[:, :], in0=ps[0:TS, 0, 0:NTILE], scalar=-1.0, in1=slotf[:, :],
                                        op0=ALU.add, op1=ALU.add))
            link(v.tensor_copy(slot_tab[:, :, 1], slotf[:, :]))
            v.tensor_single_scalar(slot_tab[:, :, 0], slot_tab[:, :, 1], 1, op=ALU.arith_shift_right).then_inc(s("slots_done"), 1)
            for j0 in range(0, NOV, 16):
                n = min(16, NOV - j0)
                c3 = tmpf[0:1, 0:n, :]
                link(v.tensor_tensor(c3, inc[0:1, :].unsqueeze(1).to_broadcast([1, n, NEX]),
                                     iota_row[0:1, j0:j0 + n].unsqueeze(2).to_broadcast([1, n, NEX]), ALU.is_le))
                link(v.tensor_reduce(counts[0:1, j0:j0 + n], c3, AX_X, ALU.add))
            v.tensor_copy(over_i[:, :], counts[0:1, 0:NOV])
            v.tensor_copy(nover_i[:, :], inc[0:1, NEX - 1:NEX]).then_inc(s("over_done"), 1)
            shared_hidden(3)

            def routing_weights():
                v.wait_ge(s("exp_top"), 1)
                link(v.tensor_scalar(wk[:, :, :], wk[:, :, :], 1.0, None, ALU.add))
                link(v.reciprocal(wk[:, :, :], wk[:, :, :]))
                link(v.tensor_tensor(wsum[:, :], wk[:, :, 0], wk[:, :, 1], ALU.add))
                link(v.reciprocal(wsum[:, :], wsum[:, :]))
                link(v.tensor_tensor(wk[:, :, :], wk[:, :, :], wsum[:, :].unsqueeze(2).to_broadcast([P, NT, 2]), ALU.mult))
                link(v.tensor_tensor(tmpf, ohf, wk[:, :, :].rearrange("p t k -> p (t k)").unsqueeze(2)
                                     .to_broadcast([P, 2 * NT, NEX]), ALU.mult))
                v.tensor_tensor(cw[:, :, :], tmp[:, :, 0, :], tmp[:, :, 1, :], ALU.add).then_inc(s("cw_done"), 1)
                v.wait_ge(s("cw_done"), 1)
                v.memset(cwT[NEX:NEX + 1, :], 1.0).then_inc(s("cw_done"), 1)

            def scale_in(u, e, bank, k, done):
                for a in range(A):
                    o = v.tensor_scalar(xgT[:, k, a, :], ps[:, bank, a * TS:(a + 1) * TS], gT[:, 0, a, e], gT[:, 1, a, e],
                                        ALU.mult, ALU.add)
                o.then_inc(s(done), 1)

            def hidden(e, bank, k, done):
                for m in range(M):
                    o = v.scalar_tensor_tensor(out=hT[:, k, m, :], in0=ps[:, bank, m * TS:(m + 1) * TS], scalar=bT[:, 1, m, e],
                                               in1=s1[:, k, m, :], op0=ALU.add, op1=ALU.mult)
                o.then_inc(s(done), 1)

            def experts(i, lo, last, z=False):
                for u in range(U):
                    e = U * i + u
                    if z and u == 2:
                        v.wait_ge(s("pe_z"), i - 1)
                        zt = x_sb[:, bass.ds(i - 2, 1), :].rearrange("p a d -> p (a d)")
                        v.tensor_tensor(zt, ps[:, 1, :], zt, ALU.add).then_inc(s("z_added"), 1)
                    if not (last and u == U - 1):
                        v.wait_ge(s("pe_xgT"), e + 2)
                        if U * lo + u >= 1:
                            v.wait_ge(s("pe_h3"), e)
                        scale_in(u, bass.ds(e + 1, 1), 0, (u + 1) % 2, "xgT_done")
                    v.wait_ge(s("pe_h3"), e + 1)
                    v.wait_ge(s("act_s1"), e + 1)
                    if U * lo + u >= 2:
                        v.wait_ge(s("pe_y"), e - 1)
                    hidden(bass.ds(e, 1), 4 + u % 2, u % 2, "hT_done")
                    if lo < 2:
                        if e == 2:
                            routing_weights()
                        for n, (kind, k) in enumerate(BESIDE[e]):
                            if kind == "up":
                                shared_hidden(k)
                            elif kind == "down":
                                shared_add(k, SPARE[n])

            v.wait_ge(s("pe_xgT"), 1)
            scale_in(0, slice(0, 1), 0, 0, "xgT_done")
            shared_add(2, SPARE[1])
            experts(0, 0, False)
            experts(1, 1, False)
            v.wait_ge(s("zh_added"), NT)
            with v.Fori(2, NT + 2) as i:
                experts(i, 2, False, z=True)
            with v.Fori(NT + 2, NIT - 1) as i:
                experts(i, 2, False)
            experts(NIT - 1, NIT - 1, True)
            n = v.value_load(nover_i[0:1, 0:1], min_val=0, max_val=NOV)
            with v.If(n > 0):
                v.nop().then_inc(s("ov_end"), 1)
                with v.Fori(0, n) as j:
                    v.wait_ge(s("ov_step"), 7 * j + 1)
                    e = v.value_load(over_i[0:1, bass.ds(j, 1)], min_val=0, max_val=NEX - 1)
                    scale_in(0, bass.ds(e, 1), 0, 0, "ov_step")
                    v.wait_ge(s("ov_step"), 7 * j + 4)
                    hidden(bass.ds(e, 1), 4, 0, "ov_step")
            for t in range(NT):
                v.wait_ge(s(f"y_in{t % 4}"), 16 * (t // 4 + 1))
                rows = P if t < NT - 1 else LAST
                for k in range(2):
                    o = v.scalar_tensor_tensor(out=x_sb[0:rows, t, :], in0=yin[0:rows, t % 4, k, :], scalar=wk[0:rows, t, k:k + 1],
                                               in1=x_sb[0:rows, t, :], op0=ALU.mult, op1=ALU.add)
                    if k == 0:
                        link(o)
                o.then_inc(s("out_ready"), 1)


_INS = ['x', 'src', 'dst', 'edge_type_8', 'edge_weight', 'L0_gnn_W', 'L0_gnn_a_src', 'L0_gnn_a_dst', 'L0_gnn_et_emb',
        'L0_gnn_ln_gamma', 'L0_gnn_ln_beta', 'L0_ffn_Wg', 'L0_ffn_bg', 'L0_ffn_gamma', 'L0_ffn_beta', 'L0_ffn_W1',
        'L0_ffn_b1', 'L0_ffn_W3', 'L0_ffn_b3', 'L0_ffn_W2', 'L0_ffn_b2', 'L0_ffn_gs', 'L0_ffn_bs', 'L0_ffn_Ws1',
        'L0_ffn_bs1', 'L0_ffn_Ws3', 'L0_ffn_bs3', 'L0_ffn_Ws2', 'L0_ffn_bs2']


def kernel(**inputs):
    import numpy as _np
    import concourse.bacc as _bacc
    from concourse import mybir as _mybir
    from concourse.bass_utils import run_bass_kernel_spmd as _run

    nc = _bacc.Bacc("TRN2", target_bir_lowering=False, num_devices=1)
    arrays, args = {}, []
    for name in _INS:
        a = _np.ascontiguousarray(inputs[name])
        arrays[f"in_{name}_dram"] = a
        args.append(nc.dram_tensor(f"in_{name}_dram", a.shape, _mybir.dt.from_np(a.dtype), kind="ExternalInput").ap())
    out = nc.dram_tensor("out_0_dram", (1250, 512), _mybir.dt.float32, kind="ExternalOutput").ap()
    gnn_moe_kernel(nc, *args, out)
    r = _run(nc, [arrays], core_ids=[0])
    return r.results[0]["out_0_dram"]
```
